# Optimizing a Trainium2 kernel written in Bass

```python
import numpy as np
import jax
import jax.numpy as jnp

def _softmax(x, axis=-1):
    return jax.nn.softmax(x, axis=axis)

def _gelu(x):
    return jax.nn.gelu(x, approximate=True)

def _silu(x):
    return jax.nn.silu(x)

def _sigmoid(x):
    return jax.nn.sigmoid(x)

def _layernorm(x, axis=-1, eps=1e-05):
    m = jnp.mean(x, axis=axis, keepdims=True)
    v = jnp.var(x, axis=axis, keepdims=True)
    return (x - m) / jnp.sqrt(v + eps)

def _scatter_add(tgt, idx, src, axis=0):
    return tgt.at[idx].add(src)

def _segment_sum(src, seg, n):
    return jax.ops.segment_sum(src, seg, n)
kernel_name = 'mk_flamingo_gated_d2_seqx_r8_c8ef26'

def setup_inputs(seed: int=0):
    np.random.seed(seed)
    _w = jnp.asarray

    def _rec_inputs():
        import jax
        import jax.numpy as jnp
        _rk = jax.random.key(seed)
        x = -0.0002928 + 1 * jax.random.normal(jax.random.fold_in(_rk, 1), (64, 64, 128), jnp.float32)
        _lenS = 64 - jax.random.randint(jax.random.fold_in(_rk, 7), (64,), 0, max(1, 64 // 4) + 1, jnp.int32)
        _lenS2 = 64 - jax.random.randint(jax.random.fold_in(_rk, 8), (64,), 0, max(1, 64 // 4) + 1, jnp.int32)
        _ctx_2048P = jax.random.normal(jax.random.fold_in(_rk, 11), (64, 16, 256), jnp.float32)
        _ctx_2048c = jax.random.dirichlet(jax.random.fold_in(_rk, 511), 0.3 * jnp.ones((16,), jnp.float32), (64, 64))
        _ctx_2048t = jnp.einsum('bsk,bkd->bsd', _ctx_2048c, _ctx_2048P)
        _ctx_2048t = _ctx_2048t * jax.lax.rsqrt(jnp.mean(jnp.square(_ctx_2048t)) + 1e-12) * 0.953939
        ctx_2048 = -0.000514642 + 1.00011 * (_ctx_2048t + 0.3 * jax.random.normal(jax.random.fold_in(_rk, 611), (64, 64, 256), jnp.float32))
        _validS = jnp.arange(64)[None, :] < _lenS[:, None]
        _validS2 = jnp.arange(64)[None, :] < _lenS2[:, None]
        _causal = jnp.tril(jnp.ones((64, 64), dtype=bool))
        mask_BxS2_if0 = jnp.where(jnp.ones((64, 64), dtype=bool), 4, 0).astype(jnp.int32)
        _g = jax.random.normal(jax.random.fold_in(_rk, 9001), (2, 2), jnp.float32)
        _g = jnp.sign(_g) * jnp.maximum(jnp.abs(_g), 1.0) + (_g == 0) * 1.0
        g_xattn = _g[0]
        g_ffn = _g[1]
        return (x, ctx_2048, mask_BxS2_if0, g_xattn, g_ffn)
    x, ctx_2048, mask_BxS2_if0, g_xattn, g_ffn = _rec_inputs()

    def _L0_xattn_setup():
        import jax, jax.numpy as jnp
        import numpy as np
        NUM_HEADS = 16
        key = jax.random.key(seed)
        ks = jax.random.split(key, 5)
        dim = 128
        B, N, N_c = (4, 128, 32)
        x = jax.random.normal(ks[0], (B, N, dim), dtype=jnp.float32)
        context = jax.random.normal(ks[1], (B, N_c, 2 * dim), dtype=jnp.float32)
        w_qkv = jax.random.normal(ks[2], (3 * dim, dim), dtype=jnp.float32) * 0.02
        w_proj = jax.random.normal(ks[3], (dim, dim), dtype=jnp.float32) * 0.02
        b_proj = jax.random.normal(ks[4], (dim,), dtype=jnp.float32) * 0.02
        return {'x': x, 'context': context, 'w_qkv': w_qkv, 'w_proj': w_proj, 'b_proj': b_proj}
    _L0_xattn_all = _L0_xattn_setup()
    _L0_xattn_in = {k: v for k, v in _L0_xattn_all.items() if k in ('w_qkv', 'w_proj', 'b_proj')}
    del _L0_xattn_all

    def _L0_ffn_setup():
        import jax, jax.numpy as jnp
        import numpy as np
        H = 128
        I = 256
        E = 8
        B, S = (2, 128)

        def _swiglu(x, wg, wu, wd):
            return jax.nn.silu(x @ wg) * (x @ wu) @ wd
        key = jax.random.key(seed)
        ks = jax.random.split(key, 8)
        sc_h = 1.0 / np.sqrt(H)
        sc_i = 1.0 / np.sqrt(I)
        return {'hidden_states': jax.random.normal(ks[0], (B, S, H), jnp.float32), 'gate_w': jax.random.normal(ks[1], (H, E), jnp.float32) * sc_h, 'sh_gate': jax.random.normal(ks[2], (H, I), jnp.float32) * sc_h, 'sh_up': jax.random.normal(ks[3], (H, I), jnp.float32) * sc_h, 'sh_down': jax.random.normal(ks[4], (I, H), jnp.float32) * sc_i, 'rt_gate': jax.random.normal(ks[5], (E, H, I), jnp.float32) * sc_h, 'rt_up': jax.random.normal(ks[6], (E, H, I), jnp.float32) * sc_h, 'rt_down': jax.random.normal(ks[7], (E, I, H), jnp.float32) * sc_i}
    _L0_ffn_all = _L0_ffn_setup()
    _L0_ffn_in = {k: v for k, v in _L0_ffn_all.items() if k in ('gate_w', 'sh_gate', 'sh_up', 'sh_down', 'rt_gate', 'rt_up', 'rt_down')}
    del _L0_ffn_all

    def _L1_xattn_setup():
        import jax, jax.numpy as jnp
        import numpy as np
        B, L, P = (4, 512, 128)
        D_MODEL = 128
        D_GLOBAL = 256
        HEADDIM = 32
        EPSILON = 0.001
        RMS_EPS = 1e-05

        def rmsnorm(x, g, eps=RMS_EPS):
            var = jnp.mean(jnp.square(x), axis=-1, keepdims=True)
            return x * jax.lax.rsqrt(var + eps) * g

        def _hnet_depool(h, h_patch_full, patch_lens):
            h_patch = h_patch_full[..., :D_MODEL]
            bsz, plen = (h_patch.shape[0], h_patch.shape[1])
            seqlen = h.shape[1]
            logp = jnp.full((bsz, plen), -EPSILON, dtype=jnp.float32)
            bidx = jnp.cumsum(patch_lens, axis=1) - 1
            boundary_mask = jnp.zeros((bsz, seqlen), dtype=jnp.int32)
            boundary_mask = boundary_mask.at[jnp.arange(bsz)[:, None], bidx].set(1)
            dt = (-jnp.log(-jnp.expm1(logp))).astype(h_patch.dtype)
            x = h_patch / dt[..., None]
            n_heads = D_MODEL // HEADDIM
            A = -jnp.ones((n_heads,), dtype=jnp.float32)
            bcoef = jnp.exp(logp).astype(h_patch.dtype)
            x4 = x.reshape(bsz, plen, n_heads, HEADDIM)
            a = jnp.exp(dt[:, :, None] * A[None, None, :])
            u = (dt * bcoef)[:, :, None, None] * x4
            a_b = jnp.broadcast_to(a[..., None], u.shape)

            def comb(lft, rgt):
                aL, uL = lft
                aR, uR = rgt
                return (aL * aR, uL * aR + uR)
            _, s = jax.lax.associative_scan(comb, (a_b, u), axis=1)
            depool = s.reshape(bsz, plen, D_MODEL)
            plug = jnp.clip(jnp.cumsum(boundary_mask, axis=1) - 1, 0, plen - 1)
            depool_out = depool[jnp.arange(bsz)[:, None], plug]
            return depool_out + h
        key = jax.random.key(seed)
        k1, k2, k3, k4 = jax.random.split(key, 4)
        embeds = jax.random.normal(k1, (B, L, D_MODEL), dtype=jnp.float32)
        patch_embeds = jax.random.normal(k2, (B, P, D_GLOBAL), dtype=jnp.float32)
        patch_lens = jnp.full((B, P), L // P, dtype=jnp.int64)
        W_in = jax.random.normal(k3, (D_MODEL, D_MODEL), dtype=jnp.float32) * 0.02
        b_in = jnp.zeros((D_MODEL,), dtype=jnp.float32)
        g_res = jnp.ones((D_MODEL,), dtype=jnp.float32)
        g_init = jnp.ones((D_GLOBAL,), dtype=jnp.float32)
        return {'embeds': embeds, 'patch_embeds': patch_embeds, 'patch_lens': patch_lens, 'W_in': W_in, 'b_in': b_in, 'g_res': g_res, 'g_init': g_init}
    _L1_xattn_all = _L1_xattn_setup()
    _L1_xattn_in = {k: v for k, v in _L1_xattn_all.items() if k in ('W_in', 'b_in', 'g_res', 'g_init')}
    del _L1_xattn_all

    def _L1_ffn_setup():
        import jax, jax.numpy as jnp
        import numpy as np
        TOP_K = 2
        key = jax.random.key(seed)
        ks = jax.random.split(key, 5)
        B, S, H, E = (2, 128, 128, 8)
        return {'hidden_states': jax.random.normal(ks[0], (B, S, H), dtype=jnp.float32), 'router_w': jax.random.normal(ks[1], (E, H), dtype=jnp.float32) * 0.02, 'router_b': jax.random.normal(ks[2], (E,), dtype=jnp.float32) * 0.02, 'expert_w': jax.random.normal(ks[3], (E, H, H), dtype=jnp.float32) * 0.02, 'expert_b': jax.random.normal(ks[4], (E, H), dtype=jnp.float32) * 0.02}
    _L1_ffn_all = _L1_ffn_setup()
    _L1_ffn_in = {k: v for k, v in _L1_ffn_all.items() if k in ('router_w', 'router_b', 'expert_w', 'expert_b')}
    del _L1_ffn_all
    return {'x': x, 'ctx_2048': ctx_2048, 'mask_BxS2_if0': mask_BxS2_if0, 'g_xattn': g_xattn, 'g_ffn': g_ffn, 'L0_xattn_w_qkv': _L0_xattn_in['w_qkv'], 'L0_xattn_w_proj': _L0_xattn_in['w_proj'], 'L0_xattn_b_proj': _L0_xattn_in['b_proj'], 'L0_ffn_gate_w': _L0_ffn_in['gate_w'], 'L0_ffn_sh_gate': _L0_ffn_in['sh_gate'], 'L0_ffn_sh_up': _L0_ffn_in['sh_up'], 'L0_ffn_sh_down': _L0_ffn_in['sh_down'], 'L0_ffn_rt_gate': _L0_ffn_in['rt_gate'], 'L0_ffn_rt_up': _L0_ffn_in['rt_up'], 'L0_ffn_rt_down': _L0_ffn_in['rt_down'], 'L1_xattn_W_in': _L1_xattn_in['W_in'], 'L1_xattn_b_in': _L1_xattn_in['b_in'], 'L1_xattn_g_res': _L1_xattn_in['g_res'], 'L1_xattn_g_init': _L1_xattn_in['g_init'], 'L1_ffn_router_w': _L1_ffn_in['router_w'], 'L1_ffn_router_b': _L1_ffn_in['router_b'], 'L1_ffn_expert_w': _L1_ffn_in['expert_w'], 'L1_ffn_expert_b': _L1_ffn_in['expert_b']}

def reference(x, ctx_2048, mask_BxS2_if0, g_xattn, g_ffn, L0_xattn_w_qkv, L0_xattn_w_proj, L0_xattn_b_proj, L0_ffn_gate_w, L0_ffn_sh_gate, L0_ffn_sh_up, L0_ffn_sh_down, L0_ffn_rt_gate, L0_ffn_rt_up, L0_ffn_rt_down, L1_xattn_W_in, L1_xattn_b_in, L1_xattn_g_res, L1_xattn_g_init, L1_ffn_router_w, L1_ffn_router_b, L1_ffn_expert_w, L1_ffn_expert_b):
    import jax
    import jax.numpy as jnp

    def _L0_xattn_ref(x, context, w_qkv, w_proj, b_proj):
        import jax, jax.numpy as jnp
        import numpy as np
        NUM_HEADS = 16
        B, N, C = x.shape
        H = NUM_HEADS
        D = C // H
        scale = D ** (-0.5)
        qkv = (x @ w_qkv.T).reshape(B, N, 3, H, D).transpose(2, 0, 3, 1, 4)
        q, k, v = (qkv[0], qkv[1], qkv[2])
        N_c = context.shape[1]
        kv = context.reshape(B, N_c, 2, H, D).transpose(2, 0, 3, 1, 4)
        extra_k, extra_v = (kv[0], kv[1])
        k = jnp.concatenate([extra_k, k], axis=2)
        v = jnp.concatenate([extra_v, v], axis=2)
        dtype = q.dtype
        attn = jnp.einsum('bhnd,bhmd->bhnm', q * scale, k).astype(jnp.float32)
        attn = jax.nn.softmax(attn, axis=-1).astype(dtype)
        out = jnp.einsum('bhnm,bhmd->bhnd', attn, v)
        out = out.transpose(0, 2, 1, 3).reshape(B, N, C)
        return out @ w_proj.T + b_proj

    def _L0_ffn_ref(hidden_states, gate_w, sh_gate, sh_up, sh_down, rt_gate, rt_up, rt_down):
        import jax, jax.numpy as jnp
        import numpy as np
        H = 128
        I = 256
        E = 8
        B, S = (2, 128)

        def _swiglu(x, wg, wu, wd):
            return jax.nn.silu(x @ wg) * (x @ wu) @ wd
        b, s, h = hidden_states.shape
        x = hidden_states.reshape(-1, h)
        logits = x @ gate_w
        top_val = jnp.max(logits, axis=-1, keepdims=True)
        top_id = jnp.argmax(logits, axis=-1)
        score = jax.nn.sigmoid(top_val)
        xs = x * score
        g = jnp.einsum('th,ehi->eti', xs, rt_gate)
        u = jnp.einsum('th,ehi->eti', xs, rt_up)
        act = jax.nn.silu(g) * u
        y = jnp.einsum('eti,eih->eth', act, rt_down)
        onehot = jax.nn.one_hot(top_id, E, dtype=x.dtype)
        routed = jnp.einsum('eth,te->th', y, onehot)
        shared = _swiglu(x, sh_gate, sh_up, sh_down)
        return (shared + routed).reshape(b, s, h)

    def _L1_xattn_ref(embeds, patch_embeds, patch_lens, W_in, b_in, g_res, g_init):
        import jax, jax.numpy as jnp
        import numpy as np
        B, L, P = (4, 512, 128)
        D_MODEL = 128
        D_GLOBAL = 256
        HEADDIM = 32
        EPSILON = 0.001
        RMS_EPS = 1e-05

        def rmsnorm(x, g, eps=RMS_EPS):
            var = jnp.mean(jnp.square(x), axis=-1, keepdims=True)
            return x * jax.lax.rsqrt(var + eps) * g

        def _hnet_depool(h, h_patch_full, patch_lens):
            h_patch = h_patch_full[..., :D_MODEL]
            bsz, plen = (h_patch.shape[0], h_patch.shape[1])
            seqlen = h.shape[1]
            logp = jnp.full((bsz, plen), -EPSILON, dtype=jnp.float32)
            bidx = jnp.cumsum(patch_lens, axis=1) - 1
            boundary_mask = jnp.zeros((bsz, seqlen), dtype=jnp.int32)
            boundary_mask = boundary_mask.at[jnp.arange(bsz)[:, None], bidx].set(1)
            dt = (-jnp.log(-jnp.expm1(logp))).astype(h_patch.dtype)
            x = h_patch / dt[..., None]
            n_heads = D_MODEL // HEADDIM
            A = -jnp.ones((n_heads,), dtype=jnp.float32)
            bcoef = jnp.exp(logp).astype(h_patch.dtype)
            x4 = x.reshape(bsz, plen, n_heads, HEADDIM)
            a = jnp.exp(dt[:, :, None] * A[None, None, :])
            u = (dt * bcoef)[:, :, None, None] * x4
            a_b = jnp.broadcast_to(a[..., None], u.shape)

            def comb(lft, rgt):
                aL, uL = lft
                aR, uR = rgt
                return (aL * aR, uL * aR + uR)
            _, s = jax.lax.associative_scan(comb, (a_b, u), axis=1)
            depool = s.reshape(bsz, plen, D_MODEL)
            plug = jnp.clip(jnp.cumsum(boundary_mask, axis=1) - 1, 0, plen - 1)
            depool_out = depool[jnp.arange(bsz)[:, None], plug]
            return depool_out + h
        h = rmsnorm(embeds, g_res)
        h = jnp.einsum('bld,ed->ble', h, W_in) + b_in
        h_patch = rmsnorm(patch_embeds, g_init)
        return _hnet_depool(h, h_patch, patch_lens)

    def _L1_ffn_ref(hidden_states, router_w, router_b, expert_w, expert_b):
        import jax, jax.numpy as jnp
        import numpy as np
        TOP_K = 2
        logits = jnp.einsum('bsh,eh->bse', hidden_states, router_w) + router_b
        routing_weights = jax.nn.softmax(logits, axis=-1)
        _, top_k_indices = jax.lax.top_k(routing_weights, TOP_K)
        E = router_w.shape[0]
        mask = jax.nn.one_hot(top_k_indices, E, dtype=hidden_states.dtype).sum(axis=-2)
        out = jnp.einsum('bse,ehd,bsd->bsh', mask, expert_w, hidden_states)
        out = out + jnp.einsum('bse,eh->bsh', mask, expert_b)
        return out
    x = x + jnp.tanh(g_xattn[0]) * _L0_xattn_ref(_layernorm(x, axis=-1), ctx_2048, L0_xattn_w_qkv, L0_xattn_w_proj, L0_xattn_b_proj)
    x = x + jnp.tanh(g_ffn[0]) * _L0_ffn_ref(_layernorm(x, axis=-1), L0_ffn_gate_w, L0_ffn_sh_gate, L0_ffn_sh_up, L0_ffn_sh_down, L0_ffn_rt_gate, L0_ffn_rt_up, L0_ffn_rt_down)
    x = x + jnp.tanh(g_xattn[1]) * _L1_xattn_ref(_layernorm(x, axis=-1), ctx_2048, mask_BxS2_if0, L1_xattn_W_in, L1_xattn_b_in, L1_xattn_g_res, L1_xattn_g_init)
    x = x + jnp.tanh(g_ffn[1]) * _L1_ffn_ref(_layernorm(x, axis=-1), L1_ffn_router_w, L1_ffn_router_b, L1_ffn_expert_w, L1_ffn_expert_b)
    return x

_drawn_inputs = setup_inputs


def setup_inputs(seed=0):
    import zlib

    import numpy as np

    out = dict(_drawn_inputs(seed))
    spreads = {'g_ffn': (-1.0, 0.6),
     'L1_xattn_b_in': (0.0, 0.1),
     'L1_xattn_g_res': (1.0, 0.2),
     'L1_xattn_g_init': (1.0, 0.2)}
    factors = {'L0_xattn_w_qkv': 3.692, 'L1_ffn_expert_b': 3.806}
    for name, (base, spread) in spreads.items():
        noise = np.random.default_rng([zlib.crc32(name.encode()), seed]).standard_normal(out[name].shape)
        drawn = base * np.exp(spread * noise) if base else spread * noise
        out[name] = jnp.asarray(drawn.astype(out[name].dtype))
    for name, factor in factors.items():
        out[name] = (out[name] * factor).astype(out[name].dtype)
    return out
```

```python
from contextlib import ExitStack

import numpy as np

import concourse.bass as bass
from concourse import mybir

F32 = mybir.dt.float32
F16 = mybir.dt.float16
BF16 = mybir.dt.bfloat16
I32 = mybir.dt.int32
U32 = mybir.dt.uint32
ALU = mybir.AluOpType
ACT = mybir.ActivationFunctionType
AX = mybir.AxisListType
ds = bass.ds

P = 128
CREDIT = 2
TURN = 4
EPS = 1e-5


class Tile:

    def __init__(self, n, turn=None, unroll=TURN):
        self.n, self.turn = n, turn
        self.t = n if turn is None else n + unroll * turn
        self.pair = n // 2 if turn is None else n // 2 + unroll // 2 * turn
        self.par, self.slot = n % 2, n % 4

    def cols(self, width):
        return ds(self.t * width, width)

    def done(self, per_tile=1, event=0):
        return (self.t + CREDIT) * per_tile + event + 1

    def freed(self, per_tile=1, event=0, back=None):
        back = CREDIT * per_tile if back is None else back
        return (self.t + CREDIT) * per_tile + event + 1 - back


def walk(eng, tiles, depth, step, before_loop=None, unroll=TURN):
    first = -(-depth // unroll) * unroll
    assert tiles % unroll == 0 and tiles > first

    def peeled(s):
        step(lambda lag: Tile(s - lag) if 0 <= s - lag < tiles else None)

    for s in range(first):
        peeled(s)
    if before_loop:
        before_loop()
    with eng.Fori(0, (tiles - first) // unroll) as turn:
        for k in range(unroll):
            step(lambda lag: Tile(first + k - lag, turn, unroll))
    for s in range(tiles, tiles + depth):
        peeled(s)


def when(eng, sem, value):
    eng.wait_ge(sem, value)


def hold(eng, sem, value):
    eng.wait_ge(sem, value)
    eng.nop(nofuse=True)


def flamingo_gated_two_layers(nc, x, ctx_k, ctx_v_swapped, consts, gates, w_qkv, w_proj, b_proj, gate_w,
                              sh_gate_up, sh_down, rt_gate_up, rt_down, patch_mask, w_in, b_in, g_res, g_init,
                              router_w, router_b, expert_w, expert_b, out):
    NT = x.shape[1] // P
    D = P
    H, HD = 16, 8
    HG, G = 4, 4
    SEQ = 64
    E = 8
    FF = 256
    PAIRS = P // SEQ
    NS = (NT * P + E * (P - 1)) // P
    NS += -NS % TURN
    CT = 4
    NC = NT // CT
    LAGS = 6

    with ExitStack() as ctx:
        def sb(name, shape, dt=F32):
            return ctx.enter_context(nc.sbuf_tensor(name, shape, dt))

        def sem(name):
            return ctx.enter_context(nc.semaphore(name))

        X = sb("X", [P, NT * D])
        CK = sb("CK", [P, NT * D])
        CV = sb("CV", [P, NT * D])
        VALL = sb("VALL", [P, NT * D])
        CW = [P, P, P, P, E, E, NS, 1, SEQ]
        CO = [sum(CW[:i]) for i in range(len(CW))]
        cst = sb("cst", [P, sum(CW)])
        identf, upper, ones, decay, exp_no, exp_no8, tile_start, patch_no, place_no = (
            cst[:, o:o + w] for o, w in zip(CO, CW))
        ident16 = sb("ident16", [P, P], F16)
        halfneg = sb("halfneg", [P, 1])
        epsc = sb("epsc", [P, 1])
        gate = sb("gate", [P, 4])
        tgate = sb("tgate", [P, 4])
        wqkv = sb("wqkv", [P, 3 * D])
        wproj = sb("wproj", [P, D])
        bproj = sb("bproj", [P, D])
        st = sb("st", [P, 2, 6])
        mv = sb("mv", [P, 2, 2])
        ve = sb("ve", [P, 2])
        rstd = sb("rstd", [P, 2])
        xn = sb("xn", [P, 2, D])
        xnT = sb("xnT", [P, 2, P])
        stack = sb("stack", [P, 2, 3, H, 32], F16)
        qc = sb("qc", [P, G, P], F16)
        kt = sb("kt", [P, 4, 2, G, P], F16)
        vp = sb("vp", [P, 2, 2, H, 32])
        arena = sb("arena", [P, NS * D])
        negm = sb("negm", [P, 2, HG, G], F16)
        mT = sb("mT", [H, 2, P], F16)
        qbd = arena[:, 0:4 * G * HG * P // 2].bitcast(F16).rearrange("p (s g h t) -> p s g h t", s=4, g=G, h=HG)
        pexp = sb("pexp", [P, 4, 512])
        oS = sb("oS", [P, 2, 512])
        rden = sb("rden", [P, 2, H])
        on = sb("on", [P, 2, D])
        onT = sb("onT", [P, 2, P])

        spare = stack.rearrange("p s w h c -> p (s w h c)").bitcast(F32)
        def twin(k):
            return spare[:, k * 2 * D:(k + 1) * 2 * D].rearrange("p (s d) -> p s d", s=2)

        XN2 = VALL
        XNT = sb("XNT", [P, NT * P])
        gatew = sb("gatew", [P, 64])
        LG = onT.rearrange("p s d -> p (s d)").rearrange("p (t e) -> p t e", e=E)
        top = sb("top", [P, NT])
        score = sb("score", [P, NT])
        isel = spare[:, 800:800 + NT * E].rearrange("p (t e) -> p t e", e=E)
        first8 = sb("first8", [P, NT])
        onehot = sb("onehot", [P, E, NT], BF16)
        upper16 = sb("upper16", [P, P], BF16)
        ones16 = sb("ones16", [P, P], BF16)
        tot = spare[:, 1056:1056 + NT * E].rearrange("p (e t) -> p e t", e=E)
        run = on.rearrange("p s d -> p (s d)").rearrange("p (e t) -> p e t", e=E)
        onesf = sb("onesf", [P, E * NT])
        cnt = sb("cnt", [P, 6, E])
        cnti = sb("cnti", [P, 2, E], I32)
        posf = sb("posf", [P, NT])
        posu = sb("posu", [P, NT], U32)
        tcmp = spare[:, 512:512 + NS * (E - 1)].rearrange("p (s e) -> p s e", e=E - 1)
        texpf = sb("texpf", [P, NS])
        texp = sb("texp", [P, NS], I32)
        shgu = sb("shgu", [P, 2 * FF])
        shd = sb("shd", [P, FF])
        rgu = sb("rgu", [P, E * 2 * FF])
        rdn = sb("rdn", [P, E * FF])
        sg = oS
        hact = pexp.rearrange("p (c i) t -> p c i t", c=2)
        XS = sb("XS", [P, NS * D])
        zeros = XS[:, 0:8 * D]
        xs = qc.rearrange("p g t -> p (g t)").bitcast(F32).rearrange("p (s d) -> p s d", s=2)
        xsT = sb("xsT", [P, 2, P])
        act2T = spare[:, 0:2 * FF].rearrange("p (s f) -> p s f", s=2)
        YS = arena
        ssk = sb("ssk", [P, NT])
        ssv = sb("ssv", [P, 2, NT])
        sqj = sb("sqj", [P, 2, D], BF16)
        crms = sb("crms", [P, NT])
        pm_i = sb("pm_i", [SEQ, SEQ], I32)
        pm = sb("pm", [SEQ, 6, SEQ])
        pcmp = kt[0:SEQ].rearrange("p s b g t -> p (s b g t)").bitcast(BF16).rearrange("p (a b) -> p a b", a=SEQ)
        winT = sb("winT", [P, D])
        binB = sb("binB", [P, D])
        gres = sb("gres", [P, 1])
        ginit = sb("ginit", [P, D])
        rw1 = sb("rw1", [P, 64])
        rb1 = sb("rb1", [P, E])
        w1 = sb("w1", [P, E * D])
        b1 = sb("b1", [E, D])
        mvl = sb("mvl", [P, 2, 2])
        mv2 = sb("mv2", [P, 2, 2])
        rchain = sb("rchain", [P, 2, 6])
        rr = sb("rr", [P, 2])
        hn, hnT = on, onT
        hp, dp, pick, zs = twin(2), twin(3), twin(4), twin(5)
        lg1 = sb("lg1", [P, 2, E])
        mx8 = sb("mx8", [P, 2, 8])
        ix8 = sb("ix8", [P, 2, 8], U32)
        ixf = sb("ixf", [P, 2, 2])
        mask1 = sb("mask1", [P, 2, 2, E])
        mask1T = sb("mask1T", [E, 2, P])
        z = vp.rearrange("p s b h c -> p s (b h c)")

        sorted_x = nc.dram_tensor("sorted_x", (NS * P, D), F32).ap()
        sorted_y = nc.dram_tensor("sorted_y", (NS * P, D), F32).ap()
        plugs = nc.dram_tensor("plugs", (NT * PAIRS, SEQ), F32).ap()

        PS = ctx.enter_context(nc.psum_tensor("PS", [P, 8, 512], F32))

        def hi_twice(par, w):
            at = stack[:, par, w, :, 0:16 if w == 0 else 32].rearrange("p h (c d) -> p h c d", c=2)
            return at[:, :, :, 0:8]

        def twice_over(src):
            return src.unsqueeze(2).to_broadcast([P, H, 2, HD])

        def bank16(b):
            return PS[:, b, :].bitcast(F16)

        TILE_CHUNKS = [(0, 2), (2, 8), (8, NT)]
        x_in = [sem(f"x_in{c}") for c in range(3)]
        ck_in = [sem(f"ck_in{c}") for c in range(3)]
        cv_in = [sem(f"cv_in{c}") for c in range(3)]
        consts_in = sem("consts_in")
        weights_in = sem("weights_in")
        weights_ready = sem("weights_ready")
        pool_consts = sem("pool_consts")
        gates_ready = sem("gates_ready")
        names = ("stats moments normed var_eps rstd_ready bias_added hi_ready v_kept lo_ready "
                 "ctx_hi v_half ctx_stacked xnT_done qkv_done xnT_kept qk_turned ctx_turned q_kept q_spread "
                 "k_kept ctx_kept scored maxed max_turned max_kept scored_t exped v_spread averaged "
                 "o_kept o_turned recip_ready o_normed on_turned on_kept projected x_updated")
        S = {n: sem("a_" + n) for n in names.split()}
        shift_placed = [sem("a_shift_placed0"), sem("a_shift_placed1")]
        for n in "stats moments var_eps rstd_ready normed kept xnT_done xnT_kept routed logits".split():
            S["r_" + n] = sem("r_" + n)
        more_in = sem("more_in")
        late_in = sem("late_in")
        late_ready = sem("late_ready")
        bias_ready = sem("bias_ready")
        zeroed = sem("zeroed")
        zero_tile = sem("zero_tile")
        sort_step = sem("sort_step")
        score_ready = sem("score_ready")
        ranked = sem("ranked")
        texp_ready = sem("texp_ready")
        scaled = sem("scaled")
        scattered = sem("scattered")
        for n in "gated lifted acted down added squared".split():
            S["h_" + n] = sem("h_" + n)
        xs_in = [sem(f"xs_in{c}") for c in range(NS // 8)]
        for n in "xs_in copied turned turned_kept lifted gated acted act_turned act_kept down kept".split():
            S["e_" + n] = sem("e_" + n)
        stored = sem("stored")
        y_in = [sem(f"y_in{c}") for c in range(NT // 4)]
        swapped = sem("swapped")
        swap_in = sem("swap_in")
        crms_step = sem("crms_step")
        plug_step = sem("plug_step")
        plug_out = sem("plug_out")
        plug_in = sem("plug_in")
        places_cleared = sem("places_cleared")
        for n in ("y_in x2 stats moments p0 p1 p2 p3 p4 p5 zb ixf rr normed hnT_done hnT_kept hp_ready picked depooled dp_ready "
                  "mixed x3 stats2 moments2 q0 rstd2 normed2 xnT_done xnT_kept routed lg m8 i8 mk0 mask_ready "
                  "mask_turned mask_kept lifted biased scaled_a scaled_v summed out_ready").split():
            S["l_" + n] = sem("l_" + n)
        out_done = sem("out_done")
        PLUG_STEPS = 8

        block = ctx.enter_context(nc.Block())

        def arrived(eng, sems, tile):
            if tile is not None and tile.turn is None:
                for c, (lo, _) in enumerate(TILE_CHUNKS):
                    if tile.n == lo:
                        hold(eng, sems[c], 16)

        def credit(eng, *entries):
            for name, per_tile in entries:
                eng.sem_inc(S[name], CREDIT * per_tile)

        @block.sync
        def _(sp):
            sp.dma_start(X[:, 0:2 * D], x[:, 0:2 * D]).then_inc(x_in[0], 16)
            sp.dma_start(cst[:], consts).then_inc(consts_in, 16)
            sp.dma_start(CK[:, 0:2 * D], ctx_k[:, 0:2 * D]).then_inc(ck_in[0], 16)
            sp.dma_start(wqkv[:], w_qkv).then_inc(weights_in, 16)
            sp.dma_start(gate[:], gates).then_inc(consts_in, 16)
            sp.dma_start(wproj[:], w_proj).then_inc(weights_in, 16)
            sp.dma_start(bproj[:], b_proj).then_inc(weights_in, 16)
            for c in range(3):
                lo, hi = TILE_CHUNKS[c]
                if c:
                    sp.dma_start(X[:, lo * D:hi * D], x[:, lo * D:hi * D]).then_inc(x_in[c], 16)
                    sp.dma_start(CK[:, lo * D:hi * D], ctx_k[:, lo * D:hi * D]).then_inc(ck_in[c], 16)
                sp.dma_start(CV[:, lo * D:hi * D], ctx_v_swapped[:, lo * D:hi * D]).then_inc(cv_in[c], 16)
            for dst, src in ((gatew, gate_w), (shgu, sh_gate_up), (pm_i, patch_mask)):
                sp.dma_start(dst[:], src).then_inc(more_in, 16)
            for dst, src in ((shd, sh_down), (rgu, rt_gate_up), (rdn, rt_down), (winT, w_in), (binB, b_in),
                             (gres, g_res), (ginit, g_init), (rw1, router_w), (rb1, router_b), (w1, expert_w),
                             (b1, expert_b)):
                sp.dma_start(dst[:], src).then_inc(late_in, 16)
            sp.wait_ge(zero_tile, 1)
            sx = sorted_x.rearrange("(c p r) d -> c p (r d)", p=P, r=8)
            for c in range(NS // 8):
                sp.dma_start(sx[c], zeros).then_inc(zeroed, 16)

            def step(stage):
                a = stage(3)
                if a:
                    when(sp, S["max_kept"], a.done())
                    for hg in range(HG):
                        sp.dma_start(qbd[32 * hg + 24:32 * hg + 25, a.slot, :, hg, :],
                                     mT[HG * hg:HG * hg + G, a.par, :]).then_inc(shift_placed[a.par], 16)

            walk(sp, NT, LAGS, step)
            credit(sp, ("e_xs_in", 1), ("l_y_in", 1))
            sp.wait_ge(scattered, 16 * NT)
            for c in range(NS // 8):
                sp.dma_start(XS[:, c * 8 * D:(c + 1) * 8 * D].rearrange("p (t d) -> p t d", t=8),
                             sorted_x[c * 8 * P:(c + 1) * 8 * P].rearrange("(t p) d -> p t d", p=P))\
                    .then_inc(xs_in[c], 16)
            for c in range(NS // 8):
                sp.wait_ge(xs_in[c], 16)
                sp.sem_inc(S["e_xs_in"], 8)
            sp.wait_ge(plug_step, PLUG_STEPS)
            sp.dma_start(plugs, pm[:, 5, :]).then_inc(plug_out, 16)
            sp.wait_ge(plug_out, 16)
            sp.wait_ge(places_cleared, 1)
            for q in range(PAIRS):
                rows = slice(SEQ * q, SEQ * q + SEQ)
                sp.dma_start(XNT[rows].rearrange("p (t s) -> p t s", t=NT)[:, :, SEQ * q:SEQ * q + SEQ],
                             plugs.rearrange("(t q) s -> q t s", q=PAIRS)[q:q + 1].to_broadcast([SEQ, NT, SEQ]))\
                    .then_inc(plug_in, 16)
            sp.wait_ge(S["h_squared"], Tile(NC - 1).done(2 * CT, 2 * CT - 1))
            for q in range(PAIRS):
                sp.dma_start(ssv[SEQ * q:SEQ * q + SEQ, 1, :], ssv[SEQ * (1 - q):SEQ * (2 - q), 0, :])\
                    .then_inc(swap_in, 16)

            def store(stage):
                d = stage(4)
                if d:
                    when(sp, S["e_kept"], d.done())
                    sp.dma_start(sorted_y[ds(d.t * P, P)], YS[:, d.cols(D)]).then_inc(stored, 16)

            walk(sp, NS, 4, store)
            for c in range(NT // 4):
                sp.wait_ge(y_in[c], 64)
                sp.sem_inc(S["l_y_in"], 4)

            def store_out(stage):
                o = stage(5)
                if o:
                    when(sp, S["l_out_ready"], o.done())
                    sp.dma_start(out[:, o.cols(D)], X[:, o.cols(D)]).then_inc(out_done, 16)

            walk(sp, NT, 5, store_out)
            sp.wait_ge(out_done, 16 * NT)

        @block.gpsimd
        def _(pool):
            credit(pool, ("rstd_ready", 1), ("var_eps", 1), ("bias_added", 1), ("v_spread", 1),
                   ("v_half", 1))
            pool.memset(zeros, 0.0).then_inc(zero_tile, 1)
            pool.memset(halfneg[:], -0.5)
            pool.memset(epsc[:], EPS)
            pool.memset(stack[:], 0.0)
            pool.memset(vp[:], 1.0).then_inc(pool_consts, 1)
            hold(pool, pool_consts, 1)
            pool.memset(stack[:, :, 1:3, :, 24:25], 1.0)
            pool.memset(qbd, 0.0).then_inc(pool_consts, 1)
            hold(pool, pool_consts, 2)

            def step(stage):
                l, f, a = stage(0), stage(1), stage(4)
                if a:
                    arrived(pool, cv_in, a)
                    hold(pool, S["v_kept"], a.done())
                    hold(pool, S["averaged"], a.freed(4, 3))
                    if f:
                        hold(pool, S["bias_added"], f.freed(back=1))
                    for half in range(2):
                        if half:
                            hold(pool, S["v_half"], a.done())
                        rows = slice(64 * half, 64 * half + 64)
                        pool.tensor_copy(vp[rows, a.par, half, :, 0:HD],
                                         VALL[rows, a.cols(D)].rearrange("p (h d) -> p h d", h=H))
                        pool.tensor_copy(vp[rows, a.par, 1 - half, :, 0:HD],
                                         CV[rows, a.cols(D)].rearrange("p (h d) -> p h d", h=H))\
                            .then_inc(S["v_spread" if half else "v_half"], 1)
                    hold(pool, S["v_spread"], a.done())
                if l:
                    hold(pool, S["moments"], l.done())
                    pool.tensor_tensor(ve[:, l.par:l.par + 1], mv[:, l.par, 1:2], epsc[:], ALU.add)\
                        .then_inc(S["var_eps"], 1)
                    when(pool, S["var_eps"], l.done())
                    pool.tensor_tensor(rstd[:, l.par:l.par + 1], ve[:, l.par:l.par + 1], halfneg[:], ALU.pow)\
                        .then_inc(S["rstd_ready"], 1)
                if f:
                    hold(pool, S["normed"], f.done())
                    if f.turn is None and f.n == 0:
                        hold(pool, weights_ready, 3)
                    xt = X[:, f.cols(D)]
                    pool.tensor_tensor(xt, xt, bproj[:], ALU.add).then_inc(S["bias_added"], 1)

            def loads():
                hold(pool, cv_in[2], 16)

            walk(pool, NT, LAGS, step, loads)

            def inverse_root(l, moments, done):
                hold(pool, S[moments], l.done())
                pool.tensor_tensor(ve[:, l.par:l.par + 1], mv[:, l.par, 1:2], epsc[:], ALU.add)\
                    .then_inc(S["r_var_eps"], 1)
                when(pool, S["r_var_eps"], l.done())
                pool.tensor_tensor(rstd[:, l.par:l.par + 1], ve[:, l.par:l.par + 1], halfneg[:], ALU.pow)\
                    .then_inc(S[done], 1)

            def router_step(stage):
                l = stage(0)
                if l:
                    inverse_root(l, "r_moments", "r_rstd_ready")

            credit(pool, ("r_var_eps", 1), ("r_rstd_ready", 1))
            walk(pool, NT, 2, router_step)

            hold(pool, late_in, 16 * 11)
            hold(pool, gates_ready, 1)
            for w, k in ((shd, 2), (rdn, 2), (binB, 1), (ginit, 1), (w1, 3)):
                pool.tensor_scalar(w[:], w[:], tgate[:, k:k + 1], None, ALU.mult).then_inc(late_ready, 1)
            pool.tensor_scalar(winT[:], winT[:], gres[:], tgate[:, 1:2], ALU.mult, ALU.mult).then_inc(late_ready, 1)

            hold(pool, zeroed, 16 * (NS // 8))
            for t in range(NT):
                if t % 8 == 0:
                    hold(pool, scaled, t // 8 + 1)
                pool.indirect_dma_start(out=sorted_x, out_offset=bass.IndirectOffsetOnAxis(ap=posu[:, t:t + 1], axis=0),
                                        in_=XN2[:, t * D:t * D + D], in_offset=None).then_inc(scattered, 16)
            hold(pool, S["h_lifted"], Tile(NC - 1).done(2, 1))
            pool.memset(XNT[:], -1.0).then_inc(places_cleared, 1)

            credit(pool, ("e_copied", 1))

            def sorted_step(stage):
                l = stage(0)
                if l:
                    hold(pool, S["e_xs_in"], l.done())
                    hold(pool, S["e_turned"], l.freed())
                    pool.tensor_copy(xs[:, l.par, :], XS[:, l.cols(D)]).then_inc(S["e_copied"], 1)

            walk(pool, NS, 4, sorted_step)

            hold(pool, crms_step, 2)
            pool.tensor_tensor(crms[:], crms[:], halfneg[:].to_broadcast([P, NT]), ALU.pow).then_inc(crms_step, 1)
            hold(pool, stored, 16 * NS)
            for t in range(NT):
                pool.indirect_dma_start(out=XN2[:, t * D:t * D + D], out_offset=None, in_=sorted_y,
                                        in_offset=bass.IndirectOffsetOnAxis(ap=posu[:, t:t + 1], axis=0))\
                    .then_inc(y_in[t // 4], 16)

            credit(pool, ("l_p0", 1), ("l_p1", 1), ("l_p2", 1), ("l_p3", 1), ("l_p4", 1), ("l_rr", 1),
                   ("l_q0", 1), ("l_rstd2", 1))

            def last_step(stage):
                l, s = stage(0), stage(2)
                if l:
                    k = slice(l.par, l.par + 1)
                    var = mvl[:, l.par, 1:2]
                    hold(pool, S["l_moments"], l.done())
                    for n, (o, a, c, op) in enumerate(((0, var, epsc[:], ALU.add), (1, None, halfneg[:], ALU.pow),
                                                       (2, var, None, ALU.mult), (3, None, 1, ALU.mult),
                                                       (4, None, epsc[:], ALU.add), (5, None, halfneg[:], ALU.pow))):
                        if n:
                            when(pool, S[f"l_p{n - 1}"], l.done())
                        prev = rchain[:, l.par, o - 1:o]
                        a = prev if a is None else a
                        c = prev if c is None else rchain[:, l.par, 1:2] if isinstance(c, int) else c
                        ins = pool.tensor_tensor(rchain[:, l.par, o:o + 1], a, c, op)
                        ins.then_inc(S["l_p5" if n == 5 else f"l_p{n}"], 1)
                    when(pool, S["l_p5"], l.done())
                    pool.tensor_tensor(rr[:, k], rchain[:, l.par, 1:2], rchain[:, l.par, 5:6], ALU.mult)\
                        .then_inc(S["l_rr"], 1)
                if s:
                    hold(pool, S["l_moments2"], s.done())
                    pool.tensor_tensor(ve[:, s.par:s.par + 1], mv2[:, s.par, 1:2], epsc[:], ALU.add)\
                        .then_inc(S["l_q0"], 1)
                    when(pool, S["l_q0"], s.done())
                    pool.tensor_tensor(rstd[:, s.par:s.par + 1], ve[:, s.par:s.par + 1], halfneg[:], ALU.pow)\
                        .then_inc(S["l_rstd2"], 1)

            credit(pool, ("l_p5", 1))
            walk(pool, NT, 5, last_step)

        @block.scalar
        def _(act):
            credit(act, ("xnT_kept", 1), ("exped", 4), ("on_kept", 1), ("hi_ready", 1), ("v_kept", 1),
                   ("max_kept", 1), ("o_kept", 1), ("ctx_hi", 1), ("q_kept", 1))
            act.wait_ge(consts_in, 32)
            nc.scalar.activation(tgate[:], gate[:], ACT.Tanh).then_inc(gates_ready, 1)

            def ctx_hi(f):
                arrived(act, ck_in, f)
                hold(act, S["ctx_turned"], f.freed())
                nc.scalar.copy(hi_twice(f.par, 2), twice_over(CK[:, f.cols(D)].rearrange("p (h d) -> p h d", h=H)))\
                    .then_inc(S["ctx_hi"], 1)

            def exp_chunk(b, j):
                when(act, S["scored_t"], b.done(4, j))
                hold(act, S["averaged"], b.freed(4, j, back=4))
                nc.scalar.activation(pexp[:, j, :], PS[:, 2 + j % 2, :], ACT.Exp).then_inc(S["exped"], 1)

            def step(stage):
                f, s, a, b, n = (stage(i) for i in (1, 2, 3, 5, 6))
                if s:
                    when(act, S["q_spread"], s.freed(back=1))
                    when(act, S["qk_turned"], s.done())
                    nc.scalar.copy(qc[:], bank16(5)[:, 0:512].rearrange("p (g t) -> p g t", g=G))\
                        .then_inc(S["q_kept"], 1)
                if b:
                    exp_chunk(b, 0)
                    exp_chunk(b, 1)
                if f:
                    when(act, S["qkv_done"], f.freed())
                    when(act, S["xnT_done"], f.done())
                    nc.scalar.copy(xnT[:, f.par, :], PS[:, 4, 0:P]).then_inc(S["xnT_kept"], 1)
                    if f.turn is None and f.n == 0:
                        hold(act, pool_consts, 2)
                    ctx_hi(f)
                if b:
                    exp_chunk(b, 2)
                if f:
                    when(act, S["qk_turned"], f.freed())
                    when(act, S["qkv_done"], f.done())
                    for w in range(2):
                        src = PS[:, 4, P * (1 + w):P * (2 + w)].rearrange("p (h d) -> p h d", h=H)
                        last = nc.scalar.copy(hi_twice(f.par, w), twice_over(src))
                    last.then_inc(S["hi_ready"], 1)
                    nc.scalar.copy(VALL[:, f.cols(D)], PS[:, 4, 3 * P:4 * P]).then_inc(S["v_kept"], 1)
                if b:
                    exp_chunk(b, 3)
                if n:
                    when(act, S["projected"], n.freed())
                    when(act, S["on_turned"], n.done())
                    nc.scalar.copy(onT[:, n.par, :], PS[:, 6, 0:P]).then_inc(S["on_kept"], 1)
                if a:
                    if not (a.turn is None and a.n < 2):
                        hold(act, shift_placed[a.par], 64 * a.pair)
                    when(act, S["max_turned"], a.done())
                    nc.scalar.copy(mT[:, a.par, :], bank16(0)[0:H, 0:P]).then_inc(S["max_kept"], 1)
                if b:
                    when(act, S["o_turned"], b.freed())
                    when(act, S["averaged"], b.done(4, 3))
                    nc.scalar.copy(oS[:, b.par, :], PS[:, 7, :]).then_inc(S["o_kept"], 1)

            walk(act, NT, LAGS, step, lambda: hold(act, ck_in[2], 16))

            credit(act, ("r_kept", 1), ("r_xnT_kept", 1), ("h_gated", 2), ("h_squared", 2 * CT),
                   ("e_turned_kept", 1), ("e_gated", 1),
                   ("e_act_kept", 1), ("l_hnT_kept", 1), ("l_xnT_kept", 1), ("l_mask_kept", 1), ("l_scaled_a", 1))

            def router_step(stage):
                f = stage(1)
                if f:
                    hold(act, S["r_normed"], f.done())
                    nc.scalar.copy(XN2[:, f.cols(D)], xn[:, f.par, :]).then_inc(S["r_kept"], 1)
                    hold(act, S["r_routed"], f.freed())
                    hold(act, S["r_xnT_done"], f.done())
                    nc.scalar.copy(xnT[:, f.par, :], PS[:, f.par, 0:P])
                    nc.scalar.copy(XNT[:, f.cols(P)], PS[:, f.par, 0:P]).then_inc(S["r_xnT_kept"], 1)

            walk(act, NT, 2, router_step)
            act.wait_ge(sort_step, 1)
            nc.scalar.activation(score[:], top[:], ACT.Sigmoid).then_inc(score_ready, 1)

            def shared_step(stage):
                c = stage(0)
                if c:
                    for i in range(2):
                        when(act, S["h_lifted"], c.done(2, i))
                        hold(act, S["h_acted"], c.freed(2, i, back=2))
                        nc.scalar.activation(sg[:, i, :], PS[:, 2 * i, :], ACT.Silu).then_inc(S["h_gated"], 1)
                    for q in range(CT):
                        for half, ss in ((CK, ssk[:, ds(c.t * CT + q, 1)]), (CV, ssv[:, 0, ds(c.t * CT + q, 1)])):
                            k = int(half is CV)
                            when(act, S["h_squared"], c.freed(2 * CT, 2 * q + k, back=2))
                            nc.scalar.activation(sqj[:, k, :], half[:, ds((c.t * CT + q) * D, D)], ACT.Square,
                                                 accum_out=ss).then_inc(S["h_squared"], 1)

            walk(act, NC, 1, shared_step, unroll=2)

            def sorted_step(stage):
                f, s, a = stage(1), stage(2), stage(3)
                if f:
                    hold(act, S["e_lifted"], f.freed())
                    when(act, S["e_turned"], f.done())
                    nc.scalar.copy(xsT[:, f.par, :], PS[:, f.par, 0:P]).then_inc(S["e_turned_kept"], 1)
                if s:
                    hold(act, S["e_acted"], s.freed())
                    when(act, S["e_lifted"], s.done())
                    nc.scalar.activation(sg[:, s.par, 0:FF], PS[:, 2 + s.par, 0:FF], ACT.Silu)\
                        .then_inc(S["e_gated"], 1)
                if a:
                    hold(act, S["e_down"], a.freed())
                    when(act, S["e_act_turned"], a.done())
                    nc.scalar.copy(act2T[:, a.par, :], PS[:, 4 + a.par, 0:FF]).then_inc(S["e_act_kept"], 1)

            walk(act, NS, 4, sorted_step)

            def last_step(stage):
                f, a, n = stage(1), stage(3), stage(5)
                if n:
                    hold(act, S["l_summed"], n.freed())
                    hold(act, S["l_mask_ready"], n.done())
                    when(act, S["l_lifted"], n.done())
                    for e in range(E // 2):
                        last = nc.scalar.activation(z[:, n.par, e * D:e * D + D], PS[:, 5, e * D:e * D + D], ACT.Copy,
                                                    scale=mask1[:, n.par, 1, e:e + 1])
                    last.then_inc(S["l_scaled_a"], 1)
                    hold(act, S["l_biased"], n.freed())
                    when(act, S["l_mask_turned"], n.done())
                    nc.scalar.copy(mask1T[:, n.par, :], PS[0:E, 4, P:2 * P]).then_inc(S["l_mask_kept"], 1)
                if f:
                    hold(act, S["l_mixed"], f.freed())
                    when(act, S["l_hnT_done"], f.done())
                    nc.scalar.copy(hnT[:, f.par, :], PS[:, 0, 0:P]).then_inc(S["l_hnT_kept"], 1)
                if a:
                    hold(act, S["l_lifted"], a.freed())
                    when(act, S["l_xnT_done"], a.done())
                    nc.scalar.copy(xnT[:, a.par, :], PS[:, 3, 0:P]).then_inc(S["l_xnT_kept"], 1)

            walk(act, NT, 5, last_step)

        @block.vector
        def _(dve):
            credit(dve, ("stats", 1), ("moments", 1), ("normed", 1), ("lo_ready", 2), ("ctx_stacked", 1),
                   ("q_spread", 1), ("k_kept", 1), ("ctx_kept", 1), ("maxed", 4), ("recip_ready", 1),
                   ("o_normed", 1), ("x_updated", 1))
            dve.wait_ge(consts_in, 32)
            dve.tensor_copy(ident16[:], identf).then_inc(weights_ready, 1)
            dve.wait_ge(weights_in, 48)
            dve.tensor_scalar(wqkv[:, 0:D], wqkv[:, 0:D], float(HD) ** -0.5, None, ALU.mult)
            dve.wait_ge(gates_ready, 1)
            dve.tensor_scalar(wproj[:], wproj[:], tgate[:, 0:1], None, ALU.mult).then_inc(weights_ready, 1)
            dve.tensor_scalar(bproj[:], bproj[:], tgate[:, 0:1], None, ALU.mult).then_inc(weights_ready, 1)
            dve.wait_ge(pool_consts, 2)

            def max_chunk(a, j):
                when(dve, S["scored"], a.done(4, j))
                dve.tensor_reduce(negm[:, a.par, :, j], PS[:, j % 2, :].rearrange("p (h k) -> p h k", h=HG),
                                  AX.X, ALU.max, negate=True).then_inc(S["maxed"], 1)

            def step(stage):
                l, f, s, a, n = (stage(i) for i in (0, 1, 2, 3, 6))
                if a:
                    max_chunk(a, 0)
                    max_chunk(a, 1)
                if l:
                    arrived(dve, x_in, l)
                    dve.bn_stats(st[:, l.par, :], X[:, l.cols(D)]).then_inc(S["stats"], 1)
                    hold(dve, S["stats"], l.done())
                    dve.bn_aggr(mv[:, l.par, :], st[:, l.par, :]).then_inc(S["moments"], 1)
                if s:
                    hold(dve, S["q_kept"], s.done())
                    for b in range(2):
                        src = bank16(5)[:, 512:1024].rearrange("p (g t) -> p g t", g=G)[:, :, 64 * b:64 * b + 64]
                        last = dve.tensor_copy(kt[:, s.slot, b, :, 64 * b:64 * b + 64], src)
                    last.then_inc(S["k_kept"], 1)
                if s:
                    when(dve, S["ctx_turned"], s.done())
                    for b in range(2):
                        src = bank16(6)[:, 0:512].rearrange("p (g t) -> p g t", g=G)[:, :, 64 * b:64 * b + 64]
                        last = dve.tensor_copy(kt[:, s.slot, b, :, 64 * (1 - b):128 - 64 * b], src)
                    last.then_inc(S["ctx_kept"], 1)
                if s:
                    for hg in range(HG):
                        rows = slice(32 * hg, 32 * hg + 32)
                        last = dve.tensor_copy(qbd[rows, s.slot, :, hg, :], qc[rows])
                    last.then_inc(S["q_spread"], 1)
                if a:
                    max_chunk(a, 2)
                if n:
                    when(dve, S["o_turned"], n.done())
                    o = PS[:, 5, :].rearrange("p (h w) -> p h w", h=H)
                    dve.reciprocal(rden[:, n.par, :], o[:, :, HD:HD + 1]).then_inc(S["recip_ready"], 1)
                    when(dve, S["recip_ready"], n.done())
                    dve.tensor_tensor(on[:, n.par, :].rearrange("p (h d) -> p h d", h=H), o[:, :, 0:HD],
                                      rden[:, n.par, :].unsqueeze(2).to_broadcast([P, H, HD]), ALU.mult)\
                        .then_inc(S["o_normed"], 1)
                if a:
                    max_chunk(a, 3)
                if f:
                    hold(dve, S["v_kept"], f.done())
                    for w, col in ((0, 16), (1, 8)):
                        dve.tensor_tensor(stack[:, f.par, w, :, col:col + 8],
                                          PS[:, 4, P * (1 + w):P * (2 + w)].rearrange("p (h d) -> p h d", h=H),
                                          stack[:, f.par, w, :, 0:8], ALU.subtract).then_inc(S["lo_ready"], 1)
                    when(dve, S["ctx_hi"], f.done())
                    dve.tensor_tensor(stack[:, f.par, 2, :, 8:16], CK[:, f.cols(D)].rearrange("p (h d) -> p h d", h=H),
                                      stack[:, f.par, 2, :, 0:8], ALU.subtract).then_inc(S["ctx_stacked"], 1)
                if l:
                    when(dve, S["xnT_done"], l.freed())
                    when(dve, S["rstd_ready"], l.done())
                    dve.tensor_scalar(xn[:, l.par, :], X[:, l.cols(D)], mv[:, l.par, 0:1],
                                      rstd[:, l.par:l.par + 1], ALU.subtract, ALU.mult).then_inc(S["normed"], 1)
                if n:
                    hold(dve, S["bias_added"], n.done())
                    when(dve, S["projected"], n.done())
                    dve.tensor_tensor(X[:, n.cols(D)], PS[:, 6, P:2 * P], X[:, n.cols(D)], ALU.add)\
                        .then_inc(S["x_updated"], 1)

            walk(dve, NT, LAGS, step, lambda: hold(dve, x_in[2], 16))

            credit(dve, ("r_stats", 1), ("r_moments", 1), ("r_normed", 1), ("r_logits", 1), ("h_acted", 2),
                   ("h_added", 1), ("e_acted", 1), ("e_kept", 1),
                   *((n, 1) for n in ("l_x2 l_stats l_moments l_normed l_hp_ready l_picked l_dp_ready l_x3 l_stats2 "
                                      "l_moments2 l_normed2 l_lg l_m8 l_i8 l_mk0 l_mask_ready l_scaled_v l_summed "
                                      "l_out_ready").split()))

            def moments(l, stats, done, into):
                dve.bn_stats(st[:, l.par, :], X[:, l.cols(D)]).then_inc(S[stats], 1)
                hold(dve, S[stats], l.done())
                dve.bn_aggr(into[:, l.par, :], st[:, l.par, :]).then_inc(S[done], 1)

            def router_step(stage):
                l, f, s = stage(0), stage(1), stage(2)
                if l:
                    if l.turn is None and l.n == 0:
                        hold(dve, S["x_updated"], Tile(NT - 1).done())
                    moments(l, "r_stats", "r_moments", mv)
                if f:
                    hold(dve, S["r_xnT_done"], f.freed())
                    hold(dve, S["r_kept"], f.freed())
                    when(dve, S["r_rstd_ready"], f.done())
                    dve.tensor_scalar(xn[:, f.par, :], X[:, f.cols(D)], mv[:, f.par, 0:1],
                                      rstd[:, f.par:f.par + 1], ALU.subtract, ALU.mult).then_inc(S["r_normed"], 1)
                if s:
                    hold(dve, S["r_routed"], s.done())
                    dve.tensor_copy(LG[:, ds(s.t, 1), :], PS[:, 2 + s.par, 0:E].unsqueeze(1))\
                        .then_inc(S["r_logits"], 1)

            walk(dve, NT, 2, router_step)

            chained = [0]

            def then(ins):
                chained[0] += 1
                ins.then_inc(sort_step, 1)
                dve.wait_ge(sort_step, chained[0])

            def over_tiles(a):
                return a.unsqueeze(2).to_broadcast([P, E, NT])

            hold(dve, S["r_logits"], Tile(NT - 1).done())
            then(dve.tensor_reduce(top[:], LG[:], AX.X, ALU.max))
            then(dve.tensor_tensor(isel[:], LG[:], top[:].unsqueeze(2).to_broadcast([P, NT, E]), ALU.is_equal))
            no8 = exp_no8.unsqueeze(1).to_broadcast([P, NT, E])
            then(dve.tensor_tensor(isel[:], isel[:], no8, ALU.mult))
            then(dve.tensor_reduce(first8[:], isel[:], AX.X, ALU.min))
            dve.tensor_copy(upper16[:], upper)
            dve.tensor_copy(ones16[:], ones)
            dve.memset(onesf[:], 1.0)
            then(dve.tensor_tensor(onehot[:].rearrange("p e t -> p t e"),
                                   first8[:].unsqueeze(2).to_broadcast([P, NT, E]), no8, ALU.is_equal))
            dve.wait_ge(ranked, 1)
            then(dve.tensor_copy(tot[:], PS[:, 5, 0:E * NT].rearrange("p (e t) -> p e t", e=E)))
            then(dve.tensor_tensor_scan(run[:].rearrange("p e t -> p (e t)"), onesf[:],
                                        tot[:].rearrange("p e t -> p (e t)"), 0.0, ALU.mult, ALU.add))
            then(dve.tensor_reduce(cnt[:, 0, :], tot[:], AX.X, ALU.add))
            then(dve.tensor_scalar(cnti[:, 0, :], cnt[:, 0, :], float(P - 1), None, ALU.add))
            then(dve.tensor_scalar(cnti[:, 1, :], cnti[:, 0, :], 7, 7, ALU.logical_shift_right, ALU.logical_shift_left))
            then(dve.tensor_copy(cnt[:, 1, :], cnti[:, 1, :]))
            then(dve.tensor_tensor_scan(cnt[:, 2, :], onesf[:, 0:E], cnt[:, 1, :], 0.0, ALU.mult, ALU.add))
            then(dve.tensor_tensor(cnt[:, 3, :], cnt[:, 2, :], cnt[:, 1, :], ALU.subtract))
            then(dve.tensor_tensor(cnt[:, 4, :], cnt[:, 0, :], run[:, :, NT - 1], ALU.subtract))
            then(dve.tensor_tensor(cnt[:, 5, :], cnt[:, 3, :], cnt[:, 4, :], ALU.add))
            then(dve.tensor_tensor(run[:], run[:], tot[:], ALU.subtract))
            then(dve.tensor_tensor(run[:], PS[:, 4, 0:E * NT].rearrange("p (e t) -> p e t", e=E), run[:], ALU.add))
            then(dve.tensor_tensor(run[:], run[:], over_tiles(cnt[:, 5, :]), ALU.add))
            then(dve.tensor_tensor(run[:], run[:], onehot[:], ALU.mult))
            then(dve.tensor_reduce(posf[:], run[:].rearrange("p e t -> p t e"), AX.X, ALU.add))
            then(dve.tensor_copy(posu[:], posf[:]))
            dve.wait_ge(score_ready, 1)
            for c in range(NT // 8):
                rows = XN2[:, c * 8 * D:(c + 1) * 8 * D].rearrange("p (t d) -> p t d", t=8)
                dve.tensor_tensor(rows, rows, score[:, c * 8:(c + 1) * 8].unsqueeze(2).to_broadcast([P, 8, D]),
                                  ALU.mult).then_inc(scaled, 1)
            then(dve.tensor_tensor(tcmp[:], tile_start.unsqueeze(2).to_broadcast([P, NS, E - 1]),
                                   cnt[:, 2, 0:E - 1].unsqueeze(1).to_broadcast([P, NS, E - 1]), ALU.is_ge))
            then(dve.tensor_reduce(texpf[:], tcmp[:], AX.X, ALU.add))
            dve.tensor_copy(texp[:], texpf[:]).then_inc(texp_ready, 1)

            def shared_step(stage):
                c, d = stage(0), stage(1)
                if c:
                    for i in range(2):
                        if i == 0:
                            hold(dve, S["h_down"], c.freed())
                        when(dve, S["h_gated"], c.done(2, i))
                        dve.tensor_tensor(hact[:, c.par, i, :], PS[:, 2 * i + 1, :], sg[:, i, :], ALU.mult)\
                            .then_inc(S["h_acted"], 1)
                if d:
                    when(dve, S["h_down"], d.done())
                    xc = X[:, ds(d.t * CT * D, CT * D)]
                    dve.tensor_tensor(xc, PS[:, 6 + d.par, :], xc, ALU.add).then_inc(S["h_added"], 1)

            walk(dve, NC, 1, shared_step, unroll=2)

            plugged = [0]

            def next_plug(ins):
                plugged[0] += 1
                ins.then_inc(plug_step, 1)
                dve.wait_ge(plug_step, plugged[0])

            def seq3(a, axis):
                return a.unsqueeze(axis).to_broadcast([SEQ, SEQ, SEQ])

            dve.wait_ge(more_in, 48)
            place = place_no[0:SEQ]
            next_plug(dve.tensor_copy(pm[:, 0, :], pm_i[:]))
            next_plug(dve.tensor_tensor_scan(pm[:, 1, :], onesf[0:SEQ, 0:SEQ], pm[:, 0, :], -1.0, ALU.mult, ALU.add))
            next_plug(dve.tensor_scalar(pm[:, 2, :], pm[:, 1, :], 0.0, float(SEQ), ALU.is_lt, ALU.mult))
            next_plug(dve.tensor_tensor(pm[:, 2, :], pm[:, 1, :], pm[:, 2, :], ALU.add))
            next_plug(dve.tensor_tensor(pcmp[:], seq3(place, 2), seq3(pm[:, 2, :], 1), ALU.is_equal))
            next_plug(dve.tensor_reduce(pm[:, 3, :], pcmp[:], AX.X, ALU.max))
            next_plug(dve.tensor_tensor_scan(pm[:, 4, :], onesf[0:SEQ, 0:SEQ], pm[:, 3, :], -1.0, ALU.mult, ALU.add))
            next_plug(dve.tensor_scalar(pm[:, 5, :], pm[:, 4, :], 0.0, float(SEQ - 1), ALU.max, ALU.min))
            assert plugged[0] == PLUG_STEPS
            dve.wait_ge(swap_in, 32)
            dve.tensor_tensor(crms[:], ssk[:], ssv[:, 1, :], ALU.add).then_inc(crms_step, 1)
            dve.wait_ge(crms_step, 1)
            dve.tensor_scalar(crms[:], crms[:], 0.5 / D, EPS, ALU.mult, ALU.add).then_inc(crms_step, 1)
            hold(dve, late_in, 16 * 11)
            dve.tensor_scalar(b1[:], b1[:], tgate[0:E, 3:4], None, ALU.mult).then_inc(bias_ready, 1)

            def sorted_step(stage):
                s, b = stage(2), stage(4)
                if s:
                    hold(dve, S["e_act_turned"], s.freed())
                    when(dve, S["e_gated"], s.done())
                    dve.tensor_tensor(hact[:, s.par, 0, 0:FF], PS[:, 2 + s.par, FF:2 * FF], sg[:, s.par, 0:FF],
                                      ALU.mult).then_inc(S["e_acted"], 1)
                if b:
                    hold(dve, S["e_down"], b.done())
                    dve.tensor_copy(YS[:, b.cols(D)], PS[:, 6 + b.par, 0:D]).then_inc(S["e_kept"], 1)

            walk(dve, NS, 4, sorted_step)

            def last_step(stage):
                l, f, s, a, b, n = (stage(i) for i in range(6))
                if n:
                    hold(dve, S["l_summed"], n.freed(back=1))
                    when(dve, S["l_lifted"], n.done())
                    dve.tensor_tensor(z[:, n.par, 4 * D:].rearrange("p (e d) -> p e d", d=D),
                                      PS[:, 6, :].rearrange("p (e d) -> p e d", d=D),
                                      mask1[:, n.par, 1, 4:8].unsqueeze(2).to_broadcast([P, 4, D]), ALU.mult)\
                        .then_inc(S["l_scaled_v"], 1)
                if b:
                    when(dve, S["l_routed"], b.done())
                    dve.tensor_tensor(lg1[:, b.par, :], PS[:, 4, 0:E], rb1[:], ALU.add).then_inc(S["l_lg"], 1)
                    hold(dve, S["l_lg"], b.done())
                    dve.max(mx8[:, b.par, :], lg1[:, b.par, :]).then_inc(S["l_m8"], 1)
                    hold(dve, S["l_m8"], b.done())
                    dve.max_index(ix8[:, b.par, :], mx8[:, b.par, :], lg1[:, b.par, :]).then_inc(S["l_i8"], 1)
                    hold(dve, S["l_mask_turned"], b.freed())
                    hold(dve, S["l_scaled_a"], b.freed())
                    when(dve, S["l_i8"], b.done())
                    dve.tensor_copy(ixf[:, b.par, :], ix8[:, b.par, 0:2]).then_inc(S["l_ixf"], 1)
                    when(dve, S["l_ixf"], b.done())
                    dve.tensor_scalar(mask1[:, b.par, 0, :], exp_no, ixf[:, b.par, 0:1], None, ALU.is_equal)\
                        .then_inc(S["l_mk0"], 1)
                    when(dve, S["l_mk0"], b.done())
                    dve.scalar_tensor_tensor(out=mask1[:, b.par, 1, :], in0=exp_no, scalar=ixf[:, b.par, 1:2],
                                             in1=mask1[:, b.par, 0, :], op0=ALU.is_equal, op1=ALU.add)\
                        .then_inc(S["l_mask_ready"], 1)
                if l:
                    when(dve, S["l_y_in"], l.done())
                    dve.tensor_tensor(X[:, l.cols(D)], X[:, l.cols(D)], XN2[:, l.cols(D)], ALU.add)\
                        .then_inc(S["l_x2"], 1)
                    hold(dve, S["l_x2"], l.done())
                    moments(l, "l_stats", "l_moments", mvl)
                if f:
                    hold(dve, S["l_hnT_done"], f.freed())
                    when(dve, S["l_rr"], f.done())
                    dve.tensor_scalar(hn[:, f.par, :], X[:, f.cols(D)], mvl[:, f.par, 0:1], rr[:, f.par:f.par + 1],
                                      ALU.subtract, ALU.mult).then_inc(S["l_normed"], 1)
                    if f.turn is None and f.n == 0:
                        hold(dve, crms_step, 3)
                        hold(dve, plug_in, 32)
                        hold(dve, late_ready, 6)
                    hold(dve, S["l_depooled"], f.freed())
                    dve.scalar_tensor_tensor(out=hp[:, f.par, :], in0=CK[:, f.cols(D)], scalar=crms[:, ds(f.t, 1)],
                                             in1=ginit[:], op0=ALU.mult, op1=ALU.mult).then_inc(S["l_hp_ready"], 1)
                    when(dve, S["l_mixed"], f.freed())
                    dve.tensor_scalar(pick[:, f.par, :], XNT[:, f.cols(P)], patch_no, None, ALU.is_equal)\
                        .then_inc(S["l_picked"], 1)
                if s:
                    when(dve, S["l_mixed"], s.done())
                    dve.tensor_tensor(X[:, s.cols(D)], PS[:, 2, 0:D], X[:, s.cols(D)], ALU.add).then_inc(S["l_x3"], 1)
                    hold(dve, S["l_x3"], s.done())
                    moments(s, "l_stats2", "l_moments2", mv2)
                if f:
                    when(dve, S["l_depooled"], f.done())
                    dve.tensor_tensor(dp[:, f.par, :], PS[:, 1, 0:D], binB[:], ALU.add).then_inc(S["l_dp_ready"], 1)
                if a:
                    hold(dve, S["l_xnT_done"], a.freed())
                    when(dve, S["l_rstd2"], a.done())
                    dve.tensor_scalar(xn[:, a.par, :], X[:, a.cols(D)], mv2[:, a.par, 0:1], rstd[:, a.par:a.par + 1],
                                      ALU.subtract, ALU.mult).then_inc(S["l_normed2"], 1)
                if n:
                    hold(dve, S["l_scaled_v"], n.done())
                    when(dve, S["l_scaled_a"], n.done())
                    dve.tensor_reduce(zs[:, n.par, :], z[:, n.par, :].rearrange("p (e d) -> p d e", d=D), AX.X, ALU.add)\
                        .then_inc(S["l_summed"], 1)
                    hold(dve, S["l_summed"], n.done())
                    when(dve, S["l_biased"], n.done())
                    dve.tensor_tensor(zs[:, n.par, :], PS[:, 7, 0:D], zs[:, n.par, :], ALU.add).then_inc(S["l_zb"], 1)
                    when(dve, S["l_zb"], n.done())
                    dve.tensor_tensor(X[:, n.cols(D)], X[:, n.cols(D)], zs[:, n.par, :], ALU.add)\
                        .then_inc(S["l_out_ready"], 1)

            credit(dve, ("l_zb", 1), ("l_ixf", 1))
            walk(dve, NT, 5, last_step)

        @block.tensor
        def _(pe):
            credit(pe, ("xnT_done", 1), ("qkv_done", 1), ("qk_turned", 1), ("ctx_turned", 1), ("scored", 4),
                   ("max_turned", 1), ("scored_t", 4), ("averaged", 4), ("o_turned", 1), ("on_turned", 1),
                   ("projected", 1))
            pe.wait_ge(weights_ready, 3)
            pe.wait_ge(pool_consts, 2)

            def scores_for_max(a, j):
                if j == 0:
                    hold(pe, S["q_spread"], a.done())
                    hold(pe, S["k_kept"], a.done())
                    hold(pe, S["ctx_kept"], a.done())
                hold(pe, S["maxed"], a.freed(4, j, back=2))
                for hg in range(HG):
                    for b in range(2):
                        last = nc.tensor.matmul(PS[64 * b:64 * b + 64, j % 2, hg * P:hg * P + P],
                                                qbd[:, a.slot, j, hg, 64 * b:64 * b + 64], kt[:, a.slot, b, j, :],
                                                start=True, stop=True)
                last.then_inc(S["scored"], 1)

            def scores_by_key(b, j):
                if j == 0:
                    hold(pe, shift_placed[b.par], 64 * (b.pair + 1))
                hold(pe, S["exped"], b.freed(4, j, back=2))
                seq = j // 2
                for g2 in range(2):
                    g = 2 * (j % 2) + g2
                    last = nc.tensor.matmul(PS[:, 2 + j % 2, 256 * g2:256 * g2 + 256], kt[:, b.slot, seq, g, :],
                                            qbd[:, b.slot, g, :, SEQ * seq:SEQ * seq + SEQ], start=True, stop=True)
                last.then_inc(S["scored_t"], 1)

            def average(b, j):
                if j == 0:
                    hold(pe, S["v_spread"], b.done())
                    hold(pe, S["o_kept"], b.freed(back=1))
                hold(pe, S["exped"], b.done(4, j))
                seq = j // 2
                for g2 in range(2):
                    g = 2 * (j % 2) + g2
                    for hg in range(HG):
                        last = nc.tensor.matmul(PS[32 * hg:32 * hg + 32, 7, g * P + SEQ * seq:g * P + SEQ * seq + SEQ],
                                                vp[:, b.par, seq, g * HG + hg, :],
                                                pexp[:, j, (g2 * HG + hg) * SEQ:(g2 * HG + hg + 1) * SEQ],
                                                start=True, stop=True)
                last.then_inc(S["averaged"], 1)

            def turn_stack(s, w, bank, col, done):
                for g in range(G):
                    last = nc.tensor.transpose(
                        bank16(bank)[:, col + g * P:col + (g + 1) * P],
                        stack[:, s.par, w, g * HG:g * HG + HG, :].rearrange("p h c -> p (h c)"), ident16[:])
                if done:
                    last.then_inc(S[done], 1)

            def step(stage):
                f, s, a, c, b, n = (stage(i) for i in range(1, 7))
                m = stage(7)
                if a:
                    if c:
                        hold(pe, S["max_kept"], c.done())
                    scores_for_max(a, 0)
                    scores_for_max(a, 1)
                if s:
                    hold(pe, S["hi_ready"], s.done())
                    hold(pe, S["lo_ready"], s.done(2, 1))
                    if m:
                        hold(pe, S["o_normed"], m.done())
                    turn_stack(s, 0, 5, 0, None)
                    turn_stack(s, 1, 5, 512, "qk_turned")
                if b:
                    scores_by_key(b, 0)
                    scores_by_key(b, 1)
                if s:
                    hold(pe, S["ctx_stacked"], s.done())
                    if m:
                        hold(pe, S["x_updated"], m.done())
                    turn_stack(s, 2, 6, 0, "ctx_turned")
                if f:
                    if s:
                        hold(pe, S["v_kept"], s.done())
                        hold(pe, S["lo_ready"], s.done(2, 1))
                    when(pe, S["normed"], f.done())
                    nc.tensor.transpose(PS[:, 4, 0:P], xn[:, f.par, :], identf).then_inc(S["xnT_done"], 1)
                if b:
                    average(b, 0)
                    scores_by_key(b, 2)
                if a:
                    scores_for_max(a, 2)
                if f:
                    hold(pe, S["xnT_kept"], f.done())
                    nc.tensor.matmul(PS[:, 4, P:4 * P], xnT[:, f.par, :], wqkv[:], start=True, stop=True)\
                        .then_inc(S["qkv_done"], 1)
                if b:
                    average(b, 1)
                    scores_by_key(b, 3)
                if a:
                    scores_for_max(a, 3)
                if n:
                    hold(pe, S["o_kept"], n.done())
                    if s:
                        hold(pe, S["k_kept"], s.done())
                    for g in range(G):
                        last = nc.tensor.transpose(PS[:, 5, g * P:g * P + P], oS[:, n.par, g * P:g * P + P], identf)
                    last.then_inc(S["o_turned"], 1)
                if b:
                    average(b, 2)
                if n:
                    if s:
                        hold(pe, S["ctx_kept"], s.done())
                    when(pe, S["o_normed"], n.done())
                    nc.tensor.transpose(PS[:, 6, 0:P], on[:, n.par, :], identf).then_inc(S["on_turned"], 1)
                if b:
                    average(b, 3)
                if a:
                    hold(pe, S["maxed"], a.done(4, 3))
                    nc.tensor.transpose(bank16(0)[0:H, 0:P], negm[:, a.par, :, :].rearrange("p h g -> p (h g)"),
                                        ident16[:]).then_inc(S["max_turned"], 1)
                if n:
                    hold(pe, S["on_kept"], n.done())
                    nc.tensor.matmul(PS[:, 6, P:2 * P], onT[:, n.par, :], wproj[:], start=True, stop=True)\
                        .then_inc(S["projected"], 1)

            walk(pe, NT, LAGS, step)

            credit(pe, *((n, 1) for n in ("r_xnT_done r_routed h_down e_turned e_act_turned e_lifted e_down "
                                          "l_hnT_done l_depooled l_mixed l_xnT_done l_routed l_mask_turned l_lifted "
                                          "l_biased").split()), ("h_lifted", 2))
            hold(pe, S["x_updated"], Tile(NT - 1).done())
            hold(pe, more_in, 48)

            def router_step(stage):
                f, s = stage(1), stage(2)
                if f:
                    hold(pe, S["r_xnT_kept"], f.freed())
                    when(pe, S["r_normed"], f.done())
                    nc.tensor.transpose(PS[:, f.par, 0:P], xn[:, f.par, :], identf).then_inc(S["r_xnT_done"], 1)
                if s:
                    hold(pe, S["r_logits"], s.freed())
                    when(pe, S["r_xnT_kept"], s.done())
                    nc.tensor.matmul(PS[:, 2 + s.par, 0:64], xnT[:, s.par, :], gatew[:], start=True, stop=True)\
                        .then_inc(S["r_routed"], 1)

            walk(pe, NT, 2, router_step)
            pe.wait_ge(sort_step, 5)
            oh = onehot[:].rearrange("p e t -> p (e t)")
            nc.tensor.matmul(PS[:, 4, 0:E * NT], upper16[:], oh, start=True, stop=True)
            nc.tensor.matmul(PS[:, 5, 0:E * NT], ones16[:], oh, start=True, stop=True).then_inc(ranked, 1)

            def shared_step(stage):
                c, d = stage(0), stage(1)
                if c:
                    if c.turn is None and c.n == 0:
                        hold(pe, S["r_xnT_kept"], Tile(NT - 1).done())
                        hold(pe, S["r_logits"], Tile(NT - 1).done())
                    for i in range(2):
                        hold(pe, S["h_acted"], c.freed(2, i, back=2))
                        rows = XNT[:, ds(c.t * CT * P, CT * P)]
                        nc.tensor.matmul(PS[:, 2 * i, :], shgu[:, i * P:i * P + P], rows, start=True, stop=True)
                        nc.tensor.matmul(PS[:, 2 * i + 1, :], shgu[:, FF + i * P:FF + i * P + P], rows,
                                         start=True, stop=True).then_inc(S["h_lifted"], 1)
                if d:
                    if d.turn is None and d.n == 0:
                        hold(pe, late_ready, 6)
                    hold(pe, S["h_acted"], d.done(2, 1))
                    hold(pe, S["h_added"], d.freed())
                    for q in range(CT):
                        for i in range(2):
                            last = nc.tensor.matmul(PS[:, 6 + d.par, q * P:q * P + P],
                                                    hact[:, d.par, i, q * P:q * P + P], shd[:, i * D:i * D + D],
                                                    start=(i == 0), stop=(i == 1))
                    last.then_inc(S["h_down"], 1)

            walk(pe, NC, 1, shared_step, unroll=2)

            pe.wait_ge(texp_ready, 1)
            hold(pe, S["h_added"], Tile(NC - 1).done())

            def sorted_step(stage):
                f, s, a, b = (stage(i) for i in range(1, 5))
                if f:
                    hold(pe, S["e_turned_kept"], f.freed())
                    when(pe, S["e_copied"], f.done())
                    nc.tensor.transpose(PS[:, f.par, 0:P], xs[:, f.par, :], identf).then_inc(S["e_turned"], 1)
                if s:
                    hold(pe, S["e_acted"], s.freed())
                    hold(pe, S["e_turned_kept"], s.done())
                    e = pe.value_load(texp[0:1, ds(s.t, 1)], min_val=0, max_val=E - 1)
                    nc.tensor.matmul(PS[:, 2 + s.par, :], xsT[:, s.par, :], rgu[:, ds(e * (2 * FF), 2 * FF)],
                                     start=True, stop=True).then_inc(S["e_lifted"], 1)
                if a:
                    hold(pe, S["e_act_kept"], a.freed())
                    hold(pe, S["e_acted"], a.done())
                    for i in range(2):
                        last = nc.tensor.transpose(PS[:, 4 + a.par, i * P:i * P + P],
                                                   hact[:, a.par, 0, i * P:i * P + P], identf)
                    last.then_inc(S["e_act_turned"], 1)
                if b:
                    hold(pe, S["e_kept"], b.freed())
                    hold(pe, S["e_act_kept"], b.done())
                    e = pe.value_load(texp[0:1, ds(b.t, 1)], min_val=0, max_val=E - 1)
                    for i in range(2):
                        last = nc.tensor.matmul(PS[:, 6 + b.par, 0:D], act2T[:, b.par, i * P:i * P + P],
                                                rdn[:, ds(e * FF + i * D, D)], start=(i == 0), stop=(i == 1))
                    last.then_inc(S["e_down"], 1)

            walk(pe, NS, 4, sorted_step)
            hold(pe, S["e_kept"], Tile(NS - 1).done())
            hold(pe, bias_ready, 1)

            def last_step(stage):
                f, s, a, b, n = (stage(i) for i in range(1, 6))
                if n:
                    hold(pe, S["l_mask_ready"], n.done())
                    nc.tensor.transpose(PS[0:E, 4, P:2 * P], mask1[:, n.par, 1, :], identf)\
                        .then_inc(S["l_mask_turned"], 1)
                if b:
                    if n:
                        hold(pe, S["l_mask_kept"], n.done())
                    hold(pe, S["l_lg"], b.freed(back=1))
                    hold(pe, S["l_xnT_kept"], b.done())
                    nc.tensor.matmul(PS[:, 4, 0:64], xnT[:, b.par, :], rw1[:], start=True, stop=True)\
                        .then_inc(S["l_routed"], 1)
                    hold(pe, S["l_scaled_a"], b.freed(back=1))
                    hold(pe, S["l_scaled_v"], b.freed(back=1))
                    nc.tensor.matmul(PS[:, 5, :], xnT[:, b.par, :], w1[:, 0:4 * D], start=True, stop=True)
                    nc.tensor.matmul(PS[:, 6, :], xnT[:, b.par, :], w1[:, 4 * D:], start=True, stop=True)\
                        .then_inc(S["l_lifted"], 1)
                if f:
                    hold(pe, S["l_hnT_kept"], f.freed(back=1))
                    when(pe, S["l_normed"], f.done())
                    nc.tensor.transpose(PS[:, 0, 0:P], hn[:, f.par, :], identf).then_inc(S["l_hnT_done"], 1)
                    hold(pe, S["l_dp_ready"], f.freed(back=1))
                    hold(pe, S["l_hp_ready"], f.done())
                    nc.tensor.matmul(PS[:, 1, 0:D], decay, hp[:, f.par, :], start=True, stop=True)\
                        .then_inc(S["l_depooled"], 1)
                if s:
                    hold(pe, S["l_x3"], s.freed(back=1))
                    hold(pe, S["l_hnT_kept"], s.done())
                    hold(pe, S["l_dp_ready"], s.done())
                    hold(pe, S["l_picked"], s.done())
                    nc.tensor.matmul(PS[:, 2, 0:D], hnT[:, s.par, :], winT[:], start=True, stop=False)
                    nc.tensor.matmul(PS[:, 2, 0:D], pick[:, s.par, :], dp[:, s.par, :], start=False, stop=True)\
                        .then_inc(S["l_mixed"], 1)
                if a:
                    hold(pe, S["l_xnT_kept"], a.freed(back=1))
                    when(pe, S["l_normed2"], a.done())
                    nc.tensor.transpose(PS[:, 3, 0:P], xn[:, a.par, :], identf).then_inc(S["l_xnT_done"], 1)
                if n:
                    hold(pe, S["l_zb"], n.freed(back=1))
                    hold(pe, S["l_mask_kept"], n.done())
                    nc.tensor.matmul(PS[:, 7, 0:D], mask1T[:, n.par, :], b1[:], start=True, stop=True)\
                        .then_inc(S["l_biased"], 1)

            walk(pe, NT, 5, last_step)


def constants(ns):
    p = np.arange(P)
    same = p[:, None] // 64 == p[None, :] // 64
    ago = p[None, :] - p[:, None]
    keep = np.exp(np.float64(-1e-3))
    fade = -np.expm1(np.float64(-1e-3))
    decay = np.where(same & (ago >= 0), keep * fade ** np.maximum(ago, 0), 0.0)
    rows = (np.arange(8), np.arange(8) - 8, np.arange(ns) * P)
    return np.concatenate([np.eye(P), p[:, None] < p[None, :], np.ones((P, P)), decay]
                          + [np.broadcast_to(r, (P, r.size)) for r in rows]
                          + [p[:, None] % 64, np.broadcast_to(np.arange(64), (P, 64))], 1).astype(np.float32)


def kernel(**inputs):
    import numpy as _np
    import concourse.bacc as _bacc
    from concourse import mybir as _mybir
    from concourse.bass_utils import run_bass_kernel_spmd as _run

    i = {k: _np.asarray(v) for k, v in inputs.items()}
    nt, ns = 32, 40

    def pad64(a):
        return _np.pad(a, ((0, 0), (0, 64 - a.shape[1])))

    def by_tile(a):
        return a.reshape(nt, 128, -1).transpose(1, 0, 2).reshape(128, -1)

    ctx = i["ctx_2048"].reshape(nt, 2, 64, 256)
    arrays = {
        "x": by_tile(i["x"]),
        "ctx_k": by_tile(ctx[..., :128]),
        "ctx_v_swapped": by_tile(ctx[:, ::-1, :, 128:]),
        "consts": constants(ns),
        "gates": _np.broadcast_to(_np.concatenate([i["g_xattn"], i["g_ffn"]]), (128, 4)),
        "w_qkv": i["L0_xattn_w_qkv"].T,
        "w_proj": i["L0_xattn_w_proj"].T,
        "b_proj": _np.broadcast_to(i["L0_xattn_b_proj"], (128, 128)),
        "gate_w": pad64(i["L0_ffn_gate_w"]),
        "sh_gate_up": _np.concatenate([i["L0_ffn_sh_gate"], i["L0_ffn_sh_up"]], 1),
        "sh_down": i["L0_ffn_sh_down"].reshape(2, 128, 128).transpose(1, 0, 2).reshape(128, 256),
        "rt_gate_up": _np.concatenate([i["L0_ffn_rt_gate"], i["L0_ffn_rt_up"]], 2).transpose(1, 0, 2).reshape(128, -1),
        "rt_down": i["L0_ffn_rt_down"].reshape(8, 2, 128, 128).transpose(2, 0, 1, 3).reshape(128, -1),
        "patch_mask": i["mask_BxS2_if0"],
        "w_in": i["L1_xattn_W_in"].T,
        "b_in": _np.broadcast_to(i["L1_xattn_b_in"], (128, 128)),
        "g_res": i["L1_xattn_g_res"].reshape(128, 1),
        "g_init": _np.broadcast_to(i["L1_xattn_g_init"][:128], (128, 128)),
        "router_w": pad64(i["L1_ffn_router_w"].T),
        "router_b": _np.broadcast_to(i["L1_ffn_router_b"], (128, 8)),
        "expert_w": i["L1_ffn_expert_w"].transpose(2, 0, 1).reshape(128, -1),
        "expert_b": i["L1_ffn_expert_b"],
    }
    arrays = {f"in_{k}_dram": _np.ascontiguousarray(v) for k, v in arrays.items()}
    nc = _bacc.Bacc("TRN2", target_bir_lowering=False, num_devices=1)
    args = [nc.dram_tensor(k, v.shape, _mybir.dt.from_np(v.dtype), kind="ExternalInput").ap() for k, v in arrays.items()]
    args.append(nc.dram_tensor("out_dram", (128, nt * 128), _mybir.dt.float32, kind="ExternalOutput").ap())
    flamingo_gated_two_layers(nc, *args)
    r = _run(nc, [arrays], core_ids=[0])
    return r.results[0]["out_dram"].reshape(128, nt, 128).transpose(1, 0, 2).reshape(64, 64, 128)
```

```python
from contextlib import ExitStack

import numpy as np

import concourse.bass as bass
from concourse import mybir

F32 = mybir.dt.float32
F16 = mybir.dt.float16
BF16 = mybir.dt.bfloat16
I32 = mybir.dt.int32
U32 = mybir.dt.uint32
ALU = mybir.AluOpType
ACT = mybir.ActivationFunctionType
AX = mybir.AxisListType
ds = bass.ds

P = 128
CREDIT = 2
TURN = 4
EPS = 1e-5


class Tile:

    def __init__(self, n, turn=None, unroll=TURN):
        self.n, self.turn = n, turn
        self.t = n if turn is None else n + unroll * turn
        self.pair = n // 2 if turn is None else n // 2 + unroll // 2 * turn
        self.quad = n // 4 if turn is None else n // 4 + turn
        self.par, self.slot = n % 2, n % 4

    def cols(self, width):
        return ds(self.t * width, width)

    def done(self, per_tile=1, event=0):
        return (self.t + CREDIT) * per_tile + event + 1

    def freed(self, per_tile=1, event=0, back=None):
        back = CREDIT * per_tile if back is None else back
        return (self.t + CREDIT) * per_tile + event + 1 - back


def walk(eng, tiles, depth, step, before_loop=None, unroll=TURN):
    first = -(-depth // unroll) * unroll
    assert tiles % unroll == 0 and tiles > first

    def peeled(s):
        step(lambda lag: Tile(s - lag) if 0 <= s - lag < tiles else None)

    for s in range(first):
        peeled(s)
    if before_loop:
        before_loop()
    with eng.Fori(0, (tiles - first) // unroll) as turn:
        for k in range(unroll):
            step(lambda lag: Tile(first + k - lag, turn, unroll))
    for s in range(tiles, tiles + depth):
        peeled(s)


def flamingo_gated_two_layers(nc, x, ctx_k, ctx_v_swapped, consts, gates, w_qkv, w_proj, b_proj, gate_w,
                              sh_gate_up, sh_down, rt_gate_up, rt_down, patch_mask, w_in, b_in, g_res, g_init,
                              router_w, router_b, expert_w, expert_b, out):
    NT = x.shape[1] // P
    D = P
    H, HD = 16, 8
    HG, G = 4, 4
    SEQ = 64
    E = 8
    FF = 256
    PAIRS = P // SEQ
    NS = (NT * P + E * (P - 1)) // P
    NS += -NS % TURN
    CT = 4
    NC = NT // CT
    LAGS = 6

    with ExitStack() as ctx:
        def sb(name, shape, dt=F32):
            return ctx.enter_context(nc.sbuf_tensor(name, shape, dt))

        def sem(name):
            return ctx.enter_context(nc.semaphore(name))

        X = sb("X", [P, NT * D])
        CK = sb("CK", [P, NT * D])
        CV = sb("CV", [P, NT * D])
        VALL = sb("VALL", [P, NT * D])
        CW = [P, P, P, P, E, E, NS, 1, SEQ]
        CO = [sum(CW[:i]) for i in range(len(CW))]
        cst = sb("cst", [P, sum(CW)])
        identf, upper, ones, decay, exp_no, exp_no8, tile_start, patch_no, place_no = (
            cst[:, o:o + w] for o, w in zip(CO, CW))
        ident16 = sb("ident16", [P, P], F16)
        halfneg = sb("halfneg", [P, 1])
        epsc = sb("epsc", [P, 1])
        gate = sb("gate", [P, 4])
        tgate = sb("tgate", [P, 4])
        wqkv = sb("wqkv", [P, 3 * D])
        wproj = sb("wproj", [P, D])
        bproj = sb("bproj", [P, D])
        st = sb("st", [P, 2, 6])
        mv = sb("mv", [P, 2, 2])
        ve = sb("ve", [P, 2])
        rstd = sb("rstd", [P, 2])
        xn = sb("xn", [P, 2, D])
        xnT = sb("xnT", [P, 2, P])
        stack = sb("stack", [P, 2, 3, H, 32], F16)
        qc = sb("qc", [P, G, P], F16)
        kt = sb("kt", [P, 4, 2, G, P], F16)
        vp = sb("vp", [P, 2, 2, H, 32])
        arena = sb("arena", [P, NS * D])
        negm = sb("negm", [P, 2, HG, G], F16)
        mT = sb("mT", [H, 2, P], F16)
        qbd = arena[:, 0:4 * G * HG * P // 2].bitcast(F16).rearrange("p (s g h t) -> p s g h t", s=4, g=G, h=HG)
        pexp = sb("pexp", [P, 4, 512])
        oS = sb("oS", [P, 2, 512])
        rden = sb("rden", [P, 2, H])
        on = sb("on", [P, 2, D])
        onT = sb("onT", [P, 2, P])

        spare = stack.rearrange("p s w h c -> p (s w h c)").bitcast(F32)
        def twin(k):
            return spare[:, k * 2 * D:(k + 1) * 2 * D].rearrange("p (s d) -> p s d", s=2)

        XN2 = VALL
        XNT = sb("XNT", [P, NT * P])
        gatew = sb("gatew", [P, 64])
        LG = onT.rearrange("p s d -> p (s d)").rearrange("p (t e) -> p t e", e=E)
        top = sb("top", [P, NT])
        score = sb("score", [P, NT])
        isel = spare[:, 800:800 + NT * E].rearrange("p (t e) -> p t e", e=E)
        first8 = sb("first8", [P, NT])
        onehot = sb("onehot", [P, E, NT], BF16)
        upper16 = sb("upper16", [P, P], BF16)
        ones16 = sb("ones16", [P, P], BF16)
        tot = spare[:, 1056:1056 + NT * E].rearrange("p (e t) -> p e t", e=E)
        run = on.rearrange("p s d -> p (s d)").rearrange("p (e t) -> p e t", e=E)
        onesf = sb("onesf", [P, E * NT])
        cnt = sb("cnt", [P, 6, E])
        cnti = sb("cnti", [P, 2, E], I32)
        posf = sb("posf", [P, NT])
        posu = sb("posu", [P, NT], U32)
        tcmp = spare[:, 512:512 + NS * (E - 1)].rearrange("p (s e) -> p s e", e=E - 1)
        texpf = sb("texpf", [P, NS])
        texp = sb("texp", [P, NS // 4], I32)
        shgu = sb("shgu", [P, 2 * FF])
        shd = sb("shd", [P, FF])
        rgu = sb("rgu", [P, E * 2 * FF])
        rdn = sb("rdn", [P, E * FF])
        sg = oS
        hact = pexp.rearrange("p (c i) t -> p c i t", c=2)
        zeros = sb("zeros", [P, 8 * D])
        xs = sb("xs", [P, 4, D])
        xsT = sb("xsT", [P, 2, P])
        act2T = spare[:, 0:2 * FF].rearrange("p (s f) -> p s f", s=2)
        YS = arena
        ssk = sb("ssk", [P, NT])
        ssv = sb("ssv", [P, 2, NT])
        sqj = sb("sqj", [P, 2, D], BF16)
        crms = sb("crms", [P, NT])
        pm_i = sb("pm_i", [SEQ, SEQ], I32)
        pm = sb("pm", [SEQ, 6, SEQ])
        pcmp = kt[0:SEQ].rearrange("p s b g t -> p (s b g t)").bitcast(BF16).rearrange("p (a b) -> p a b", a=SEQ)
        winT = sb("winT", [P, D])
        binB = sb("binB", [P, D])
        gres = sb("gres", [P, 1])
        ginit = sb("ginit", [P, D])
        rw1 = sb("rw1", [P, 64])
        rb1 = sb("rb1", [P, E])
        w1 = sb("w1", [P, E * D])
        b1 = sb("b1", [E, D])
        mvr = sb("mvr", [P, NT])
        ve2 = sb("ve2", [P, 2])
        str_ = sb("str_", [P, 2, 6])
        rstdr = sb("rstdr", [P, NT])
        mvl = sb("mvl", [P, NT, 2])
        mv2 = sb("mv2", [P, 2, 2])
        rchain = sb("rchain", [P, 2, NT])
        rr = sb("rr", [P, NT])
        mrr = sb("mrr", [P, NT])
        xnT4 = sb("xnT4", [P, 4, P])
        hn, hnT = on, onT
        hp, dp, pick = twin(2), twin(3), twin(4)
        DP = CV
        lg1 = sb("lg1", [P, 2, E])
        mx8 = sb("mx8", [P, 2, 8])
        ix8 = sb("ix8", [P, 2, 8], U32)
        ixf = sb("ixf", [P, 2, 2])
        mask1 = sb("mask1", [P, 2, 2, E], F16)
        mask1T = sb("mask1T", [E, 2, P])
        z = vp.rearrange("p s b h c -> p s (b h c)").rearrange("p s (e t) -> p s e t", e=E)

        sorted_x = nc.dram_tensor("sorted_x", (NS * P, D), F32).ap()
        sorted_y = nc.dram_tensor("sorted_y", (NS * P, D), F32).ap()
        plugs = nc.dram_tensor("plugs", (NT * PAIRS, SEQ), F32).ap()

        PS = ctx.enter_context(nc.psum_tensor("PS", [P, 8, 512], F32))

        def hi_twice(par, w):
            at = stack[:, par, w, :, 0:16 if w == 0 else 32].rearrange("p h (c d) -> p h c d", c=2)
            return at[:, :, :, 0:8]

        def twice_over(src):
            return src.unsqueeze(2).to_broadcast([P, H, 2, HD])

        def bank16(b):
            return PS[:, b, :].bitcast(F16)

        TILE_CHUNKS = [(0, 2), (2, 8), (8, NT)]
        x_in = [sem(f"x_in{c}") for c in range(3)]
        ck_in = [sem(f"ck_in{c}") for c in range(3)]
        cv_in = [sem(f"cv_in{c}") for c in range(3)]
        consts_in = sem("consts_in")
        weights_in = sem("weights_in")
        weights_ready = sem("weights_ready")
        pool_consts = sem("pool_consts")
        gates_ready = sem("gates_ready")
        names = ("stats moments normed var_eps rstd_ready bias_added hi_ready v_kept lo_ready "
                 "ctx_hi v_half ctx_stacked xnT_done qkv_done xnT_kept qk_turned ctx_turned q_kept q_spread "
                 "k_kept ctx_kept scored maxed max_turned max_kept scored_t exped v_spread averaged "
                 "o_kept o_turned recip_ready o_normed on_turned on_kept projected x_updated")
        S = {n: sem("a_" + n) for n in names.split()}
        shift_placed = [sem("a_shift_placed0"), sem("a_shift_placed1")]
        for n in "stats moments var_eps copied normed kept xnT_done xnT_kept routed logits".split():
            S["r_" + n] = sem("r_" + n)
        more_in = sem("more_in")
        late_in = sem("late_in")
        late_ready = sem("late_ready")
        bias_ready = sem("bias_ready")
        zeroed = sem("zeroed")
        zero_tile = sem("zero_tile")
        sort_step = sem("sort_step")
        score_ready = sem("score_ready")
        ranked = sem("ranked")
        texp_ready = sem("texp_ready")
        scaled = sem("scaled")
        scattered = sem("scattered")
        for n in "gated lifted acted down added squared".split():
            S["h_" + n] = sem("h_" + n)
        xs_in = [sem(f"xs_in{c}") for c in range(4)]
        for n in "turned turned_kept lifted gated acted act_turned act_kept down kept".split():
            S["e_" + n] = sem("e_" + n)
        stored = sem("stored")
        y_in = [sem(f"y_in{c}") for c in range(NT // 4)]
        swapped = sem("swapped")
        swap_in = sem("swap_in")
        crms_step = sem("crms_step")
        plug_step = sem("plug_step")
        plug_out = sem("plug_out")
        plug_in = sem("plug_in")
        places_cleared = sem("places_cleared")
        rms_step = sem("rms_step")
        rms_ready = sem("rms_ready")
        rms_eps = sem("rms_eps")
        mean_ready = sem("mean_ready")
        for n in "hp_ready depooled dp_kept picked placed put".split():
            S["c_" + n] = sem("c_" + n)
        for n in ("y_in x2 stats moments copied hn_ready hnT_done hnT_kept added mixed x3 stats2 moments2 var_eps rstd "
                  "normed xnT_done xnT_kept routed lg m8 i8 ixf mk0 mask_ready spread mask_turned mask_kept masked "
                  "summed out_ready").split():
            S["l_" + n] = sem("l_" + n)
        out_done = sem("out_done")
        PLUG_STEPS = 8

        block = ctx.enter_context(nc.Block())

        def arrived(eng, sems, tile):
            if tile is not None and tile.turn is None:
                for c, (lo, _) in enumerate(TILE_CHUNKS):
                    if tile.n == lo:
                        eng.wait_ge(sems[c], 16)
                        eng.nop(nofuse=True)

        def credit(eng, *entries):
            for name, per_tile in entries:
                eng.sem_inc(S[name], CREDIT * per_tile)

        @block.sync
        def _(sp):
            sp.dma_start(X[:, 0:2 * D], x[:, 0:2 * D]).then_inc(x_in[0], 16)
            sp.dma_start(cst[:], consts).then_inc(consts_in, 16)
            sp.dma_start(CK[:, 0:2 * D], ctx_k[:, 0:2 * D]).then_inc(ck_in[0], 16)
            sp.dma_start(wqkv[:], w_qkv).then_inc(weights_in, 16)
            sp.dma_start(gate[:], gates).then_inc(consts_in, 16)
            sp.dma_start(wproj[:], w_proj).then_inc(weights_in, 16)
            sp.dma_start(bproj[:], b_proj).then_inc(weights_in, 16)
            for c in range(3):
                lo, hi = TILE_CHUNKS[c]
                if c:
                    sp.dma_start(X[:, lo * D:hi * D], x[:, lo * D:hi * D]).then_inc(x_in[c], 16)
                    sp.dma_start(CK[:, lo * D:hi * D], ctx_k[:, lo * D:hi * D]).then_inc(ck_in[c], 16)
                sp.dma_start(CV[:, lo * D:hi * D], ctx_v_swapped[:, lo * D:hi * D]).then_inc(cv_in[c], 16)
            for dst, src in ((gatew, gate_w), (shgu, sh_gate_up), (pm_i, patch_mask)):
                sp.dma_start(dst[:], src).then_inc(more_in, 16)
            for dst, src in ((shd, sh_down), (rgu, rt_gate_up), (rdn, rt_down), (winT, w_in), (binB, b_in),
                             (gres, g_res), (ginit, g_init), (rw1, router_w), (rb1, router_b), (w1, expert_w),
                             (b1, expert_b)):
                sp.dma_start(dst[:], src).then_inc(late_in, 16)
            sp.wait_ge(zero_tile, 1)
            sx = sorted_x.rearrange("(c p r) d -> c p (r d)", p=P, r=8)
            for c in range(NS // 8):
                sp.dma_start(sx[c], zeros[:]).then_inc(zeroed, 16)

            def step(stage):
                a = stage(3)
                if a:
                    sp.wait_ge(S["max_kept"], a.done())
                    for hg in range(HG):
                        sp.dma_start(qbd[32 * hg + 24:32 * hg + 25, a.slot, :, hg, :],
                                     mT[HG * hg:HG * hg + G, a.par, :]).then_inc(shift_placed[a.par], 16)

            walk(sp, NT, LAGS, step)
            credit(sp, ("l_y_in", 1))
            sp.wait_ge(scattered, 16 * NT)

            def load_and_store(stage):
                l, d = stage(0), stage(7)
                if l:
                    if not (l.turn is None and l.n < 4):
                        sp.wait_ge(S["e_turned"], l.freed(back=4))
                    sp.dma_start(xs[:, l.slot, :], sorted_x[ds(l.t * P, P)]).then_inc(xs_in[l.slot], 16)
                if d:
                    sp.wait_ge(S["e_kept"], d.done())
                    sp.dma_start(sorted_y[ds(d.t * P, P)], YS[:, d.cols(D)]).then_inc(stored, 16)

            walk(sp, NS, 7, load_and_store)
            for c in range(NT // 4):
                sp.wait_ge(y_in[c], 64)
                sp.sem_inc(S["l_y_in"], 4)

            def store_out(stage):
                o = stage(9)
                if o:
                    sp.wait_ge(S["l_out_ready"], o.done())
                    sp.dma_start(out[:, o.cols(D)], X[:, o.cols(D)]).then_inc(out_done, 16)

            walk(sp, NT, 9, store_out)
            sp.wait_ge(out_done, 16 * NT)

        @block.gpsimd
        def _(pool):
            credit(pool, ("rstd_ready", 1), ("var_eps", 1), ("bias_added", 1), ("v_spread", 1),
                   ("v_half", 1), ("r_copied", 1), ("r_var_eps", 1))
            pool.memset(zeros[:], 0.0).then_inc(zero_tile, 1)
            pool.memset(halfneg[:], -0.5)
            pool.memset(epsc[:], EPS)
            pool.memset(stack[:], 0.0)
            pool.memset(vp[:], 1.0).then_inc(pool_consts, 1)
            pool.wait_ge(pool_consts, 1)
            pool.memset(stack[:, :, 1:3, :, 24:25], 1.0)
            pool.memset(qbd, 0.0).then_inc(pool_consts, 1)
            pool.wait_ge(pool_consts, 2)

            def step(stage):
                l, f, a, m = stage(0), stage(1), stage(4), stage(7)
                if m:
                    pool.wait_ge(S["r_moments"], m.done())
                    pool.tensor_tensor(ve2[:, m.par:m.par + 1], mv2[:, m.par, 1:2], epsc[:], ALU.add)\
                        .then_inc(S["r_var_eps"], 1)
                    pool.tensor_copy(mvr[:, ds(m.t, 1)], mv2[:, m.par, 0:1])
                    pool.wait_ge(S["r_var_eps"], m.done())
                    pool.tensor_tensor(rstdr[:, ds(m.t, 1)], ve2[:, m.par:m.par + 1], halfneg[:], ALU.pow)\
                        .then_inc(S["r_copied"], 1)
                if a:
                    arrived(pool, cv_in, a)
                    pool.wait_ge(S["v_kept"], a.done())
                    pool.wait_ge(S["averaged"], a.freed(4, 3))
                    if f:
                        pool.wait_ge(S["bias_added"], f.freed(back=1))
                    for half in range(2):
                        if half:
                            pool.wait_ge(S["v_half"], a.done())
                        rows = slice(64 * half, 64 * half + 64)
                        pool.tensor_copy(vp[rows, a.par, half, :, 0:HD],
                                         VALL[rows, a.cols(D)].rearrange("p (h d) -> p h d", h=H))
                        pool.tensor_copy(vp[rows, a.par, 1 - half, :, 0:HD],
                                         CV[rows, a.cols(D)].rearrange("p (h d) -> p h d", h=H))\
                            .then_inc(S["v_spread" if half else "v_half"], 1)
                    pool.wait_ge(S["v_spread"], a.done())
                if l:
                    pool.wait_ge(S["moments"], l.done())
                    pool.tensor_tensor(ve[:, l.par:l.par + 1], mv[:, l.par, 1:2], epsc[:], ALU.add)\
                        .then_inc(S["var_eps"], 1)
                    pool.wait_ge(S["var_eps"], l.done())
                    pool.tensor_tensor(rstd[:, l.par:l.par + 1], ve[:, l.par:l.par + 1], halfneg[:], ALU.pow)\
                        .then_inc(S["rstd_ready"], 1)
                if f:
                    pool.wait_ge(S["normed"], f.done())
                    if f.turn is None and f.n == 0:
                        pool.wait_ge(weights_ready, 3)
                    xt = X[:, f.cols(D)]
                    pool.tensor_tensor(xt, xt, bproj[:], ALU.add).then_inc(S["bias_added"], 1)

            def loads():
                pool.wait_ge(cv_in[2], 16)

            walk(pool, NT, LAGS + 1, step, loads)

            pool.wait_ge(late_in, 16 * 11)
            pool.wait_ge(gates_ready, 1)
            for w, k in ((shd, 2), (rdn, 2), (binB, 1), (ginit, 1), (w1, 3)):
                pool.tensor_scalar(w[:], w[:], tgate[:, k:k + 1], None, ALU.mult).then_inc(late_ready, 1)
            pool.tensor_scalar(winT[:], winT[:], gres[:], tgate[:, 1:2], ALU.mult, ALU.mult).then_inc(late_ready, 1)

            pool.wait_ge(zeroed, 16 * (NS // 8))
            for t in range(NT):
                if t % 8 == 0:
                    pool.wait_ge(scaled, t // 8 + 1)
                pool.indirect_dma_start(out=sorted_x, out_offset=bass.IndirectOffsetOnAxis(ap=posu[:, t:t + 1], axis=0),
                                        in_=XN2[:, t * D:t * D + D], in_offset=None).then_inc(scattered, 16)
            pool.wait_ge(S["h_lifted"], Tile(NC - 1).done(2, 1))
            pool.memset(XNT[:], -1.0).then_inc(places_cleared, 1)

            pool.wait_ge(places_cleared, 1)
            pool.wait_ge(plug_step, PLUG_STEPS)
            pool.dma_start(plugs, pm[:, 5, :]).then_inc(plug_out, 16)
            pool.wait_ge(plug_out, 16)
            for q in range(PAIRS):
                rows = slice(SEQ * q, SEQ * q + SEQ)
                pool.dma_start(XNT[rows].rearrange("p (t s) -> p t s", t=NT)[:, :, SEQ * q:SEQ * q + SEQ],
                               plugs.rearrange("(t q) s -> q t s", q=PAIRS)[q:q + 1].to_broadcast([SEQ, NT, SEQ]))\
                    .then_inc(plug_in, 16)
            pool.wait_ge(S["h_squared"], Tile(NC - 1).done(2 * CT, 2 * CT - 1))
            for q in range(PAIRS):
                pool.dma_start(ssv[SEQ * q:SEQ * q + SEQ, 1, :], ssv[SEQ * (1 - q):SEQ * (2 - q), 0, :])\
                    .then_inc(swap_in, 16)
            pool.wait_ge(crms_step, 2)
            pool.tensor_tensor(crms[:], crms[:], halfneg[:].to_broadcast([P, NT]), ALU.pow).then_inc(crms_step, 1)
            pool.wait_ge(stored, 16 * NS)
            for t in range(NT):
                pool.indirect_dma_start(out=XN2[:, t * D:t * D + D], out_offset=None, in_=sorted_y,
                                        in_offset=bass.IndirectOffsetOnAxis(ap=posu[:, t:t + 1], axis=0))\
                    .then_inc(y_in[t // 4], 16)

            for h in range(2):
                half = slice(h * NT // 2, (h + 1) * NT // 2)
                pool.wait_ge(rms_ready, h + 1)
                pool.tensor_tensor(rr[:, half], rchain[:, 1, half], halfneg[:].to_broadcast([P, NT // 2]), ALU.pow)\
                    .then_inc(rms_step, 1)
            credit(pool, ("l_var_eps", 1), ("l_rstd", 1), ("l_added", 1))

            def last_step(stage):
                f, a = stage(1), stage(3)
                if f:
                    pool.wait_ge(S["l_hn_ready"], f.done())
                    if f.turn is None and f.n == 0:
                        pool.wait_ge(S["c_put"], Tile(NT - 1).done())
                    pool.tensor_tensor(X[:, f.cols(D)], X[:, f.cols(D)], DP[:, f.cols(D)], ALU.add)\
                        .then_inc(S["l_added"], 1)
                if a:
                    pool.wait_ge(S["l_moments2"], a.done())
                    pool.tensor_tensor(ve[:, a.par:a.par + 1], mv2[:, a.par, 1:2], epsc[:], ALU.add)\
                        .then_inc(S["l_var_eps"], 1)
                    pool.wait_ge(S["l_var_eps"], a.done())
                    pool.tensor_tensor(rstd[:, a.par:a.par + 1], ve[:, a.par:a.par + 1], halfneg[:], ALU.pow)\
                        .then_inc(S["l_rstd"], 1)

            walk(pool, NT, 9, last_step)

        @block.scalar
        def _(act):
            credit(act, ("xnT_kept", 1), ("exped", 4), ("on_kept", 1), ("hi_ready", 1), ("v_kept", 1),
                   ("max_kept", 1), ("o_kept", 1), ("ctx_hi", 1), ("q_kept", 1))
            act.wait_ge(consts_in, 32)
            nc.scalar.activation(tgate[:], gate[:], ACT.Tanh).then_inc(gates_ready, 1)

            def ctx_hi(f):
                arrived(act, ck_in, f)
                act.wait_ge(S["ctx_turned"], f.freed())
                nc.scalar.copy(hi_twice(f.par, 2), twice_over(CK[:, f.cols(D)].rearrange("p (h d) -> p h d", h=H)))\
                    .then_inc(S["ctx_hi"], 1)

            def exp_chunk(b, j):
                act.wait_ge(S["scored_t"], b.done(4, j))
                act.wait_ge(S["averaged"], b.freed(4, j, back=4))
                nc.scalar.activation(pexp[:, j, :], PS[:, 2 + j % 2, :], ACT.Exp).then_inc(S["exped"], 1)

            def step(stage):
                f, s, a, b, n = (stage(i) for i in (1, 2, 3, 5, 6))
                if s:
                    act.wait_ge(S["q_spread"], s.freed(back=1))
                    act.wait_ge(S["qk_turned"], s.done())
                    nc.scalar.copy(qc[:], bank16(5)[:, 0:512].rearrange("p (g t) -> p g t", g=G))\
                        .then_inc(S["q_kept"], 1)
                if b:
                    exp_chunk(b, 0)
                    exp_chunk(b, 1)
                if f:
                    act.wait_ge(S["qkv_done"], f.freed())
                    act.wait_ge(S["xnT_done"], f.done())
                    nc.scalar.copy(xnT[:, f.par, :], PS[:, 4, 0:P]).then_inc(S["xnT_kept"], 1)
                    if f.turn is None and f.n == 0:
                        act.wait_ge(pool_consts, 2)
                    ctx_hi(f)
                if b:
                    exp_chunk(b, 2)
                if f:
                    act.wait_ge(S["qk_turned"], f.freed())
                    act.wait_ge(S["qkv_done"], f.done())
                    for w in range(2):
                        src = PS[:, 4, P * (1 + w):P * (2 + w)].rearrange("p (h d) -> p h d", h=H)
                        last = nc.scalar.copy(hi_twice(f.par, w), twice_over(src))
                    last.then_inc(S["hi_ready"], 1)
                    nc.scalar.copy(VALL[:, f.cols(D)], PS[:, 4, 3 * P:4 * P]).then_inc(S["v_kept"], 1)
                if b:
                    exp_chunk(b, 3)
                if n:
                    act.wait_ge(S["projected"], n.freed())
                    act.wait_ge(S["on_turned"], n.done())
                    nc.scalar.copy(onT[:, n.par, :], PS[:, 6, 0:P]).then_inc(S["on_kept"], 1)
                if a:
                    if not (a.turn is None and a.n < 2):
                        act.wait_ge(shift_placed[a.par], 64 * a.pair)
                    act.wait_ge(S["max_turned"], a.done())
                    nc.scalar.copy(mT[:, a.par, :], bank16(0)[0:H, 0:P]).then_inc(S["max_kept"], 1)
                if b:
                    act.wait_ge(S["o_turned"], b.freed())
                    act.wait_ge(S["averaged"], b.done(4, 3))
                    nc.scalar.copy(oS[:, b.par, :], PS[:, 7, :]).then_inc(S["o_kept"], 1)

            walk(act, NT, LAGS, step, lambda: act.wait_ge(ck_in[2], 16))

            credit(act, ("r_kept", 1), ("r_xnT_kept", 1), ("h_gated", 2), ("h_squared", 2 * CT),
                   ("e_turned_kept", 1), ("e_gated", 1),
                   ("e_act_kept", 1), ("c_dp_kept", 1), ("l_copied", 1), ("l_hn_ready", 1), ("l_hnT_kept", 1), ("l_xnT_kept", 1),
                   ("l_mask_kept", 1))

            def router_step(stage):
                f = stage(1)
                if f:
                    act.wait_ge(S["r_normed"], f.done())
                    nc.scalar.copy(XN2[:, f.cols(D)], xn[:, f.par, :]).then_inc(S["r_kept"], 1)
                    act.wait_ge(S["r_routed"], f.freed())
                    act.wait_ge(S["r_xnT_done"], f.done())
                    nc.scalar.copy(xnT[:, f.par, :], PS[:, f.par, 0:P])
                    nc.scalar.copy(XNT[:, f.cols(P)], PS[:, f.par, 0:P]).then_inc(S["r_xnT_kept"], 1)

            walk(act, NT, 3, router_step)
            act.wait_ge(sort_step, 1)
            nc.scalar.activation(score[:], top[:], ACT.Sigmoid).then_inc(score_ready, 1)

            def shared_step(stage):
                c = stage(0)
                if c:
                    for i in range(2):
                        act.wait_ge(S["h_lifted"], c.done(2, i))
                        act.wait_ge(S["h_acted"], c.freed(2, i, back=2))
                        nc.scalar.activation(sg[:, i, :], PS[:, 2 * i, :], ACT.Silu).then_inc(S["h_gated"], 1)
                    for q in range(CT):
                        for half, ss in ((CK, ssk[:, ds(c.t * CT + q, 1)]), (CV, ssv[:, 0, ds(c.t * CT + q, 1)])):
                            k = int(half is CV)
                            act.wait_ge(S["h_squared"], c.freed(2 * CT, 2 * q + k, back=2))
                            nc.scalar.activation(sqj[:, k, :], half[:, ds((c.t * CT + q) * D, D)], ACT.Square,
                                                 accum_out=ss).then_inc(S["h_squared"], 1)

            walk(act, NC, 1, shared_step, unroll=2)

            def sorted_step(stage):
                f, s, a = stage(2), stage(3), stage(4)
                if s:
                    act.wait_ge(S["e_acted"], s.freed())
                    act.wait_ge(S["e_lifted"], s.done())
                    nc.scalar.activation(sg[:, s.par, 0:FF], PS[:, 2 + s.par, 0:FF], ACT.Silu)\
                        .then_inc(S["e_gated"], 1)
                if f:
                    act.wait_ge(S["e_lifted"], f.freed())
                    act.wait_ge(S["e_turned"], f.done())
                    nc.scalar.copy(xsT[:, f.par, :], PS[:, f.par, 0:P]).then_inc(S["e_turned_kept"], 1)
                if a:
                    act.wait_ge(S["e_down"], a.freed())
                    act.wait_ge(S["e_act_turned"], a.done())
                    nc.scalar.copy(act2T[:, a.par, :], PS[:, 4 + a.par, 0:FF]).then_inc(S["e_act_kept"], 1)

            walk(act, NS, 7, sorted_step)

            def context_step(stage):
                f, s = stage(1), stage(2)
                if f:
                    act.wait_ge(S["c_placed"], f.freed())
                    act.wait_ge(S["c_depooled"], f.done())
                    nc.scalar.copy(dp[:, f.par, :], PS[:, f.par, 0:D]).then_inc(S["c_dp_kept"], 1)
                if s:
                    act.wait_ge(S["l_moments"], s.done())
                    nc.scalar.copy(mvl[:, ds(s.t, 1), :], mv[:, s.par, :].unsqueeze(1)).then_inc(S["l_copied"], 1)

            walk(act, NT, 3, context_step)
            act.wait_ge(mean_ready, 1)

            def last_step(stage):
                l, f, b, m = stage(0), stage(1), stage(5), stage(7)
                if l:
                    act.wait_ge(S["l_hnT_done"], l.freed())
                    nc.scalar.activation(hn[:, l.par, :], X[:, l.cols(D)], ACT.Identity, bias=mrr[:, ds(l.t, 1)],
                                         scale=rr[:, ds(l.t, 1)]).then_inc(S["l_hn_ready"], 1)
                if f:
                    act.wait_ge(S["l_mixed"], f.freed())
                    act.wait_ge(S["l_hnT_done"], f.done())
                    nc.scalar.copy(hnT[:, f.par, :], PS[:, 0, 0:P]).then_inc(S["l_hnT_kept"], 1)
                if b:
                    if not (b.turn is None and b.n < 2):
                        act.wait_ge(S["l_masked"], b.freed(back=4))
                    act.wait_ge(S["l_xnT_done"], b.done())
                    nc.scalar.copy(xnT4[:, b.slot, :], PS[:, 2, 0:P]).then_inc(S["l_xnT_kept"], 1)
                if m:
                    act.wait_ge(S["l_summed"], m.freed())
                    act.wait_ge(S["l_mask_turned"], m.done())
                    nc.scalar.copy(mask1T[:, m.par, :], bank16(0)[0:E, 512:512 + P]).then_inc(S["l_mask_kept"], 1)

            walk(act, NT, 9, last_step)

        @block.vector
        def _(dve):
            credit(dve, ("stats", 1), ("moments", 1), ("normed", 1), ("lo_ready", 2), ("ctx_stacked", 1),
                   ("q_spread", 1), ("k_kept", 1), ("ctx_kept", 1), ("maxed", 4), ("recip_ready", 1),
                   ("o_normed", 1), ("x_updated", 1), ("r_stats", 1), ("r_moments", 1))
            dve.wait_ge(consts_in, 32)
            dve.tensor_copy(ident16[:], identf).then_inc(weights_ready, 1)
            dve.wait_ge(weights_in, 48)
            dve.tensor_scalar(wqkv[:, 0:D], wqkv[:, 0:D], float(HD) ** -0.5, None, ALU.mult)
            dve.wait_ge(gates_ready, 1)
            dve.tensor_scalar(wproj[:], wproj[:], tgate[:, 0:1], None, ALU.mult).then_inc(weights_ready, 1)
            dve.tensor_scalar(bproj[:], bproj[:], tgate[:, 0:1], None, ALU.mult).then_inc(weights_ready, 1)
            dve.wait_ge(pool_consts, 2)

            def max_chunk(a, j):
                dve.wait_ge(S["scored"], a.done(4, j))
                dve.tensor_reduce(negm[:, a.par, :, j], PS[:, j % 2, :].rearrange("p (h k) -> p h k", h=HG),
                                  AX.X, ALU.max, negate=True).then_inc(S["maxed"], 1)

            def step(stage):
                l, f, s, a, n, m = (stage(i) for i in (0, 1, 2, 3, 6, 7))
                if m:
                    dve.wait_ge(S["x_updated"], m.done())
                    dve.nop(nofuse=True)
                    dve.bn_stats(str_[:, m.par, :], X[:, m.cols(D)]).then_inc(S["r_stats"], 1)
                if a:
                    max_chunk(a, 0)
                    max_chunk(a, 1)
                if m:
                    dve.wait_ge(S["r_copied"], m.freed())
                    dve.wait_ge(S["r_stats"], m.done())
                    dve.nop(nofuse=True)
                    dve.bn_aggr(mv2[:, m.par, :], str_[:, m.par, :])\
                        .then_inc(S["r_moments"], 1)
                if l:
                    arrived(dve, x_in, l)
                    dve.bn_stats(st[:, l.par, :], X[:, l.cols(D)]).then_inc(S["stats"], 1)
                    dve.wait_ge(S["stats"], l.done())
                    dve.nop(nofuse=True)
                    dve.bn_aggr(mv[:, l.par, :], st[:, l.par, :]).then_inc(S["moments"], 1)
                if s:
                    dve.wait_ge(S["q_kept"], s.done())
                    for b in range(2):
                        src = bank16(5)[:, 512:1024].rearrange("p (g t) -> p g t", g=G)[:, :, 64 * b:64 * b + 64]
                        last = dve.tensor_copy(kt[:, s.slot, b, :, 64 * b:64 * b + 64], src)
                    last.then_inc(S["k_kept"], 1)
                if s:
                    dve.wait_ge(S["ctx_turned"], s.done())
                    for b in range(2):
                        src = bank16(6)[:, 0:512].rearrange("p (g t) -> p g t", g=G)[:, :, 64 * b:64 * b + 64]
                        last = dve.tensor_copy(kt[:, s.slot, b, :, 64 * (1 - b):128 - 64 * b], src)
                    last.then_inc(S["ctx_kept"], 1)
                if s:
                    for hg in range(HG):
                        rows = slice(32 * hg, 32 * hg + 32)
                        last = dve.tensor_copy(qbd[rows, s.slot, :, hg, :], qc[rows])
                    last.then_inc(S["q_spread"], 1)
                if a:
                    max_chunk(a, 2)
                if n:
                    dve.wait_ge(S["o_turned"], n.done())
                    o = PS[:, 5, :].rearrange("p (h w) -> p h w", h=H)
                    dve.reciprocal(rden[:, n.par, :], o[:, :, HD:HD + 1]).then_inc(S["recip_ready"], 1)
                    dve.wait_ge(S["recip_ready"], n.done())
                    dve.tensor_tensor(on[:, n.par, :].rearrange("p (h d) -> p h d", h=H), o[:, :, 0:HD],
                                      rden[:, n.par, :].unsqueeze(2).to_broadcast([P, H, HD]), ALU.mult)\
                        .then_inc(S["o_normed"], 1)
                if a:
                    max_chunk(a, 3)
                if f:
                    dve.wait_ge(S["v_kept"], f.done())
                    for w, col in ((0, 16), (1, 8)):
                        dve.tensor_tensor(stack[:, f.par, w, :, col:col + 8],
                                          PS[:, 4, P * (1 + w):P * (2 + w)].rearrange("p (h d) -> p h d", h=H),
                                          stack[:, f.par, w, :, 0:8], ALU.subtract).then_inc(S["lo_ready"], 1)
                    dve.wait_ge(S["ctx_hi"], f.done())
                    dve.tensor_tensor(stack[:, f.par, 2, :, 8:16], CK[:, f.cols(D)].rearrange("p (h d) -> p h d", h=H),
                                      stack[:, f.par, 2, :, 0:8], ALU.subtract).then_inc(S["ctx_stacked"], 1)
                if l:
                    dve.wait_ge(S["xnT_done"], l.freed())
                    dve.wait_ge(S["rstd_ready"], l.done())
                    dve.tensor_scalar(xn[:, l.par, :], X[:, l.cols(D)], mv[:, l.par, 0:1],
                                      rstd[:, l.par:l.par + 1], ALU.subtract, ALU.mult).then_inc(S["normed"], 1)
                if n:
                    dve.wait_ge(S["bias_added"], n.done())
                    dve.wait_ge(S["projected"], n.done())
                    dve.tensor_tensor(X[:, n.cols(D)], PS[:, 6, P:2 * P], X[:, n.cols(D)], ALU.add)\
                        .then_inc(S["x_updated"], 1)

            walk(dve, NT, LAGS + 1, step, lambda: dve.wait_ge(x_in[2], 16))

            credit(dve, ("r_normed", 1), ("r_logits", 1), ("h_acted", 2), ("h_added", 1), ("e_acted", 1), ("e_kept", 1),
                   *((n, 1) for n in ("c_hp_ready c_picked c_put l_x2 l_stats l_moments l_x3 l_stats2 l_moments2 "
                                      "l_normed l_lg l_m8 l_i8 l_ixf l_mk0 l_mask_ready l_masked l_out_ready")
                     .split()))

            def router_step(stage):
                l, a = stage(0), stage(3)
                if l:
                    if l.turn is None and l.n == 0:
                        dve.wait_ge(S["r_copied"], Tile(NT - 1).done())
                    dve.wait_ge(S["r_xnT_done"], l.freed())
                    dve.wait_ge(S["r_kept"], l.freed())
                    dve.tensor_scalar(xn[:, l.par, :], X[:, l.cols(D)], mvr[:, ds(l.t, 1)],
                                      rstdr[:, ds(l.t, 1)], ALU.subtract, ALU.mult).then_inc(S["r_normed"], 1)
                if a:
                    dve.wait_ge(S["r_routed"], a.done())
                    dve.tensor_copy(LG[:, ds(a.t, 1), :], PS[:, 2 + a.par, 0:E].unsqueeze(1))\
                        .then_inc(S["r_logits"], 1)

            walk(dve, NT, 3, router_step)

            chained = [0]

            def then(ins):
                chained[0] += 1
                ins.then_inc(sort_step, 1)
                dve.wait_ge(sort_step, chained[0])

            def over_tiles(a):
                return a.unsqueeze(2).to_broadcast([P, E, NT])

            dve.wait_ge(S["r_logits"], Tile(NT - 1).done())
            then(dve.tensor_reduce(top[:], LG[:], AX.X, ALU.max))
            then(dve.tensor_tensor(isel[:], LG[:], top[:].unsqueeze(2).to_broadcast([P, NT, E]), ALU.is_equal))
            no8 = exp_no8.unsqueeze(1).to_broadcast([P, NT, E])
            then(dve.tensor_tensor(isel[:], isel[:], no8, ALU.mult))
            then(dve.tensor_reduce(first8[:], isel[:], AX.X, ALU.min))
            dve.tensor_copy(upper16[:], upper)
            dve.tensor_copy(ones16[:], ones)
            dve.memset(onesf[:], 1.0)
            then(dve.tensor_tensor(onehot[:].rearrange("p e t -> p t e"),
                                   first8[:].unsqueeze(2).to_broadcast([P, NT, E]), no8, ALU.is_equal))
            dve.wait_ge(ranked, 1)
            then(dve.tensor_copy(tot[:], PS[:, 5, 0:E * NT].rearrange("p (e t) -> p e t", e=E)))
            then(dve.tensor_tensor_scan(run[:].rearrange("p e t -> p (e t)"), onesf[:],
                                        tot[:].rearrange("p e t -> p (e t)"), 0.0, ALU.mult, ALU.add))
            then(dve.tensor_reduce(cnt[:, 0, :], tot[:], AX.X, ALU.add))
            then(dve.tensor_scalar(cnti[:, 0, :], cnt[:, 0, :], float(P - 1), None, ALU.add))
            then(dve.tensor_scalar(cnti[:, 1, :], cnti[:, 0, :], 7, 7, ALU.logical_shift_right, ALU.logical_shift_left))
            then(dve.tensor_copy(cnt[:, 1, :], cnti[:, 1, :]))
            then(dve.tensor_tensor_scan(cnt[:, 2, :], onesf[:, 0:E], cnt[:, 1, :], 0.0, ALU.mult, ALU.add))
            then(dve.tensor_tensor(cnt[:, 3, :], cnt[:, 2, :], cnt[:, 1, :], ALU.subtract))
            then(dve.tensor_tensor(cnt[:, 4, :], cnt[:, 0, :], run[:, :, NT - 1], ALU.subtract))
            then(dve.tensor_tensor(cnt[:, 5, :], cnt[:, 3, :], cnt[:, 4, :], ALU.add))
            then(dve.tensor_tensor(run[:], run[:], tot[:], ALU.subtract))
            then(dve.tensor_tensor(run[:], PS[:, 4, 0:E * NT].rearrange("p (e t) -> p e t", e=E), run[:], ALU.add))
            then(dve.tensor_tensor(run[:], run[:], over_tiles(cnt[:, 5, :]), ALU.add))
            then(dve.tensor_tensor(run[:], run[:], onehot[:], ALU.mult))
            then(dve.tensor_reduce(posf[:], run[:].rearrange("p e t -> p t e"), AX.X, ALU.add))
            then(dve.tensor_copy(posu[:], posf[:]))
            dve.wait_ge(score_ready, 1)
            for c in range(NT // 8):
                rows = XN2[:, c * 8 * D:(c + 1) * 8 * D].rearrange("p (t d) -> p t d", t=8)
                dve.tensor_tensor(rows, rows, score[:, c * 8:(c + 1) * 8].unsqueeze(2).to_broadcast([P, 8, D]),
                                  ALU.mult).then_inc(scaled, 1)
            then(dve.tensor_tensor(tcmp[:], tile_start.unsqueeze(2).to_broadcast([P, NS, E - 1]),
                                   cnt[:, 2, 0:E - 1].unsqueeze(1).to_broadcast([P, NS, E - 1]), ALU.is_ge))
            then(dve.tensor_reduce(texpf[:], tcmp[:], AX.X, ALU.add))
            digits = texpf[:].rearrange("p (s k) -> p s k", k=4)
            for k in range(1, 4):
                then(dve.scalar_tensor_tensor(out=digits[:, :, 0], in0=digits[:, :, k], scalar=float(E ** k),
                                              in1=digits[:, :, 0], op0=ALU.mult, op1=ALU.add))
            dve.tensor_copy(texp[:], digits[:, :, 0]).then_inc(texp_ready, 1)

            def shared_step(stage):
                c, d = stage(0), stage(1)
                if c:
                    for i in range(2):
                        if i == 0:
                            dve.wait_ge(S["h_down"], c.freed())
                        dve.wait_ge(S["h_gated"], c.done(2, i))
                        dve.tensor_tensor(hact[:, c.par, i, :], PS[:, 2 * i + 1, :], sg[:, i, :], ALU.mult)\
                            .then_inc(S["h_acted"], 1)
                if d:
                    dve.wait_ge(S["h_down"], d.done())
                    xc = X[:, ds(d.t * CT * D, CT * D)]
                    dve.tensor_tensor(xc, PS[:, 6 + d.par, :], xc, ALU.add).then_inc(S["h_added"], 1)

            walk(dve, NC, 1, shared_step, unroll=2)

            plugged = [0]

            def next_plug(ins):
                plugged[0] += 1
                ins.then_inc(plug_step, 1)
                dve.wait_ge(plug_step, plugged[0])

            def seq3(a, axis):
                return a.unsqueeze(axis).to_broadcast([SEQ, SEQ, SEQ])

            dve.wait_ge(more_in, 48)
            place = place_no[0:SEQ]
            next_plug(dve.tensor_copy(pm[:, 0, :], pm_i[:]))
            next_plug(dve.tensor_tensor_scan(pm[:, 1, :], onesf[0:SEQ, 0:SEQ], pm[:, 0, :], -1.0, ALU.mult, ALU.add))
            next_plug(dve.tensor_scalar(pm[:, 2, :], pm[:, 1, :], 0.0, float(SEQ), ALU.is_lt, ALU.mult))
            next_plug(dve.tensor_tensor(pm[:, 2, :], pm[:, 1, :], pm[:, 2, :], ALU.add))
            next_plug(dve.tensor_tensor(pcmp[:], seq3(place, 2), seq3(pm[:, 2, :], 1), ALU.is_equal))
            next_plug(dve.tensor_reduce(pm[:, 3, :], pcmp[:], AX.X, ALU.max))
            next_plug(dve.tensor_tensor_scan(pm[:, 4, :], onesf[0:SEQ, 0:SEQ], pm[:, 3, :], -1.0, ALU.mult, ALU.add))
            next_plug(dve.tensor_scalar(pm[:, 5, :], pm[:, 4, :], 0.0, float(SEQ - 1), ALU.max, ALU.min))
            assert plugged[0] == PLUG_STEPS
            dve.wait_ge(swap_in, 32)
            dve.tensor_tensor(crms[:], ssk[:], ssv[:, 1, :], ALU.add).then_inc(crms_step, 1)
            dve.wait_ge(crms_step, 1)
            dve.tensor_scalar(crms[:], crms[:], 0.5 / D, EPS, ALU.mult, ALU.add).then_inc(crms_step, 1)
            dve.wait_ge(late_in, 16 * 11)
            dve.tensor_scalar(b1[:], b1[:], tgate[0:E, 3:4], None, ALU.mult).then_inc(bias_ready, 1)

            def sorted_step(stage):
                s, d = stage(3), stage(6)
                if d:
                    dve.wait_ge(S["e_down"], d.done())
                    dve.tensor_copy(YS[:, d.cols(D)], PS[:, 6 + d.par, 0:D]).then_inc(S["e_kept"], 1)
                if s:
                    dve.wait_ge(S["e_act_turned"], s.freed())
                    dve.wait_ge(S["e_gated"], s.done())
                    dve.tensor_tensor(hact[:, s.par, 0, 0:FF], PS[:, 2 + s.par, FF:2 * FF], sg[:, s.par, 0:FF],
                                      ALU.mult).then_inc(S["e_acted"], 1)

            walk(dve, NS, 7, sorted_step)
            dve.wait_ge(crms_step, 3)
            dve.wait_ge(plug_in, 32)
            dve.wait_ge(late_ready, 6)

            def context_step(stage):
                l, f, s, a = (stage(i) for i in range(4))
                if l:
                    dve.wait_ge(S["c_depooled"], l.freed())
                    dve.scalar_tensor_tensor(out=hp[:, l.par, :], in0=CK[:, l.cols(D)], scalar=crms[:, ds(l.t, 1)],
                                             in1=ginit[:], op0=ALU.mult, op1=ALU.mult).then_inc(S["c_hp_ready"], 1)
                if f:
                    dve.wait_ge(S["c_placed"], f.freed())
                    dve.tensor_scalar(pick[:, f.par, :], XNT[:, f.cols(P)], patch_no, None, ALU.is_equal)\
                        .then_inc(S["c_picked"], 1)
                if l:
                    dve.wait_ge(S["l_y_in"], l.done())
                    dve.tensor_tensor(X[:, l.cols(D)], X[:, l.cols(D)], XN2[:, l.cols(D)], ALU.add)\
                        .then_inc(S["l_x2"], 1)
                if s:
                    dve.wait_ge(S["l_copied"], s.freed())
                    dve.wait_ge(S["l_stats"], s.done())
                    dve.nop(nofuse=True)
                    dve.bn_aggr(mv[:, s.par, :], st[:, s.par, :])\
                        .then_inc(S["l_moments"], 1)
                if f:
                    dve.wait_ge(S["l_x2"], f.done())
                    dve.nop(nofuse=True)
                    dve.bn_stats(st[:, f.par, :], X[:, f.cols(D)]).then_inc(S["l_stats"], 1)
                if a:
                    dve.wait_ge(S["c_placed"], a.done())
                    dve.tensor_tensor(DP[:, a.cols(D)], PS[:, 2 + a.par, 0:D], binB[:], ALU.add)\
                        .then_inc(S["c_put"], 1)

            walk(dve, NT, 3, context_step)
            dve.wait_ge(S["l_copied"], Tile(NT - 1).done())
            var = mvl[:, :, 1]
            dve.tensor_scalar(rchain[:, 0, :], var, EPS, EPS, ALU.add, ALU.mult).then_inc(rms_eps, 1)
            dve.wait_ge(rms_eps, 1)
            for h in range(2):
                half = slice(h * NT // 2, (h + 1) * NT // 2)
                dve.tensor_tensor(rchain[:, 1, half], rchain[:, 0, half], mvl[:, half, 1], ALU.add)\
                    .then_inc(rms_ready, 1)
            dve.wait_ge(rms_step, 2)
            dve.scalar_tensor_tensor(out=mrr[:], in0=mvl[:, :, 0], scalar=-1.0, in1=rr[:], op0=ALU.mult,
                                     op1=ALU.mult).then_inc(mean_ready, 1)

            def last_step(stage):
                a, b, r, m, o = (stage(i) for i in (3, 4, 6, 7, 9))
                if a:
                    dve.wait_ge(S["l_added"], a.done())
                    dve.wait_ge(S["l_mixed"], a.done())
                    dve.tensor_tensor(X[:, a.cols(D)], PS[:, 1, 0:D], X[:, a.cols(D)], ALU.add).then_inc(S["l_x3"], 1)
                if b:
                    dve.wait_ge(S["l_xnT_done"], b.freed())
                    dve.wait_ge(S["l_rstd"], b.done())
                    dve.tensor_scalar(xn[:, b.par, :], X[:, b.cols(D)], mv2[:, b.par, 0:1], rstd[:, b.par:b.par + 1],
                                      ALU.subtract, ALU.mult).then_inc(S["l_normed"], 1)
                if r:
                    dve.wait_ge(S["l_routed"], r.done())
                    dve.tensor_tensor(lg1[:, r.par, :], PS[:, 3, 0:E], rb1[:], ALU.add).then_inc(S["l_lg"], 1)
                if a:
                    dve.wait_ge(S["l_x3"], a.done())
                    dve.nop(nofuse=True)
                    dve.bn_stats(st[:, a.par, :], X[:, a.cols(D)]).then_inc(S["l_stats2"], 1)
                if r:
                    dve.wait_ge(S["l_lg"], r.done())
                    dve.nop(nofuse=True)
                    dve.max(mx8[:, r.par, :], lg1[:, r.par, :]).then_inc(S["l_m8"], 1)
                if a:
                    dve.wait_ge(S["l_stats2"], a.done())
                    dve.nop(nofuse=True)
                    dve.bn_aggr(mv2[:, a.par, :], st[:, a.par, :]).then_inc(S["l_moments2"], 1)
                if r:
                    dve.wait_ge(S["l_m8"], r.done())
                    dve.nop(nofuse=True)
                    dve.max_index(ix8[:, r.par, :], mx8[:, r.par, :], lg1[:, r.par, :]).then_inc(S["l_i8"], 1)
                if m:
                    dve.wait_ge(S["l_spread"], m.done())
                    dve.wait_ge(S["l_summed"], m.freed())
                    dve.tensor_tensor(z[:, m.par], PS[:, 4:6, :].rearrange("p b (e t) -> p (b e) t", t=P),
                                      xnT4[:, m.slot, :].unsqueeze(1).to_broadcast([P, E, P]), ALU.mult)\
                        .then_inc(S["l_masked"], 1)
                if r:
                    dve.wait_ge(S["l_i8"], r.done())
                    dve.tensor_copy(ixf[:, r.par, :], ix8[:, r.par, 0:2]).then_inc(S["l_ixf"], 1)
                if o:
                    dve.wait_ge(S["l_summed"], o.done())
                    dve.tensor_tensor(X[:, o.cols(D)], PS[:, 6 + o.par, 0:D], X[:, o.cols(D)], ALU.add)\
                        .then_inc(S["l_out_ready"], 1)
                if r:
                    dve.wait_ge(S["l_mask_turned"], r.freed())
                    dve.wait_ge(S["l_spread"], r.freed())
                    dve.wait_ge(S["l_ixf"], r.done())
                    dve.tensor_scalar(mask1[:, r.par, 0, :], exp_no, ixf[:, r.par, 0:1], None, ALU.is_equal)\
                        .then_inc(S["l_mk0"], 1)
                    dve.wait_ge(S["l_mk0"], r.done())
                    dve.scalar_tensor_tensor(out=mask1[:, r.par, 1, :], in0=exp_no, scalar=ixf[:, r.par, 1:2],
                                             in1=mask1[:, r.par, 0, :], op0=ALU.is_equal, op1=ALU.add)\
                        .then_inc(S["l_mask_ready"], 1)

            walk(dve, NT, 9, last_step)

        @block.tensor
        def _(pe):
            credit(pe, ("xnT_done", 1), ("qkv_done", 1), ("qk_turned", 1), ("ctx_turned", 1), ("scored", 4),
                   ("max_turned", 1), ("scored_t", 4), ("averaged", 4), ("o_turned", 1), ("on_turned", 1),
                   ("projected", 1))
            pe.wait_ge(weights_ready, 3)
            pe.wait_ge(pool_consts, 2)

            def scores_for_max(a, j):
                if j == 0:
                    pe.wait_ge(S["q_spread"], a.done())
                    pe.wait_ge(S["k_kept"], a.done())
                    pe.wait_ge(S["ctx_kept"], a.done())
                pe.wait_ge(S["maxed"], a.freed(4, j, back=2))
                for hg in range(HG):
                    for b in range(2):
                        last = nc.tensor.matmul(PS[64 * b:64 * b + 64, j % 2, hg * P:hg * P + P],
                                                qbd[:, a.slot, j, hg, 64 * b:64 * b + 64], kt[:, a.slot, b, j, :],
                                                start=True, stop=True)
                last.then_inc(S["scored"], 1)

            def scores_by_key(b, j):
                if j == 0:
                    pe.wait_ge(shift_placed[b.par], 64 * (b.pair + 1))
                pe.wait_ge(S["exped"], b.freed(4, j, back=2))
                seq = j // 2
                for g2 in range(2):
                    g = 2 * (j % 2) + g2
                    last = nc.tensor.matmul(PS[:, 2 + j % 2, 256 * g2:256 * g2 + 256], kt[:, b.slot, seq, g, :],
                                            qbd[:, b.slot, g, :, SEQ * seq:SEQ * seq + SEQ], start=True, stop=True)
                last.then_inc(S["scored_t"], 1)

            def average(b, j):
                if j == 0:
                    pe.wait_ge(S["v_spread"], b.done())
                    pe.wait_ge(S["o_kept"], b.freed(back=1))
                pe.wait_ge(S["exped"], b.done(4, j))
                seq = j // 2
                for g2 in range(2):
                    g = 2 * (j % 2) + g2
                    for hg in range(HG):
                        last = nc.tensor.matmul(PS[32 * hg:32 * hg + 32, 7, g * P + SEQ * seq:g * P + SEQ * seq + SEQ],
                                                vp[:, b.par, seq, g * HG + hg, :],
                                                pexp[:, j, (g2 * HG + hg) * SEQ:(g2 * HG + hg + 1) * SEQ],
                                                start=True, stop=True)
                last.then_inc(S["averaged"], 1)

            def turn_stack(s, w, bank, col, done):
                for g in range(G):
                    last = nc.tensor.transpose(
                        bank16(bank)[:, col + g * P:col + (g + 1) * P],
                        stack[:, s.par, w, g * HG:g * HG + HG, :].rearrange("p h c -> p (h c)"), ident16[:])
                if done:
                    last.then_inc(S[done], 1)

            def step(stage):
                f, s, a, c, b, n = (stage(i) for i in range(1, 7))
                m = stage(7)
                if a:
                    if c:
                        pe.wait_ge(S["max_kept"], c.done())
                    scores_for_max(a, 0)
                    scores_for_max(a, 1)
                if s:
                    pe.wait_ge(S["hi_ready"], s.done())
                    pe.wait_ge(S["lo_ready"], s.done(2, 1))
                    if m:
                        pe.wait_ge(S["o_normed"], m.done())
                    turn_stack(s, 0, 5, 0, None)
                    turn_stack(s, 1, 5, 512, "qk_turned")
                if b:
                    scores_by_key(b, 0)
                    scores_by_key(b, 1)
                if s:
                    pe.wait_ge(S["ctx_stacked"], s.done())
                    if m:
                        pe.wait_ge(S["x_updated"], m.done())
                    turn_stack(s, 2, 6, 0, "ctx_turned")
                if f:
                    if s:
                        pe.wait_ge(S["v_kept"], s.done())
                        pe.wait_ge(S["lo_ready"], s.done(2, 1))
                    pe.wait_ge(S["normed"], f.done())
                    nc.tensor.transpose(PS[:, 4, 0:P], xn[:, f.par, :], identf).then_inc(S["xnT_done"], 1)
                if b:
                    average(b, 0)
                    scores_by_key(b, 2)
                if a:
                    scores_for_max(a, 2)
                if f:
                    pe.wait_ge(S["xnT_kept"], f.done())
                    nc.tensor.matmul(PS[:, 4, P:4 * P], xnT[:, f.par, :], wqkv[:], start=True, stop=True)\
                        .then_inc(S["qkv_done"], 1)
                if b:
                    average(b, 1)
                    scores_by_key(b, 3)
                if a:
                    scores_for_max(a, 3)
                if n:
                    pe.wait_ge(S["o_kept"], n.done())
                    if s:
                        pe.wait_ge(S["k_kept"], s.done())
                    for g in range(G):
                        last = nc.tensor.transpose(PS[:, 5, g * P:g * P + P], oS[:, n.par, g * P:g * P + P], identf)
                    last.then_inc(S["o_turned"], 1)
                if b:
                    average(b, 2)
                if n:
                    if s:
                        pe.wait_ge(S["ctx_kept"], s.done())
                    pe.wait_ge(S["o_normed"], n.done())
                    nc.tensor.transpose(PS[:, 6, 0:P], on[:, n.par, :], identf).then_inc(S["on_turned"], 1)
                if b:
                    average(b, 3)
                if a:
                    pe.wait_ge(S["maxed"], a.done(4, 3))
                    nc.tensor.transpose(bank16(0)[0:H, 0:P], negm[:, a.par, :, :].rearrange("p h g -> p (h g)"),
                                        ident16[:]).then_inc(S["max_turned"], 1)
                if n:
                    pe.wait_ge(S["on_kept"], n.done())
                    nc.tensor.matmul(PS[:, 6, P:2 * P], onT[:, n.par, :], wproj[:], start=True, stop=True)\
                        .then_inc(S["projected"], 1)

            walk(pe, NT, LAGS, step)

            credit(pe, *((n, 1) for n in ("r_xnT_done r_routed h_down e_turned e_act_turned e_lifted e_down c_depooled "
                                          "c_placed l_hnT_done l_mixed l_xnT_done l_routed l_spread l_mask_turned "
                                          "l_summed").split()), ("h_lifted", 2))
            pe.wait_ge(S["x_updated"], Tile(NT - 1).done())
            pe.wait_ge(more_in, 48)

            def router_step(stage):
                f, s = stage(1), stage(2)
                if f:
                    pe.wait_ge(S["r_xnT_kept"], f.freed())
                    pe.wait_ge(S["r_normed"], f.done())
                    nc.tensor.transpose(PS[:, f.par, 0:P], xn[:, f.par, :], identf).then_inc(S["r_xnT_done"], 1)
                if s:
                    pe.wait_ge(S["r_logits"], s.freed())
                    pe.wait_ge(S["r_xnT_kept"], s.done())
                    nc.tensor.matmul(PS[:, 2 + s.par, 0:64], xnT[:, s.par, :], gatew[:], start=True, stop=True)\
                        .then_inc(S["r_routed"], 1)

            walk(pe, NT, 3, router_step)
            pe.wait_ge(sort_step, 5)
            oh = onehot[:].rearrange("p e t -> p (e t)")
            nc.tensor.matmul(PS[:, 4, 0:E * NT], upper16[:], oh, start=True, stop=True)
            nc.tensor.matmul(PS[:, 5, 0:E * NT], ones16[:], oh, start=True, stop=True).then_inc(ranked, 1)

            def shared_step(stage):
                c, d = stage(0), stage(1)
                if c:
                    if c.turn is None and c.n == 0:
                        pe.wait_ge(S["r_xnT_kept"], Tile(NT - 1).done())
                        pe.wait_ge(S["r_logits"], Tile(NT - 1).done())
                    for i in range(2):
                        pe.wait_ge(S["h_acted"], c.freed(2, i, back=2))
                        rows = XNT[:, ds(c.t * CT * P, CT * P)]
                        nc.tensor.matmul(PS[:, 2 * i, :], shgu[:, i * P:i * P + P], rows, start=True, stop=True)
                        nc.tensor.matmul(PS[:, 2 * i + 1, :], shgu[:, FF + i * P:FF + i * P + P], rows,
                                         start=True, stop=True).then_inc(S["h_lifted"], 1)
                if d:
                    if d.turn is None and d.n == 0:
                        pe.wait_ge(late_ready, 6)
                    pe.wait_ge(S["h_acted"], d.done(2, 1))
                    pe.wait_ge(S["h_added"], d.freed())
                    for q in range(CT):
                        for i in range(2):
                            last = nc.tensor.matmul(PS[:, 6 + d.par, q * P:q * P + P],
                                                    hact[:, d.par, i, q * P:q * P + P], shd[:, i * D:i * D + D],
                                                    start=(i == 0), stop=(i == 1))
                    last.then_inc(S["h_down"], 1)

            walk(pe, NC, 1, shared_step, unroll=2)

            pe.wait_ge(texp_ready, 1)
            four_experts = pe.alloc_register("four_experts")
            expert_of = [pe.alloc_register(f"expert_of_slot{k}") for k in range(4)]
            pe.wait_ge(S["h_added"], Tile(NC - 1).done())

            def sorted_step(stage):
                f, s, a, b = (stage(i) for i in range(2, 6))
                if s:
                    e_lift = pe.snap(expert_of[s.slot], min_val=0, max_val=E - 1)
                    pe.wait_ge(S["e_acted"], s.freed())
                    pe.wait_ge(S["e_turned_kept"], s.done())
                    nc.tensor.matmul(PS[:, 2 + s.par, :], xsT[:, s.par, :], rgu[:, ds(e_lift * (2 * FF), 2 * FF)],
                                     start=True, stop=True).then_inc(S["e_lifted"], 1)
                if f:
                    pe.wait_ge(S["e_turned_kept"], f.freed())
                    pe.wait_ge(xs_in[f.slot], 16 * (f.quad + 1))
                    nc.tensor.transpose(PS[:, f.par, 0:P], xs[:, f.slot, :], identf).then_inc(S["e_turned"], 1)
                if b:
                    e_down = pe.snap(expert_of[b.slot], min_val=0, max_val=E - 1)
                    pe.wait_ge(S["e_kept"], b.freed())
                    pe.wait_ge(S["e_act_kept"], b.done())
                    for i in range(2):
                        last = nc.tensor.matmul(PS[:, 6 + b.par, 0:D], act2T[:, b.par, i * P:i * P + P],
                                                rdn[:, ds(e_down * FF + i * D, D)], start=(i == 0), stop=(i == 1))
                    last.then_inc(S["e_down"], 1)
                if a:
                    pe.wait_ge(S["e_act_kept"], a.freed())
                    pe.wait_ge(S["e_acted"], a.done())
                    for i in range(2):
                        last = nc.tensor.transpose(PS[:, 4 + a.par, i * P:i * P + P],
                                                   hact[:, a.par, 0, i * P:i * P + P], identf)
                    last.then_inc(S["e_act_turned"], 1)
                if f:
                    if f.slot == 0:
                        pe.reg_mov(four_experts, pe.value_load(texp[0:1, ds(f.quad, 1)],
                                                               min_val=0, max_val=E ** 4 - 1))
                    four = pe.snap(four_experts, min_val=0, max_val=E ** 4 - 1)
                    pe.reg_mov(expert_of[f.slot], four // E ** f.slot % E)

            walk(pe, NS, 7, sorted_step)
            pe.wait_ge(S["e_kept"], Tile(NS - 1).done())

            def context_step(stage):
                f, s = stage(1), stage(2)
                if s:
                    pe.wait_ge(S["c_put"], s.freed())
                    pe.wait_ge(S["c_dp_kept"], s.done())
                    pe.wait_ge(S["c_picked"], s.done())
                    nc.tensor.matmul(PS[:, 2 + s.par, 0:D], pick[:, s.par, :], dp[:, s.par, :], start=True, stop=True)\
                        .then_inc(S["c_placed"], 1)
                if f:
                    pe.wait_ge(S["c_dp_kept"], f.freed())
                    pe.wait_ge(S["c_hp_ready"], f.done())
                    nc.tensor.matmul(PS[:, f.par, 0:D], decay, hp[:, f.par, :], start=True, stop=True)\
                        .then_inc(S["c_depooled"], 1)

            walk(pe, NT, 3, context_step)
            pe.wait_ge(S["c_put"], Tile(NT - 1).done())
            pe.wait_ge(bias_ready, 1)

            def last_step(stage):
                f, s, b, r, m, y = (stage(i) for i in (1, 2, 5, 6, 7, 8))
                if r:
                    pe.wait_ge(S["l_lg"], r.freed(back=1))
                    pe.wait_ge(S["l_xnT_kept"], r.done())
                    nc.tensor.matmul(PS[:, 3, 0:64], xnT4[:, r.slot, :], rw1[:], start=True, stop=True)\
                        .then_inc(S["l_routed"], 1)
                if m:
                    pe.wait_ge(S["l_masked"], m.freed(back=1))
                    pe.wait_ge(S["l_mask_ready"], m.done())
                    for e in range(E):
                        last = nc.tensor.matmul(PS[:, 4 + e // 4, e % 4 * P:e % 4 * P + P],
                                                mask1[:, m.par, 1, e:e + 1].to_broadcast([P, P]), ident16[:],
                                                start=True, stop=True)
                    last.then_inc(S["l_spread"], 1)
                if f:
                    pe.wait_ge(S["l_hnT_kept"], f.freed(back=1))
                    if m:
                        pe.wait_ge(S["l_mask_kept"], m.freed(back=1))
                    pe.wait_ge(S["l_hn_ready"], f.done())
                    nc.tensor.transpose(PS[:, 0, 0:P], hn[:, f.par, :], identf).then_inc(S["l_hnT_done"], 1)
                if s:
                    pe.wait_ge(S["l_x3"], s.freed(back=1))
                    pe.wait_ge(S["l_hnT_kept"], s.done())
                    nc.tensor.matmul(PS[:, 1, 0:D], hnT[:, s.par, :], winT[:], start=True, stop=True)\
                        .then_inc(S["l_mixed"], 1)
                if b:
                    pe.wait_ge(S["l_xnT_kept"], b.freed(back=1))
                    pe.wait_ge(S["l_normed"], b.done())
                    nc.tensor.transpose(PS[:, 2, 0:P], xn[:, b.par, :], identf).then_inc(S["l_xnT_done"], 1)
                if y:
                    pe.wait_ge(S["l_out_ready"], y.freed())
                    pe.wait_ge(S["l_masked"], y.done())
                    for e in range(E):
                        nc.tensor.matmul(PS[:, 6 + y.par, 0:D], z[:, y.par, e, :], w1[:, e * D:e * D + D],
                                         start=(e == 0), stop=False)
                if m:
                    pe.wait_ge(*((S["l_hnT_kept"], f.done()) if f else (S["l_mask_kept"], m.freed(back=1))))
                    nc.tensor.transpose(bank16(0)[0:E, 512:512 + P], mask1[:, m.par, 1, :], ident16[:])\
                        .then_inc(S["l_mask_turned"], 1)
                if y:
                    pe.wait_ge(S["l_mask_kept"], y.done())
                    nc.tensor.matmul(PS[:, 6 + y.par, 0:D], mask1T[:, y.par, :], b1[:], start=False, stop=True)\
                        .then_inc(S["l_summed"], 1)

            walk(pe, NT, 9, last_step)


def constants(ns):
    p = np.arange(P)
    same = p[:, None] // 64 == p[None, :] // 64
    ago = p[None, :] - p[:, None]
    keep = np.exp(np.float64(-1e-3))
    fade = -np.expm1(np.float64(-1e-3))
    decay = np.where(same & (ago >= 0), keep * fade ** np.maximum(ago, 0), 0.0)
    rows = (np.arange(8), np.arange(8) - 8, np.arange(ns) * P)
    return np.concatenate([np.eye(P), p[:, None] < p[None, :], np.ones((P, P)), decay]
                          + [np.broadcast_to(r, (P, r.size)) for r in rows]
                          + [p[:, None] % 64, np.broadcast_to(np.arange(64), (P, 64))], 1).astype(np.float32)


def kernel(**inputs):
    import numpy as _np
    import concourse.bacc as _bacc
    from concourse import mybir as _mybir
    from concourse.bass_utils import run_bass_kernel_spmd as _run

    i = {k: _np.asarray(v) for k, v in inputs.items()}
    nt, ns = 32, 40

    def pad64(a):
        return _np.pad(a, ((0, 0), (0, 64 - a.shape[1])))

    def by_tile(a):
        return a.reshape(nt, 128, -1).transpose(1, 0, 2).reshape(128, -1)

    ctx = i["ctx_2048"].reshape(nt, 2, 64, 256)
    arrays = {
        "x": by_tile(i["x"]),
        "ctx_k": by_tile(ctx[..., :128]),
        "ctx_v_swapped": by_tile(ctx[:, ::-1, :, 128:]),
        "consts": constants(ns),
        "gates": _np.broadcast_to(_np.concatenate([i["g_xattn"], i["g_ffn"]]), (128, 4)),
        "w_qkv": i["L0_xattn_w_qkv"].T,
        "w_proj": i["L0_xattn_w_proj"].T,
        "b_proj": _np.broadcast_to(i["L0_xattn_b_proj"], (128, 128)),
        "gate_w": pad64(i["L0_ffn_gate_w"]),
        "sh_gate_up": _np.concatenate([i["L0_ffn_sh_gate"], i["L0_ffn_sh_up"]], 1),
        "sh_down": i["L0_ffn_sh_down"].reshape(2, 128, 128).transpose(1, 0, 2).reshape(128, 256),
        "rt_gate_up": _np.concatenate([i["L0_ffn_rt_gate"], i["L0_ffn_rt_up"]], 2).transpose(1, 0, 2).reshape(128, -1),
        "rt_down": i["L0_ffn_rt_down"].reshape(8, 2, 128, 128).transpose(2, 0, 1, 3).reshape(128, -1),
        "patch_mask": i["mask_BxS2_if0"],
        "w_in": i["L1_xattn_W_in"].T,
        "b_in": _np.broadcast_to(i["L1_xattn_b_in"], (128, 128)),
        "g_res": i["L1_xattn_g_res"].reshape(128, 1),
        "g_init": _np.broadcast_to(i["L1_xattn_g_init"][:128], (128, 128)),
        "router_w": pad64(i["L1_ffn_router_w"].T),
        "router_b": _np.broadcast_to(i["L1_ffn_router_b"], (128, 8)),
        "expert_w": i["L1_ffn_expert_w"].transpose(2, 0, 1).reshape(128, -1),
        "expert_b": i["L1_ffn_expert_b"],
    }
    arrays = {f"in_{k}_dram": _np.ascontiguousarray(v) for k, v in arrays.items()}
    nc = _bacc.Bacc("TRN2", target_bir_lowering=False, num_devices=1)
    args = [nc.dram_tensor(k, v.shape, _mybir.dt.from_np(v.dtype), kind="ExternalInput").ap() for k, v in arrays.items()]
    args.append(nc.dram_tensor("out_dram", (128, nt * 128), _mybir.dt.float32, kind="ExternalOutput").ap())
    flamingo_gated_two_layers(nc, *args)
    r = _run(nc, [arrays], core_ids=[0])
    return r.results[0]["out_dram"].reshape(128, nt, 128).transpose(1, 0, 2).reshape(64, 64, 128)
```

```python
from contextlib import ExitStack

import numpy as np

import concourse.bass as bass
from concourse import mybir

F32 = mybir.dt.float32
F16 = mybir.dt.float16
BF16 = mybir.dt.bfloat16
I32 = mybir.dt.int32
U32 = mybir.dt.uint32
ALU = mybir.AluOpType
ACT = mybir.ActivationFunctionType
AX = mybir.AxisListType
ds = bass.ds

P = 128
CREDIT = 2
TURN = 4
EPS = 1e-5


class Tile:

    def __init__(self, n, turn=None, unroll=TURN):
        self.n, self.turn = n, turn
        self.t = n if turn is None else n + unroll * turn
        self.pair = n // 2 if turn is None else n // 2 + unroll // 2 * turn
        self.quad = n // 4 if turn is None else n // 4 + turn
        self.par, self.slot = n % 2, n % 4

    def cols(self, width):
        return ds(self.t * width, width)

    def done(self, per_tile=1, event=0):
        return (self.t + CREDIT) * per_tile + event + 1

    def freed(self, per_tile=1, event=0, back=None):
        back = CREDIT * per_tile if back is None else back
        return (self.t + CREDIT) * per_tile + event + 1 - back


def walk(eng, tiles, depth, step, before_loop=None, unroll=TURN):
    first = -(-depth // unroll) * unroll
    assert tiles % unroll == 0 and tiles > first

    def peeled(s):
        step(lambda lag: Tile(s - lag) if 0 <= s - lag < tiles else None)

    for s in range(first):
        peeled(s)
    if before_loop:
        before_loop()
    with eng.Fori(0, (tiles - first) // unroll) as turn:
        for k in range(unroll):
            step(lambda lag: Tile(first + k - lag, turn, unroll))
    for s in range(tiles, tiles + depth):
        peeled(s)


def flamingo_gated_two_layers(nc, x, ctx_k, ctx_v_swapped, consts, gates, w_qkv, w_proj, b_proj, gate_w,
                              sh_gate_up, sh_down, rt_gate_up, rt_down, patch_mask, w_in, b_in, g_res, g_init,
                              router_w, router_b, expert_w, expert_b, out):
    NT = x.shape[1] // P
    D = P
    H, HD = 16, 8
    HG, G = 4, 4
    SEQ = 64
    E = 8
    FF = 256
    PAIRS = P // SEQ
    NS = (NT * P + E * (P - 1)) // P
    NS += -NS % TURN
    CT = 4
    NC = NT // CT
    LAGS = 6

    with ExitStack() as ctx:
        def sb(name, shape, dt=F32):
            return ctx.enter_context(nc.sbuf_tensor(name, shape, dt))

        def sem(name):
            return ctx.enter_context(nc.semaphore(name))

        X = sb("X", [P, NT * D])
        CK = sb("CK", [P, NT * D])
        CV = sb("CV", [P, NT * D])
        VALL = sb("VALL", [P, NT * D])
        CW = [P, P, P, P, E, E, NS, 1, SEQ]
        CO = [sum(CW[:i]) for i in range(len(CW))]
        cst = sb("cst", [P, sum(CW)])
        identf, upper, ones, decay, exp_no, exp_no8, tile_start, patch_no, place_no = (
            cst[:, o:o + w] for o, w in zip(CO, CW))
        ident16 = sb("ident16", [P, P], F16)
        halfneg = sb("halfneg", [P, 1])
        epsc = sb("epsc", [P, 1])
        gate = sb("gate", [P, 4])
        tgate = sb("tgate", [P, 4])
        wqkv = sb("wqkv", [P, 3 * D])
        wproj = sb("wproj", [P, D])
        bproj = sb("bproj", [P, D])
        st = sb("st", [P, 2, 6])
        mv = sb("mv", [P, 2, 2])
        ve = sb("ve", [P, 2])
        rstd = sb("rstd", [P, 2])
        xn = sb("xn", [P, 2, D])
        xnT = sb("xnT", [P, 2, P])
        stack = sb("stack", [P, 2, 3, H, 32], F16)
        qc = sb("qc", [P, G, P], F16)
        kt = sb("kt", [P, 4, 2, G, P], F16)
        vp = sb("vp", [P, 2, 2, H, 32])
        arena = sb("arena", [P, NS * D])
        negm = sb("negm", [P, 2, HG, G], F16)
        mT = sb("mT", [H, 2, P], F16)
        qbd = arena[:, 0:4 * G * HG * P // 2].bitcast(F16).rearrange("p (s g h t) -> p s g h t", s=4, g=G, h=HG)
        pexp = sb("pexp", [P, 4, 512])
        oS = sb("oS", [P, 2, 512])
        rden = sb("rden", [P, 2, H])
        on = sb("on", [P, 2, D])
        onT = sb("onT", [P, 2, P])

        spare = stack.rearrange("p s w h c -> p (s w h c)").bitcast(F32)
        def twin(k):
            return spare[:, k * 2 * D:(k + 1) * 2 * D].rearrange("p (s d) -> p s d", s=2)

        XN2 = VALL
        XNT = sb("XNT", [P, NT * P])
        gatew = sb("gatew", [P, 64])
        LG = sb("LG", [P, NT, E])
        top = sb("top", [P, NT])
        score = sb("score", [P, NT])
        isel = spare[:, 800:800 + NT * E].rearrange("p (t e) -> p t e", e=E)
        first8 = sb("first8", [P, NT])
        onehot = sb("onehot", [P, E, NT], BF16)
        upper16 = sb("upper16", [P, P], BF16)
        ones16 = sb("ones16", [P, P], BF16)
        tot = spare[:, 1056:1056 + NT * E].rearrange("p (e t) -> p e t", e=E)
        run = on.rearrange("p s d -> p (s d)").rearrange("p (e t) -> p e t", e=E)
        onesf = sb("onesf", [P, E * NT])
        cnt = sb("cnt", [P, 6, E])
        cnti = sb("cnti", [P, 2, E], I32)
        posf = sb("posf", [P, NT])
        posu = sb("posu", [P, NT], U32)
        tcmp = spare[:, 512:512 + NS * (E - 1)].rearrange("p (s e) -> p s e", e=E - 1)
        texpf = sb("texpf", [P, NS])
        texp = sb("texp", [P, NS // 4], I32)
        shgu = sb("shgu", [P, 2 * FF])
        shd = sb("shd", [P, FF])
        rgu = sb("rgu", [P, E * 2 * FF])
        rdn = sb("rdn", [P, E * FF])
        sg = oS
        hact = pexp.rearrange("p (c i) t -> p c i t", c=2)
        zeros = sb("zeros", [P, 8 * D])
        xs = sb("xs", [P, 4, D])
        xsT = sb("xsT", [P, 2, P])
        act2T = spare[:, 0:2 * FF].rearrange("p (s f) -> p s f", s=2)
        YS = arena
        ssk = sb("ssk", [P, NT])
        ssv = sb("ssv", [P, 2, NT])
        sqj = sb("sqj", [P, 2, D], BF16)
        crms = sb("crms", [P, NT])
        pm_i = sb("pm_i", [SEQ, SEQ], I32)
        ends16 = sb("ends16", [SEQ, 2, SEQ], BF16)
        pm = sb("pm", [SEQ, 6, SEQ])
        pcmp = kt[0:SEQ].rearrange("p s b g t -> p (s b g t)").bitcast(BF16).rearrange("p (a b) -> p a b", a=SEQ)
        winT = sb("winT", [P, D])
        binB = sb("binB", [P, D])
        gres = sb("gres", [P, 1])
        ginit = sb("ginit", [P, D])
        rw1 = sb("rw1", [P, 64])
        rb1 = sb("rb1", [P, E])
        w1 = sb("w1", [P, E * D])
        b1 = sb("b1", [E, D])
        mvr = sb("mvr", [P, NT])
        ve2 = sb("ve2", [P, 2])
        xr = sb("xr", [P, 2, D])
        xrT = sb("xrT", [P, 2, P])
        str_ = sb("str_", [P, 2, 6])
        rstdr = sb("rstdr", [P, NT])
        mvl = sb("mvl", [P, NT, 2])
        mv2 = sb("mv2", [P, 2, 2])
        rchain = sb("rchain", [P, 5, NT])
        rr = sb("rr", [P, NT])
        mrr = sb("mrr", [P, NT])
        xnT4 = sb("xnT4", [P, 4, P])
        hn, hnT = on, onT
        hp, dp, pick = twin(2), twin(3), twin(4)
        DP = CV
        lg1 = sb("lg1", [P, 2, E])
        mx8 = sb("mx8", [P, 2, 8])
        ix8 = sb("ix8", [P, 2, 8], U32)
        ixf = sb("ixf", [P, 2, 2])
        mask1 = sb("mask1", [P, 2, 2, E], F16)
        mask1T = sb("mask1T", [E, 2, P])
        z = vp.rearrange("p s b h c -> p s (b h c)").rearrange("p s (e t) -> p s e t", e=E)

        sorted_x = nc.dram_tensor("sorted_x", (NS * P, D), F32).ap()
        sorted_y = nc.dram_tensor("sorted_y", (NS * P, D), F32).ap()
        plugs = nc.dram_tensor("plugs", (NT * PAIRS, SEQ), F32).ap()

        PS = ctx.enter_context(nc.psum_tensor("PS", [P, 8, 512], F32))

        def hi_twice(par, w):
            at = stack[:, par, w, :, 0:16 if w == 0 else 32].rearrange("p h (c d) -> p h c d", c=2)
            return at[:, :, :, 0:8]

        def twice_over(src):
            return src.unsqueeze(2).to_broadcast([P, H, 2, HD])

        def bank16(b):
            return PS[:, b, :].bitcast(F16)

        TILE_CHUNKS = [(0, 2), (2, 8), (8, NT)]
        x_in = [sem(f"x_in{c}") for c in range(3)]
        ck_in = [sem(f"ck_in{c}") for c in range(3)]
        cv_in = [sem(f"cv_in{c}") for c in range(3)]
        consts_in = sem("consts_in")
        weights_in = sem("weights_in")
        weights_ready = sem("weights_ready")
        pool_consts = sem("pool_consts")
        gates_ready = sem("gates_ready")
        names = ("stats moments normed var_eps rstd_ready bias_added hi_ready v_kept lo_ready "
                 "ctx_hi v_half ctx_stacked xnT_done qkv_done xnT_kept qk_turned ctx_turned q_kept q_spread "
                 "k_kept ctx_kept scored maxed max_turned max_kept scored_t exped v_spread averaged "
                 "o_kept o_turned recip_ready o_normed on_turned on_kept projected x_updated")
        S = {n: sem("a_" + n) for n in names.split()}
        shift_placed = [sem("a_shift_placed0"), sem("a_shift_placed1")]
        for n in "stats moments var_eps copied normed kept xnT_done xnT_kept routed logits".split():
            S["r_" + n] = sem("r_" + n)
        more_in = sem("more_in")
        mask_in = sem("mask_in")
        ends_here = sem("ends_here")
        ends_step = sem("ends_step")
        late_in = sem("late_in")
        late_ready = sem("late_ready")
        bias_ready = sem("bias_ready")
        zeroed = sem("zeroed")
        sort_step = sem("sort_step")
        score_ready = sem("score_ready")
        ranked = sem("ranked")
        texp_ready = sem("texp_ready")
        scaled = sem("scaled")
        places_known = sem("places_known")
        scattered = sem("scattered")
        for n in "gated lifted acted down added squared".split():
            S["h_" + n] = sem("h_" + n)
        xs_in = [sem(f"xs_in{c}") for c in range(4)]
        for n in "turned turned_kept lifted gated acted act_turned act_kept down kept".split():
            S["e_" + n] = sem("e_" + n)
        stored = sem("stored")
        y_in = [sem(f"y_in{c}") for c in range(NT // 4)]
        swapped = sem("swapped")
        swap_in = sem("swap_in")
        crms_step = sem("crms_step")
        plug_step = sem("plug_step")
        plug_out = sem("plug_out")
        plug_in = sem("plug_in")
        places_cleared = sem("places_cleared")
        rms_step = sem("rms_step")
        rms_ready = sem("rms_ready")
        mean_ready = sem("mean_ready")
        for n in "hp_ready depooled dp_kept picked placed put".split():
            S["c_" + n] = sem("c_" + n)
        for n in ("y_in x2 stats moments copied hn_ready hnT_done hnT_kept added mixed x3 stats2 moments2 var_eps rstd "
                  "normed xnT_done xnT_kept routed lg m8 i8 ixf mk0 mask_ready spread mask_turned mask_kept masked "
                  "summed out_ready").split():
            S["l_" + n] = sem("l_" + n)
        out_done = sem("out_done")

        block = ctx.enter_context(nc.Block())

        def arrived(eng, sems, tile):
            if tile is not None and tile.turn is None:
                for c, (lo, _) in enumerate(TILE_CHUNKS):
                    if tile.n == lo:
                        eng.wait_ge(sems[c], 16)
                        eng.nop(nofuse=True)

        def credit(eng, *entries):
            for name, per_tile in entries:
                eng.sem_inc(S[name], CREDIT * per_tile)

        @block.sync
        def _(sp):
            sp.dma_start(X[:, 0:2 * D], x[:, 0:2 * D]).then_inc(x_in[0], 16)
            sp.dma_start(cst[:], consts).then_inc(consts_in, 16)
            sp.dma_start(CK[:, 0:2 * D], ctx_k[:, 0:2 * D]).then_inc(ck_in[0], 16)
            sp.dma_start(wqkv[:], w_qkv).then_inc(weights_in, 16)
            sp.dma_start(gate[:], gates).then_inc(consts_in, 16)
            sp.dma_start(pm_i[:], patch_mask).then_inc(mask_in, 16)
            sp.dma_start(wproj[:], w_proj).then_inc(weights_in, 16)
            sp.dma_start(bproj[:], b_proj).then_inc(weights_in, 16)
            sp.dma_start(gatew[:], gate_w).then_inc(weights_in, 16)
            for c in range(3):
                lo, hi = TILE_CHUNKS[c]
                if c:
                    sp.dma_start(X[:, lo * D:hi * D], x[:, lo * D:hi * D]).then_inc(x_in[c], 16)
                    sp.dma_start(CK[:, lo * D:hi * D], ctx_k[:, lo * D:hi * D]).then_inc(ck_in[c], 16)
                sp.dma_start(CV[:, lo * D:hi * D], ctx_v_swapped[:, lo * D:hi * D]).then_inc(cv_in[c], 16)
            for dst, src in ((shgu, sh_gate_up),):
                sp.dma_start(dst[:], src).then_inc(more_in, 16)

            def step(stage):
                a = stage(3)
                if a:
                    sp.wait_ge(S["max_kept"], a.done())
                    for hg in range(HG):
                        sp.dma_start(qbd[32 * hg + 24:32 * hg + 25, a.slot, :, hg, :],
                                     mT[HG * hg:HG * hg + G, a.par, :]).then_inc(shift_placed[a.par], 16)

            walk(sp, NT, LAGS, step)
            credit(sp, ("l_y_in", 1))
            for dst, src in ((shd, sh_down), (rgu, rt_gate_up), (rdn, rt_down), (winT, w_in), (binB, b_in),
                             (gres, g_res), (ginit, g_init), (rw1, router_w), (rb1, router_b), (w1, expert_w),
                             (b1, expert_b)):
                sp.dma_start(dst[:], src).then_inc(late_in, 16)
            sp.wait_ge(pool_consts, 2)
            sx = sorted_x.rearrange("(c p r) d -> c p (r d)", p=P, r=8)
            for c in range(NS // 8):
                sp.dma_start(sx[c], zeros[:]).then_inc(zeroed, 16)
            sp.wait_ge(scattered, 16 * NT)

            def load_and_store(stage):
                l, d = stage(0), stage(7)
                if l:
                    if not (l.turn is None and l.n < 4):
                        sp.wait_ge(S["e_turned"], l.freed(back=4))
                    sp.dma_start(xs[:, l.slot, :], sorted_x[ds(l.t * P, P)]).then_inc(xs_in[l.slot], 16)
                if d:
                    sp.wait_ge(S["e_kept"], d.done())
                    sp.dma_start(sorted_y[ds(d.t * P, P)], YS[:, d.cols(D)]).then_inc(stored, 16)

            walk(sp, NS, 7, load_and_store)
            for c in range(NT // 4):
                sp.wait_ge(y_in[c], 64)
                sp.sem_inc(S["l_y_in"], 4)

            def store_out(stage):
                o = stage(9)
                if o:
                    sp.wait_ge(S["l_out_ready"], o.done())
                    sp.dma_start(out[:, o.cols(D)], X[:, o.cols(D)]).then_inc(out_done, 16)

            walk(sp, NT, 9, store_out)
            sp.wait_ge(out_done, 16 * NT)

        @block.gpsimd
        def _(pool):
            credit(pool, ("rstd_ready", 1), ("var_eps", 1), ("bias_added", 1), ("v_spread", 1),
                   ("v_half", 1), ("r_copied", 1), ("r_var_eps", 1),
                   ("r_kept", 1))
            pool.memset(halfneg[:], -0.5)
            pool.memset(epsc[:], EPS)
            pool.memset(stack[:], 0.0)
            pool.memset(vp[:], 1.0).then_inc(pool_consts, 1)
            pool.wait_ge(pool_consts, 1)
            pool.memset(stack[:, :, 1:3, :, 24:25], 1.0)
            pool.memset(zeros[:], 0.0).then_inc(pool_consts, 1)
            pool.wait_ge(pool_consts, 2)

            def step(stage):
                l, f, a, m, c = (stage(i) for i in (0, 1, 4, 7, 9))
                if m:
                    pool.wait_ge(S["r_moments"], m.done())
                    pool.tensor_tensor(ve2[:, m.par:m.par + 1], mv2[:, m.par, 1:2], epsc[:], ALU.add)\
                        .then_inc(S["r_var_eps"], 1)
                    pool.tensor_copy(mvr[:, ds(m.t, 1)], mv2[:, m.par, 0:1])
                    pool.wait_ge(S["r_var_eps"], m.done())
                    pool.tensor_tensor(rstdr[:, ds(m.t, 1)], ve2[:, m.par:m.par + 1], halfneg[:], ALU.pow)\
                        .then_inc(S["r_copied"], 1)
                if a:
                    arrived(pool, cv_in, a)
                    pool.wait_ge(S["v_kept"], a.done())
                    pool.wait_ge(S["averaged"], a.freed(4, 3))
                    if f:
                        pool.wait_ge(S["bias_added"], f.freed(back=1))
                    for half in range(2):
                        if half:
                            pool.wait_ge(S["v_half"], a.done())
                        rows = slice(64 * half, 64 * half + 64)
                        pool.tensor_copy(vp[rows, a.par, half, :, 0:HD],
                                         VALL[rows, a.cols(D)].rearrange("p (h d) -> p h d", h=H))
                        pool.tensor_copy(vp[rows, a.par, 1 - half, :, 0:HD],
                                         CV[rows, a.cols(D)].rearrange("p (h d) -> p h d", h=H))\
                            .then_inc(S["v_spread" if half else "v_half"], 1)
                    pool.wait_ge(S["v_spread"], a.done())
                if l:
                    pool.wait_ge(S["moments"], l.done())
                    pool.tensor_tensor(ve[:, l.par:l.par + 1], mv[:, l.par, 1:2], epsc[:], ALU.add)\
                        .then_inc(S["var_eps"], 1)
                    pool.wait_ge(S["var_eps"], l.done())
                    pool.tensor_tensor(rstd[:, l.par:l.par + 1], ve[:, l.par:l.par + 1], halfneg[:], ALU.pow)\
                        .then_inc(S["rstd_ready"], 1)
                if f:
                    pool.wait_ge(S["normed"], f.done())
                    if f.turn is None and f.n == 0:
                        pool.wait_ge(weights_ready, 3)
                    xt = X[:, f.cols(D)]
                    pool.tensor_tensor(xt, xt, bproj[:], ALU.add).then_inc(S["bias_added"], 1)
                if c:
                    pool.wait_ge(S["r_normed"], c.done())
                    pool.tensor_copy(XN2[:, c.cols(D)], xr[:, c.par, :]).then_inc(S["r_kept"], 1)

            def loads():
                pool.wait_ge(cv_in[2], 16)

            walk(pool, NT, 9, step, loads)

            pool.wait_ge(late_in, 16 * 11)
            pool.wait_ge(gates_ready, 1)
            for w, k in ((shd, 2), (rdn, 2), (binB, 1), (ginit, 1), (w1, 3)):
                pool.tensor_scalar(w[:], w[:], tgate[:, k:k + 1], None, ALU.mult).then_inc(late_ready, 1)
            pool.tensor_scalar(winT[:], winT[:], gres[:], tgate[:, 1:2], ALU.mult, ALU.mult).then_inc(late_ready, 1)

            pool.wait_ge(zeroed, 16 * (NS // 8))
            pool.wait_ge(places_known, 1)
            for t in range(NT):
                if t % 8 == 0:
                    pool.wait_ge(scaled, t // 8 + 1)
                pool.indirect_dma_start(out=sorted_x, out_offset=bass.IndirectOffsetOnAxis(ap=posu[:, t:t + 1], axis=0),
                                        in_=XN2[:, t * D:t * D + D], in_offset=None).then_inc(scattered, 16)
            pool.wait_ge(S["h_lifted"], Tile(NC - 1).done(2, 1))
            pool.memset(XNT[:], -1.0).then_inc(places_cleared, 1)

            pool.wait_ge(S["h_squared"], Tile(NC - 1).done(2 * CT, 2 * CT - 1))
            for q in range(PAIRS):
                pool.dma_start(ssv[SEQ * q:SEQ * q + SEQ, 1, :], ssv[SEQ * (1 - q):SEQ * (2 - q), 0, :])\
                    .then_inc(swap_in, 16)
            pool.wait_ge(swap_in, 32)
            pool.tensor_tensor(crms[:], ssk[:], ssv[:, 1, :], ALU.add).then_inc(crms_step, 1)
            pool.wait_ge(crms_step, 1)
            pool.tensor_scalar(crms[:], crms[:], 0.5 / D, EPS, ALU.mult, ALU.add).then_inc(crms_step, 1)
            pool.wait_ge(crms_step, 2)
            pool.tensor_tensor(crms[:], crms[:], halfneg[:].to_broadcast([P, NT]), ALU.pow).then_inc(crms_step, 1)
            plugged = [0]

            def next_plug(ins):
                plugged[0] += 1
                ins.then_inc(plug_step, 1)
                pool.wait_ge(plug_step, plugged[0])

            pool.wait_ge(ends_here, 7)
            w, old, new = 1, 3, 4
            while w < SEQ:
                pool.tensor_copy(pm[:, new, 0:w], pm[:, old, 0:w])
                next_plug(pool.tensor_tensor(pm[:, new, w:], pm[:, old, w:], pm[:, old, 0:SEQ - w], ALU.add))
                w, old, new = 2 * w, new, old
            next_plug(pool.tensor_scalar(pm[:, 5, :], pm[:, old, :], -1.0, 0.0, ALU.add, ALU.max))
            next_plug(pool.tensor_scalar(pm[:, 5, :], pm[:, 5, :], float(SEQ - 1), None, ALU.min))
            pool.wait_ge(places_cleared, 1)
            pool.wait_ge(plug_step, plugged[0])
            pool.dma_start(plugs, pm[:, 5, :]).then_inc(plug_out, 16)
            pool.wait_ge(plug_out, 16)
            for q in range(PAIRS):
                rows = slice(SEQ * q, SEQ * q + SEQ)
                pool.dma_start(XNT[rows].rearrange("p (t s) -> p t s", t=NT)[:, :, SEQ * q:SEQ * q + SEQ],
                               plugs.rearrange("(t q) s -> q t s", q=PAIRS)[q:q + 1].to_broadcast([SEQ, NT, SEQ]))\
                    .then_inc(plug_in, 16)
            pool.wait_ge(stored, 16 * NS)
            for t in range(NT):
                pool.indirect_dma_start(out=XN2[:, t * D:t * D + D], out_offset=None, in_=sorted_y,
                                        in_offset=bass.IndirectOffsetOnAxis(ap=posu[:, t:t + 1], axis=0))\
                    .then_inc(y_in[t // 4], 16)

            credit(pool, ("l_var_eps", 1), ("l_rstd", 1), ("l_added", 1))

            def last_step(stage):
                f, a = stage(1), stage(3)
                if f:
                    pool.wait_ge(S["l_hn_ready"], f.done())
                    if f.turn is None and f.n == 0:
                        pool.wait_ge(S["c_put"], Tile(NT - 1).done())
                    pool.tensor_tensor(X[:, f.cols(D)], X[:, f.cols(D)], DP[:, f.cols(D)], ALU.add)\
                        .then_inc(S["l_added"], 1)
                if a:
                    pool.wait_ge(S["l_moments2"], a.done())
                    pool.tensor_tensor(ve[:, a.par:a.par + 1], mv2[:, a.par, 1:2], epsc[:], ALU.add)\
                        .then_inc(S["l_var_eps"], 1)
                    pool.wait_ge(S["l_var_eps"], a.done())
                    pool.tensor_tensor(rstd[:, a.par:a.par + 1], ve[:, a.par:a.par + 1], halfneg[:], ALU.pow)\
                        .then_inc(S["l_rstd"], 1)

            walk(pool, NT, 9, last_step)

        @block.scalar
        def _(act):
            credit(act, ("xnT_kept", 1), ("exped", 4), ("on_kept", 1), ("hi_ready", 1), ("v_kept", 1),
                   ("max_kept", 1), ("o_kept", 1), ("ctx_hi", 1), ("q_kept", 1), ("ctx_kept", 1),
                   ("r_xnT_kept", 1))
            act.wait_ge(consts_in, 32)
            nc.scalar.activation(tgate[:], gate[:], ACT.Tanh).then_inc(gates_ready, 1)

            def ctx_hi(f):
                arrived(act, ck_in, f)
                act.wait_ge(S["ctx_turned"], f.freed())
                nc.scalar.copy(hi_twice(f.par, 2), twice_over(CK[:, f.cols(D)].rearrange("p (h d) -> p h d", h=H)))\
                    .then_inc(S["ctx_hi"], 1)

            def exp_chunk(b, j):
                act.wait_ge(S["scored_t"], b.done(4, j))
                act.wait_ge(S["averaged"], b.freed(4, j, back=4))
                nc.scalar.activation(pexp[:, j, :], PS[:, 2 + j % 2, :], ACT.Exp).then_inc(S["exped"], 1)

            def step(stage):
                l, f, s, w, b, n, c = (stage(i) for i in (0, 1, 2, 4, 5, 7, 9))
                if n:
                    act.wait_ge(S["projected"], n.freed())
                    act.wait_ge(S["on_turned"], n.done())
                    nc.scalar.copy(onT[:, n.par, :], PS[:, 6, 0:P]).then_inc(S["on_kept"], 1)
                if s:
                    act.wait_ge(S["q_spread"], s.freed(back=1))
                    act.wait_ge(S["qk_turned"], s.done())
                    nc.scalar.copy(qc[:], bank16(5)[:, 0:512].rearrange("p (g t) -> p g t", g=G))\
                        .then_inc(S["q_kept"], 1)
                if b:
                    exp_chunk(b, 0)
                if f:
                    act.wait_ge(S["qkv_done"], f.freed())
                    act.wait_ge(S["xnT_done"], f.done())
                    nc.scalar.copy(xnT[:, f.par, :], PS[:, 4, 0:P]).then_inc(S["xnT_kept"], 1)
                if b:
                    exp_chunk(b, 1)
                if s:
                    act.wait_ge(S["ctx_turned"], s.done())
                    for h in range(2):
                        src = bank16(6)[:, 0:512].rearrange("p (g t) -> p g t", g=G)[:, :, 64 * h:64 * h + 64]
                        last = nc.scalar.copy(kt[:, s.slot, h, :, 64 * (1 - h):128 - 64 * h], src)
                    last.then_inc(S["ctx_kept"], 1)
                if w:
                    if not (w.turn is None and w.n < 2):
                        act.wait_ge(shift_placed[w.par], 64 * w.pair)
                    act.wait_ge(S["max_turned"], w.done())
                    nc.scalar.copy(mT[:, w.par, :], bank16(6)[0:H, 7 * P:8 * P]).then_inc(S["max_kept"], 1)
                if f:
                    act.wait_ge(S["qk_turned"], f.freed())
                    act.wait_ge(S["qkv_done"], f.done())
                    for qk in range(2):
                        src = PS[:, 4, P * (1 + qk):P * (2 + qk)].rearrange("p (h d) -> p h d", h=H)
                        last = nc.scalar.copy(hi_twice(f.par, qk), twice_over(src))
                    last.then_inc(S["hi_ready"], 1)
                    nc.scalar.copy(VALL[:, f.cols(D)], PS[:, 4, 3 * P:4 * P]).then_inc(S["v_kept"], 1)
                if b:
                    exp_chunk(b, 2)
                if c:
                    act.wait_ge(S["r_routed"], c.freed())
                    act.wait_ge(S["r_xnT_done"], c.done())
                    nc.scalar.copy(xrT[:, c.par, :], PS[:, 6, 2 * P:3 * P])
                    nc.scalar.copy(XNT[:, c.cols(P)], PS[:, 6, 2 * P:3 * P]).then_inc(S["r_xnT_kept"], 1)
                if b:
                    exp_chunk(b, 3)
                if l:
                    if l.turn is None and l.n == 0:
                        act.wait_ge(pool_consts, 2)
                    ctx_hi(l)
                if b:
                    act.wait_ge(S["o_turned"], b.freed())
                    act.wait_ge(S["averaged"], b.done(4, 3))
                    nc.scalar.copy(oS[:, b.par, :], PS[:, 7, :]).then_inc(S["o_kept"], 1)

            walk(act, NT, 9, step, lambda: act.wait_ge(ck_in[2], 16))

            credit(act, ("h_gated", 2), ("h_squared", 2 * CT),
                   ("e_turned_kept", 1), ("e_gated", 1),
                   ("e_act_kept", 1), ("c_dp_kept", 1), ("l_copied", 1), ("l_hn_ready", 1), ("l_hnT_kept", 1), ("l_xnT_kept", 1),
                   ("l_mask_kept", 1))

            act.wait_ge(sort_step, 1)
            nc.scalar.activation(score[:], top[:], ACT.Sigmoid).then_inc(score_ready, 1)
            act.wait_ge(score_ready, 1)
            act.wait_ge(S["r_kept"], Tile(NT - 1).done())
            with act.Fori(0, NT // 8) as turn:
                for k in range(8):
                    row = XN2[:, ds((turn * 8 + k) * D, D)]
                    last = nc.scalar.activation(row, row, ACT.Copy, scale=score[:, ds(turn * 8 + k, 1)])
                last.then_inc(scaled, 1)

            def shared_step(stage):
                c = stage(0)
                if c:
                    for i in range(2):
                        act.wait_ge(S["h_lifted"], c.done(2, i))
                        act.wait_ge(S["h_acted"], c.freed(2, i, back=2))
                        nc.scalar.activation(sg[:, i, :], PS[:, 2 * i, :], ACT.Silu).then_inc(S["h_gated"], 1)
                    for q in range(CT):
                        for half, ss in ((CK, ssk[:, ds(c.t * CT + q, 1)]), (CV, ssv[:, 0, ds(c.t * CT + q, 1)])):
                            k = int(half is CV)
                            act.wait_ge(S["h_squared"], c.freed(2 * CT, 2 * q + k, back=2))
                            nc.scalar.activation(sqj[:, k, :], half[:, ds((c.t * CT + q) * D, D)], ACT.Square,
                                                 accum_out=ss).then_inc(S["h_squared"], 1)

            walk(act, NC, 1, shared_step, unroll=2)

            def sorted_step(stage):
                f, s, a = stage(2), stage(3), stage(4)
                if s:
                    act.wait_ge(S["e_acted"], s.freed())
                    act.wait_ge(S["e_lifted"], s.done())
                    nc.scalar.activation(sg[:, s.par, 0:FF], PS[:, 2 + s.par, 0:FF], ACT.Silu)\
                        .then_inc(S["e_gated"], 1)
                if f:
                    act.wait_ge(S["e_lifted"], f.freed())
                    act.wait_ge(S["e_turned"], f.done())
                    nc.scalar.copy(xsT[:, f.par, :], PS[:, f.par, 0:P]).then_inc(S["e_turned_kept"], 1)
                if a:
                    act.wait_ge(S["e_down"], a.freed())
                    act.wait_ge(S["e_act_turned"], a.done())
                    nc.scalar.copy(act2T[:, a.par, :], PS[:, 4 + a.par, 0:FF]).then_inc(S["e_act_kept"], 1)

            walk(act, NS, 7, sorted_step)

            def context_step(stage):
                f = stage(1)
                if f:
                    act.wait_ge(S["c_placed"], f.freed())
                    act.wait_ge(S["c_depooled"], f.done())
                    nc.scalar.copy(dp[:, f.par, :], PS[:, f.par, 0:D]).then_inc(S["c_dp_kept"], 1)
                s = stage(8)
                if s:
                    act.wait_ge(S["l_moments"], s.done())
                    nc.scalar.copy(mvl[:, ds(s.t, 1), :], mv[:, s.par, :].unsqueeze(1)).then_inc(S["l_copied"], 1)

            walk(act, NT, 8, context_step)
            act.wait_ge(rms_step, 1)
            nc.scalar.activation(rchain[:, 2, :], rchain[:, 1, :], ACT.Sqrt).then_inc(rms_step, 1)
            act.wait_ge(mean_ready, 1)

            def last_step(stage):
                l, f, b, m = stage(0), stage(1), stage(5), stage(7)
                if l:
                    act.wait_ge(S["l_hnT_done"], l.freed())
                    nc.scalar.activation(hn[:, l.par, :], X[:, l.cols(D)], ACT.Identity, bias=mrr[:, ds(l.t, 1)],
                                         scale=rr[:, ds(l.t, 1)]).then_inc(S["l_hn_ready"], 1)
                if f:
                    act.wait_ge(S["l_mixed"], f.freed())
                    act.wait_ge(S["l_hnT_done"], f.done())
                    nc.scalar.copy(hnT[:, f.par, :], PS[:, 0, 0:P]).then_inc(S["l_hnT_kept"], 1)
                if b:
                    if not (b.turn is None and b.n < 2):
                        act.wait_ge(S["l_masked"], b.freed(back=4))
                    act.wait_ge(S["l_xnT_done"], b.done())
                    nc.scalar.copy(xnT4[:, b.slot, :], PS[:, 2, 0:P]).then_inc(S["l_xnT_kept"], 1)
                if m:
                    act.wait_ge(S["l_summed"], m.freed())
                    act.wait_ge(S["l_mask_turned"], m.done())
                    nc.scalar.copy(mask1T[:, m.par, :], bank16(0)[0:E, 512:512 + P]).then_inc(S["l_mask_kept"], 1)

            walk(act, NT, 9, last_step)

        @block.vector
        def _(dve):
            credit(dve, ("stats", 1), ("moments", 1), ("normed", 1), ("lo_ready", 2), ("ctx_stacked", 1),
                   ("q_spread", 1), ("k_kept", 1), ("maxed", 4), ("recip_ready", 1),
                   ("o_normed", 1), ("x_updated", 1), ("r_stats", 1), ("r_moments", 1), ("r_normed", 1),
                   ("r_logits", 1))
            dve.memset(qbd, 0.0)
            dve.wait_ge(consts_in, 32)
            dve.tensor_copy(ident16[:], identf).then_inc(weights_ready, 1)
            dve.wait_ge(weights_in, 64)
            dve.tensor_scalar(wqkv[:, 0:D], wqkv[:, 0:D], float(HD) ** -0.5, None, ALU.mult)
            dve.wait_ge(gates_ready, 1)
            dve.tensor_scalar(wproj[:], wproj[:], tgate[:, 0:1], None, ALU.mult).then_inc(weights_ready, 1)
            dve.tensor_scalar(bproj[:], bproj[:], tgate[:, 0:1], None, ALU.mult).then_inc(weights_ready, 1)
            dve.wait_ge(pool_consts, 2)

            dve.wait_ge(mask_in, 16)
            dve.memset(onesf[:], 1.0).then_inc(ends_step, 1)
            dve.tensor_copy(pm[:, 0, :], pm_i[:]).then_inc(ends_step, 1)
            dve.wait_ge(ends_step, 2)
            dve.tensor_tensor_scan(pm[:, 1, :], onesf[0:SEQ, 0:SEQ], pm[:, 0, :], -1.0, ALU.mult, ALU.add)\
                .then_inc(ends_step, 1)
            dve.wait_ge(ends_step, 3)
            dve.tensor_scalar(pm[:, 2, :], pm[:, 1, :], 0.0, float(SEQ), ALU.is_lt, ALU.mult).then_inc(ends_step, 1)
            dve.wait_ge(ends_step, 4)
            dve.tensor_tensor(ends16[:, 0, :], pm[:, 1, :], pm[:, 2, :], ALU.add).then_inc(ends_step, 1)
            dve.tensor_copy(ends16[:, 1, :], place_no[0:SEQ]).then_inc(ends_step, 1)

            def max_chunk(a, j):
                dve.wait_ge(S["scored"], a.done(4, j))
                dve.tensor_reduce(negm[:, a.par, :, j], PS[:, j % 2, :].rearrange("p (h k) -> p h k", h=HG),
                                  AX.X, ALU.max, negate=True).then_inc(S["maxed"], 1)

            def step(stage):
                l, f, s, a, n, m, c, g = (stage(i) for i in (0, 1, 2, 3, 6, 7, 8, 11))
                if a:
                    max_chunk(a, 0)
                if a:
                    max_chunk(a, 1)
                if l:
                    arrived(dve, x_in, l)
                    dve.bn_stats(st[:, l.par, :], X[:, l.cols(D)]).then_inc(S["stats"], 1)
                if m:
                    dve.wait_ge(S["bias_added"], m.done())
                    dve.wait_ge(S["projected"], m.done())
                    dve.tensor_tensor(X[:, m.cols(D)], PS[:, 6, P:2 * P], X[:, m.cols(D)], ALU.add)\
                        .then_inc(S["x_updated"], 1)
                if g:
                    dve.wait_ge(S["r_routed"], g.done())
                    dve.tensor_copy(LG[:, ds(g.t, 1), :], PS[:, 6, 3 * P:3 * P + E].unsqueeze(1))\
                        .then_inc(S["r_logits"], 1)
                if m:
                    dve.wait_ge(S["x_updated"], m.done())
                    dve.nop(nofuse=True)
                    dve.bn_stats(str_[:, m.par, :], X[:, m.cols(D)]).then_inc(S["r_stats"], 1)
                if f:
                    dve.wait_ge(S["ctx_hi"], f.done())
                    dve.tensor_tensor(stack[:, f.par, 2, :, 8:16], CK[:, f.cols(D)].rearrange("p (h d) -> p h d", h=H),
                                      stack[:, f.par, 2, :, 0:8], ALU.subtract).then_inc(S["ctx_stacked"], 1)
                if m:
                    dve.wait_ge(S["r_copied"], m.freed())
                    dve.wait_ge(S["r_stats"], m.done())
                    dve.nop(nofuse=True)
                    dve.bn_aggr(mv2[:, m.par, :], str_[:, m.par, :]).then_inc(S["r_moments"], 1)
                if l:
                    dve.wait_ge(S["stats"], l.done())
                    dve.nop(nofuse=True)
                    dve.bn_aggr(mv[:, l.par, :], st[:, l.par, :]).then_inc(S["moments"], 1)
                if s:
                    dve.wait_ge(S["q_kept"], s.done())
                    for b in range(2):
                        src = bank16(5)[:, 512:1024].rearrange("p (g t) -> p g t", g=G)[:, :, 64 * b:64 * b + 64]
                        last = dve.tensor_copy(kt[:, s.slot, b, :, 64 * b:64 * b + 64], src)
                    last.then_inc(S["k_kept"], 1)
                if s:
                    for hg in range(HG):
                        rows = slice(32 * hg, 32 * hg + 32)
                        last = dve.tensor_copy(qbd[rows, s.slot, :, hg, :], qc[rows])
                    last.then_inc(S["q_spread"], 1)
                if a:
                    max_chunk(a, 2)
                if c:
                    dve.wait_ge(S["r_xnT_done"], c.freed())
                    dve.wait_ge(S["r_kept"], c.freed())
                    dve.wait_ge(S["r_copied"], c.done())
                    dve.tensor_scalar(xr[:, c.par, :], X[:, c.cols(D)], mvr[:, ds(c.t, 1)],
                                      rstdr[:, ds(c.t, 1)], ALU.subtract, ALU.mult).then_inc(S["r_normed"], 1)
                if f:
                    dve.wait_ge(S["v_kept"], f.done())
                    for w, col in ((0, 16), (1, 8)):
                        dve.tensor_tensor(stack[:, f.par, w, :, col:col + 8],
                                          PS[:, 4, P * (1 + w):P * (2 + w)].rearrange("p (h d) -> p h d", h=H),
                                          stack[:, f.par, w, :, 0:8], ALU.subtract).then_inc(S["lo_ready"], 1)
                if n:
                    dve.wait_ge(S["o_turned"], n.done())
                    o = PS[:, 5, :].rearrange("p (h w) -> p h w", h=H)
                    dve.reciprocal(rden[:, n.par, :], o[:, :, HD:HD + 1]).then_inc(S["recip_ready"], 1)
                    dve.wait_ge(S["recip_ready"], n.done())
                    dve.tensor_tensor(on[:, n.par, :].rearrange("p (h d) -> p h d", h=H), o[:, :, 0:HD],
                                      rden[:, n.par, :].unsqueeze(2).to_broadcast([P, H, HD]), ALU.mult)\
                        .then_inc(S["o_normed"], 1)
                if a:
                    max_chunk(a, 3)
                if l:
                    dve.wait_ge(S["xnT_done"], l.freed())
                    dve.wait_ge(S["rstd_ready"], l.done())
                    dve.tensor_scalar(xn[:, l.par, :], X[:, l.cols(D)], mv[:, l.par, 0:1],
                                      rstd[:, l.par:l.par + 1], ALU.subtract, ALU.mult).then_inc(S["normed"], 1)

            walk(dve, NT, 11, step, lambda: dve.wait_ge(x_in[2], 16))

            credit(dve, ("h_acted", 2), ("h_added", 1), ("e_acted", 1), ("e_kept", 1),
                   *((n, 1) for n in ("c_hp_ready c_picked c_put l_x2 l_stats l_moments l_x3 l_stats2 l_moments2 "
                                      "l_normed l_lg l_m8 l_i8 l_ixf l_mk0 l_mask_ready l_masked l_out_ready")
                     .split()))

            chained = [0]

            def then(ins):
                chained[0] += 1
                ins.then_inc(sort_step, 1)
                dve.wait_ge(sort_step, chained[0])

            def over_tiles(a):
                return a.unsqueeze(2).to_broadcast([P, E, NT])

            dve.wait_ge(S["r_logits"], Tile(NT - 1).done())
            then(dve.tensor_reduce(top[:], LG[:], AX.X, ALU.max))
            then(dve.tensor_tensor(isel[:], LG[:], top[:].unsqueeze(2).to_broadcast([P, NT, E]), ALU.is_equal))
            no8 = exp_no8.unsqueeze(1).to_broadcast([P, NT, E])
            then(dve.tensor_tensor(isel[:], isel[:], no8, ALU.mult))
            then(dve.tensor_reduce(first8[:], isel[:], AX.X, ALU.min))
            dve.tensor_copy(upper16[:], upper)
            dve.tensor_copy(ones16[:], ones)
            then(dve.tensor_tensor(onehot[:].rearrange("p e t -> p t e"),
                                   first8[:].unsqueeze(2).to_broadcast([P, NT, E]), no8, ALU.is_equal))
            dve.wait_ge(ranked, 1)
            then(dve.tensor_copy(tot[:], PS[:, 5, 0:E * NT].rearrange("p (e t) -> p e t", e=E)))
            then(dve.tensor_tensor_scan(run[:].rearrange("p e t -> p (e t)"), onesf[:],
                                        tot[:].rearrange("p e t -> p (e t)"), 0.0, ALU.mult, ALU.add))
            then(dve.tensor_reduce(cnt[:, 0, :], tot[:], AX.X, ALU.add))
            then(dve.tensor_scalar(cnti[:, 0, :], cnt[:, 0, :], float(P - 1), None, ALU.add))
            then(dve.tensor_scalar(cnti[:, 1, :], cnti[:, 0, :], 7, 7, ALU.logical_shift_right, ALU.logical_shift_left))
            then(dve.tensor_copy(cnt[:, 1, :], cnti[:, 1, :]))
            then(dve.tensor_tensor_scan(cnt[:, 2, :], onesf[:, 0:E], cnt[:, 1, :], 0.0, ALU.mult, ALU.add))
            then(dve.tensor_tensor(cnt[:, 3, :], cnt[:, 2, :], cnt[:, 1, :], ALU.subtract))
            then(dve.tensor_tensor(cnt[:, 4, :], cnt[:, 0, :], run[:, :, NT - 1], ALU.subtract))
            then(dve.tensor_tensor(cnt[:, 5, :], cnt[:, 3, :], cnt[:, 4, :], ALU.add))
            then(dve.tensor_tensor(run[:], run[:], tot[:], ALU.subtract))
            then(dve.tensor_tensor(run[:], PS[:, 4, 0:E * NT].rearrange("p (e t) -> p e t", e=E), run[:], ALU.add))
            then(dve.tensor_tensor(run[:], run[:], over_tiles(cnt[:, 5, :]), ALU.add))
            then(dve.tensor_tensor(run[:], run[:], onehot[:], ALU.mult))
            then(dve.tensor_reduce(posf[:], run[:].rearrange("p e t -> p t e"), AX.X, ALU.add))
            dve.tensor_copy(posu[:], posf[:]).then_inc(places_known, 1)
            then(dve.tensor_tensor(tcmp[:], tile_start.unsqueeze(2).to_broadcast([P, NS, E - 1]),
                                   cnt[:, 2, 0:E - 1].unsqueeze(1).to_broadcast([P, NS, E - 1]), ALU.is_ge))
            then(dve.tensor_reduce(texpf[:], tcmp[:], AX.X, ALU.add))
            digits = texpf[:].rearrange("p (s k) -> p s k", k=4)
            for k in range(1, 4):
                then(dve.scalar_tensor_tensor(out=digits[:, :, 0], in0=digits[:, :, k], scalar=float(E ** k),
                                              in1=digits[:, :, 0], op0=ALU.mult, op1=ALU.add))
            dve.tensor_copy(texp[:], digits[:, :, 0]).then_inc(texp_ready, 1)

            def shared_step(stage):
                c, d = stage(0), stage(1)
                if c:
                    for i in range(2):
                        if i == 0:
                            dve.wait_ge(S["h_down"], c.freed())
                        dve.wait_ge(S["h_gated"], c.done(2, i))
                        dve.tensor_tensor(hact[:, c.par, i, :], PS[:, 2 * i + 1, :], sg[:, i, :], ALU.mult)\
                            .then_inc(S["h_acted"], 1)
                if d:
                    dve.wait_ge(S["h_down"], d.done())
                    xc = X[:, ds(d.t * CT * D, CT * D)]
                    dve.tensor_tensor(xc, PS[:, 6 + d.par, :], xc, ALU.add).then_inc(S["h_added"], 1)

            def all_pairs():
                dve.wait_ge(ends_step, 6)
                dve.tensor_tensor(pcmp, ends16[:, 1, :].unsqueeze(2).to_broadcast([SEQ, SEQ, SEQ]),
                                  ends16[:, 0, :].unsqueeze(1).to_broadcast([SEQ, SEQ, SEQ]), ALU.is_equal)\
                    .then_inc(ends_here, 1)

            walk(dve, NC, 1, shared_step, all_pairs, unroll=2)

            w = SEQ // 2
            while w:
                dve.wait_ge(ends_here, {32: 1, 16: 2, 8: 3, 4: 4, 2: 5, 1: 6}[w])
                into = pcmp[:, :, 0:w] if w > 1 else pm[:, 3, :].unsqueeze(2)
                dve.tensor_tensor(into, pcmp[:, :, 0:w], pcmp[:, :, w:2 * w], ALU.max).then_inc(ends_here, 1)
                w //= 2
            dve.wait_ge(late_in, 16 * 11)
            dve.tensor_scalar(b1[:], b1[:], tgate[0:E, 3:4], None, ALU.mult).then_inc(bias_ready, 1)

            def sorted_step(stage):
                s, d = stage(3), stage(6)
                if d:
                    dve.wait_ge(S["e_down"], d.done())
                    dve.tensor_copy(YS[:, d.cols(D)], PS[:, 6 + d.par, 0:D]).then_inc(S["e_kept"], 1)
                if s:
                    dve.wait_ge(S["e_act_turned"], s.freed())
                    dve.wait_ge(S["e_gated"], s.done())
                    dve.tensor_tensor(hact[:, s.par, 0, 0:FF], PS[:, 2 + s.par, FF:2 * FF], sg[:, s.par, 0:FF],
                                      ALU.mult).then_inc(S["e_acted"], 1)

            walk(dve, NS, 7, sorted_step)
            dve.wait_ge(crms_step, 3)
            dve.wait_ge(plug_in, 32)
            dve.wait_ge(late_ready, 6)

            def context_step(stage):
                l, f, a, x, y, w = (stage(i) for i in (0, 1, 3, 6, 7, 8))
                if l:
                    dve.wait_ge(S["c_depooled"], l.freed())
                    dve.scalar_tensor_tensor(out=hp[:, l.par, :], in0=CK[:, l.cols(D)], scalar=crms[:, ds(l.t, 1)],
                                             in1=ginit[:], op0=ALU.mult, op1=ALU.mult).then_inc(S["c_hp_ready"], 1)
                if f:
                    dve.wait_ge(S["c_placed"], f.freed())
                    dve.tensor_scalar(pick[:, f.par, :], XNT[:, f.cols(P)], patch_no, None, ALU.is_equal)\
                        .then_inc(S["c_picked"], 1)
                if a:
                    dve.wait_ge(S["c_placed"], a.done())
                    dve.tensor_tensor(DP[:, a.cols(D)], PS[:, 2 + a.par, 0:D], binB[:], ALU.add)\
                        .then_inc(S["c_put"], 1)
                if x:
                    dve.wait_ge(S["l_y_in"], x.done())
                    dve.tensor_tensor(X[:, x.cols(D)], X[:, x.cols(D)], XN2[:, x.cols(D)], ALU.add)\
                        .then_inc(S["l_x2"], 1)
                if w:
                    dve.wait_ge(S["l_copied"], w.freed())
                    dve.wait_ge(S["l_stats"], w.done())
                    dve.nop(nofuse=True)
                    dve.bn_aggr(mv[:, w.par, :], st[:, w.par, :]).then_inc(S["l_moments"], 1)
                if y:
                    dve.wait_ge(S["l_x2"], y.done())
                    dve.nop(nofuse=True)
                    dve.bn_stats(st[:, y.par, :], X[:, y.cols(D)]).then_inc(S["l_stats"], 1)

            walk(dve, NT, 8, context_step)
            dve.wait_ge(S["l_copied"], Tile(NT - 1).done())
            rooted = [0]

            def root_step(ins):
                rooted[0] += 1
                ins.then_inc(rms_ready, 1)
                dve.wait_ge(rms_ready, rooted[0])

            v, root, r0, r1 = (rchain[:, k, :] for k in (1, 2, 3, 4))
            root_step(dve.tensor_scalar(rchain[:, 0, :], mvl[:, :, 1], EPS, EPS, ALU.add, ALU.mult))
            dve.tensor_tensor(v, rchain[:, 0, :], mvl[:, :, 1], ALU.add).then_inc(rms_step, 1)
            dve.wait_ge(rms_step, 2)
            root_step(dve.reciprocal(r0, root))
            root_step(dve.tensor_tensor(r1, r0, r0, ALU.mult))
            root_step(dve.tensor_tensor(r1, r1, v, ALU.mult))
            root_step(dve.tensor_scalar(r1, r1, -0.5, 1.5, ALU.mult, ALU.add))
            root_step(dve.tensor_tensor(rr[:], r1, r0, ALU.mult))
            dve.scalar_tensor_tensor(out=mrr[:], in0=mvl[:, :, 0], scalar=-1.0, in1=rr[:], op0=ALU.mult,
                                     op1=ALU.mult).then_inc(mean_ready, 1)

            def last_step(stage):
                a, b, r, m, o = (stage(i) for i in (3, 4, 6, 7, 9))
                if a:
                    dve.wait_ge(S["l_added"], a.done())
                    dve.wait_ge(S["l_mixed"], a.done())
                    dve.tensor_tensor(X[:, a.cols(D)], PS[:, 1, 0:D], X[:, a.cols(D)], ALU.add).then_inc(S["l_x3"], 1)
                if b:
                    dve.wait_ge(S["l_xnT_done"], b.freed())
                    dve.wait_ge(S["l_rstd"], b.done())
                    dve.tensor_scalar(xn[:, b.par, :], X[:, b.cols(D)], mv2[:, b.par, 0:1], rstd[:, b.par:b.par + 1],
                                      ALU.subtract, ALU.mult).then_inc(S["l_normed"], 1)
                if r:
                    dve.wait_ge(S["l_routed"], r.done())
                    dve.tensor_tensor(lg1[:, r.par, :], PS[:, 3, 0:E], rb1[:], ALU.add).then_inc(S["l_lg"], 1)
                if a:
                    dve.wait_ge(S["l_x3"], a.done())
                    dve.nop(nofuse=True)
                    dve.bn_stats(st[:, a.par, :], X[:, a.cols(D)]).then_inc(S["l_stats2"], 1)
                if r:
                    dve.wait_ge(S["l_lg"], r.done())
                    dve.nop(nofuse=True)
                    dve.max(mx8[:, r.par, :], lg1[:, r.par, :]).then_inc(S["l_m8"], 1)
                if a:
                    dve.wait_ge(S["l_stats2"], a.done())
                    dve.nop(nofuse=True)
                    dve.bn_aggr(mv2[:, a.par, :], st[:, a.par, :]).then_inc(S["l_moments2"], 1)
                if r:
                    dve.wait_ge(S["l_m8"], r.done())
                    dve.nop(nofuse=True)
                    dve.max_index(ix8[:, r.par, :], mx8[:, r.par, :], lg1[:, r.par, :]).then_inc(S["l_i8"], 1)
                if m:
                    dve.wait_ge(S["l_spread"], m.done())
                    dve.wait_ge(S["l_summed"], m.freed())
                    dve.tensor_tensor(z[:, m.par], PS[:, 4:6, :].rearrange("p b (e t) -> p (b e) t", t=P),
                                      xnT4[:, m.slot, :].unsqueeze(1).to_broadcast([P, E, P]), ALU.mult)\
                        .then_inc(S["l_masked"], 1)
                if r:
                    dve.wait_ge(S["l_i8"], r.done())
                    dve.tensor_copy(ixf[:, r.par, :], ix8[:, r.par, 0:2]).then_inc(S["l_ixf"], 1)
                if o:
                    dve.wait_ge(S["l_summed"], o.done())
                    dve.tensor_tensor(X[:, o.cols(D)], PS[:, 6 + o.par, 0:D], X[:, o.cols(D)], ALU.add)\
                        .then_inc(S["l_out_ready"], 1)
                if r:
                    dve.wait_ge(S["l_mask_turned"], r.freed())
                    dve.wait_ge(S["l_spread"], r.freed())
                    dve.wait_ge(S["l_ixf"], r.done())
                    dve.tensor_scalar(mask1[:, r.par, 0, :], exp_no, ixf[:, r.par, 0:1], None, ALU.is_equal)\
                        .then_inc(S["l_mk0"], 1)
                    dve.wait_ge(S["l_mk0"], r.done())
                    dve.scalar_tensor_tensor(out=mask1[:, r.par, 1, :], in0=exp_no, scalar=ixf[:, r.par, 1:2],
                                             in1=mask1[:, r.par, 0, :], op0=ALU.is_equal, op1=ALU.add)\
                        .then_inc(S["l_mask_ready"], 1)

            walk(dve, NT, 9, last_step)

        @block.tensor
        def _(pe):
            credit(pe, ("xnT_done", 1), ("qkv_done", 1), ("qk_turned", 1), ("ctx_turned", 1), ("scored", 4),
                   ("max_turned", 1), ("scored_t", 4), ("averaged", 4), ("o_turned", 1), ("on_turned", 1),
                   ("projected", 1), ("r_xnT_done", 1), ("r_routed", 1))
            pe.wait_ge(weights_ready, 3)
            pe.wait_ge(pool_consts, 2)

            def scores_for_max(a, j):
                if j == 0:
                    pe.wait_ge(S["q_spread"], a.done())
                    pe.wait_ge(S["k_kept"], a.done())
                    pe.wait_ge(S["ctx_kept"], a.done())
                pe.wait_ge(S["maxed"], a.freed(4, j, back=2))
                for hg in range(HG):
                    for b in range(2):
                        last = nc.tensor.matmul(PS[64 * b:64 * b + 64, j % 2, hg * P:hg * P + P],
                                                qbd[:, a.slot, j, hg, 64 * b:64 * b + 64], kt[:, a.slot, b, j, :],
                                                start=True, stop=True)
                last.then_inc(S["scored"], 1)

            def scores_by_key(b, j):
                if j == 0:
                    pe.wait_ge(shift_placed[b.par], 64 * (b.pair + 1))
                pe.wait_ge(S["exped"], b.freed(4, j, back=2))
                seq = j // 2
                for g2 in range(2):
                    g = 2 * (j % 2) + g2
                    last = nc.tensor.matmul(PS[:, 2 + j % 2, 256 * g2:256 * g2 + 256], kt[:, b.slot, seq, g, :],
                                            qbd[:, b.slot, g, :, SEQ * seq:SEQ * seq + SEQ], start=True, stop=True)
                last.then_inc(S["scored_t"], 1)

            def average(b, j):
                if j == 0:
                    pe.wait_ge(S["v_spread"], b.done())
                    pe.wait_ge(S["o_kept"], b.freed(back=1))
                pe.wait_ge(S["exped"], b.done(4, j))
                seq = j // 2
                for g2 in range(2):
                    g = 2 * (j % 2) + g2
                    for hg in range(HG):
                        last = nc.tensor.matmul(PS[32 * hg:32 * hg + 32, 7, g * P + SEQ * seq:g * P + SEQ * seq + SEQ],
                                                vp[:, b.par, seq, g * HG + hg, :],
                                                pexp[:, j, (g2 * HG + hg) * SEQ:(g2 * HG + hg + 1) * SEQ],
                                                start=True, stop=True)
                last.then_inc(S["averaged"], 1)

            def turn_stack(s, w, bank, col, done):
                for g in range(G):
                    last = nc.tensor.transpose(
                        bank16(bank)[:, col + g * P:col + (g + 1) * P],
                        stack[:, s.par, w, g * HG:g * HG + HG, :].rearrange("p h c -> p (h c)"), ident16[:])
                if done:
                    last.then_inc(S[done], 1)

            def step(stage):
                f, s, a, c, b, n = (stage(i) for i in range(1, 7))
                m, rt, rk, rl = (stage(i) for i in (7, 9, 10, 11))
                if a:
                    scores_for_max(a, 0)
                if a:
                    pe.wait_ge(S["ctx_kept"], a.done())
                if b:
                    pe.wait_ge(S["max_kept"], b.done())
                if rk:
                    pe.wait_ge(S["r_xnT_kept"], rk.done())
                if m:
                    pe.wait_ge(S["o_normed"], m.done())
                    nc.tensor.transpose(PS[:, 6, 0:P], on[:, m.par, :], identf).then_inc(S["on_turned"], 1)
                if a:
                    scores_for_max(a, 1)
                if s:
                    pe.wait_ge(S["hi_ready"], s.done())
                    pe.wait_ge(S["lo_ready"], s.done(2, 1))
                    turn_stack(s, 0, 5, 0, None)
                    turn_stack(s, 1, 5, 512, "qk_turned")
                if m:
                    pe.wait_ge(S["on_kept"], m.done())
                if rl:
                    nc.tensor.matmul(PS[:, 6, 3 * P:3 * P + 64], xrT[:, rl.par, :], gatew[:], start=True, stop=True)\
                        .then_inc(S["r_routed"], 1)
                if m:
                    nc.tensor.matmul(PS[:, 6, P:2 * P], onT[:, m.par, :], wproj[:], start=True, stop=True)\
                        .then_inc(S["projected"], 1)
                if b:
                    scores_by_key(b, 0)
                    scores_by_key(b, 1)
                if f:
                    if s:
                        pe.wait_ge(S["v_kept"], s.done())
                        pe.wait_ge(S["lo_ready"], s.done(2, 1))
                    pe.wait_ge(S["normed"], f.done())
                    nc.tensor.transpose(PS[:, 4, 0:P], xn[:, f.par, :], identf).then_inc(S["xnT_done"], 1)
                if a:
                    scores_for_max(a, 2)
                if rl:
                    pe.wait_ge(S["r_logits"], rl.done())
                if m:
                    pe.wait_ge(S["x_updated"], m.done())
                if rt:
                    pe.wait_ge(S["r_normed"], rt.done())
                    nc.tensor.transpose(PS[:, 6, 2 * P:3 * P], xr[:, rt.par, :], identf).then_inc(S["r_xnT_done"], 1)
                if c:
                    pe.wait_ge(S["maxed"], c.done(4, 3))
                    nc.tensor.transpose(bank16(6)[0:H, 7 * P:8 * P], negm[:, c.par, :, :].rearrange("p h g -> p (h g)"),
                                        ident16[:]).then_inc(S["max_turned"], 1)
                if s:
                    pe.wait_ge(S["ctx_stacked"], s.done())
                    turn_stack(s, 2, 6, 0, "ctx_turned")
                if b:
                    average(b, 0)
                if f:
                    pe.wait_ge(S["xnT_kept"], f.done())
                    nc.tensor.matmul(PS[:, 4, P:4 * P], xnT[:, f.par, :], wqkv[:], start=True, stop=True)\
                        .then_inc(S["qkv_done"], 1)
                if b:
                    scores_by_key(b, 2)
                if b:
                    average(b, 1)
                    scores_by_key(b, 3)
                if a:
                    scores_for_max(a, 3)
                if n:
                    pe.wait_ge(S["o_kept"], n.done())
                    if s:
                        pe.wait_ge(S["k_kept"], s.done())
                    for g in range(G):
                        last = nc.tensor.transpose(PS[:, 5, g * P:g * P + P], oS[:, n.par, g * P:g * P + P], identf)
                    last.then_inc(S["o_turned"], 1)
                if b:
                    average(b, 2)
                    average(b, 3)

            walk(pe, NT, 11, step)

            credit(pe, *((n, 1) for n in ("h_down e_turned e_act_turned e_lifted e_down c_depooled c_placed l_hnT_done "
                                          "l_mixed l_xnT_done l_routed l_spread l_mask_turned l_summed").split()),
                   ("h_lifted", 2))
            pe.wait_ge(S["x_updated"], Tile(NT - 1).done())
            pe.wait_ge(S["r_logits"], Tile(NT - 1).done())
            pe.wait_ge(more_in, 16)
            pe.wait_ge(sort_step, 5)
            oh = onehot[:].rearrange("p e t -> p (e t)")
            nc.tensor.matmul(PS[:, 4, 0:E * NT], upper16[:], oh, start=True, stop=True)
            nc.tensor.matmul(PS[:, 5, 0:E * NT], ones16[:], oh, start=True, stop=True).then_inc(ranked, 1)

            def shared_step(stage):
                c, d = stage(0), stage(1)
                if c:
                    if c.turn is None and c.n == 0:
                        pe.wait_ge(S["r_xnT_kept"], Tile(NT - 1).done())
                        pe.wait_ge(S["r_logits"], Tile(NT - 1).done())
                    for i in range(2):
                        pe.wait_ge(S["h_acted"], c.freed(2, i, back=2))
                        rows = XNT[:, ds(c.t * CT * P, CT * P)]
                        nc.tensor.matmul(PS[:, 2 * i, :], shgu[:, i * P:i * P + P], rows, start=True, stop=True)
                        nc.tensor.matmul(PS[:, 2 * i + 1, :], shgu[:, FF + i * P:FF + i * P + P], rows,
                                         start=True, stop=True).then_inc(S["h_lifted"], 1)
                if d:
                    if d.turn is None and d.n == 0:
                        pe.wait_ge(late_ready, 6)
                    pe.wait_ge(S["h_acted"], d.done(2, 1))
                    pe.wait_ge(S["h_added"], d.freed())
                    for q in range(CT):
                        for i in range(2):
                            last = nc.tensor.matmul(PS[:, 6 + d.par, q * P:q * P + P],
                                                    hact[:, d.par, i, q * P:q * P + P], shd[:, i * D:i * D + D],
                                                    start=(i == 0), stop=(i == 1))
                    last.then_inc(S["h_down"], 1)

            walk(pe, NC, 1, shared_step, unroll=2)

            pe.wait_ge(texp_ready, 1)
            four_experts = pe.alloc_register("four_experts")
            expert_of = [pe.alloc_register(f"expert_of_slot{k}") for k in range(4)]
            pe.wait_ge(S["h_added"], Tile(NC - 1).done())

            def sorted_step(stage):
                f, s, a, b = (stage(i) for i in range(2, 6))
                if s:
                    e_lift = pe.snap(expert_of[s.slot], min_val=0, max_val=E - 1)
                    pe.wait_ge(S["e_acted"], s.freed())
                    pe.wait_ge(S["e_turned_kept"], s.done())
                    nc.tensor.matmul(PS[:, 2 + s.par, :], xsT[:, s.par, :], rgu[:, ds(e_lift * (2 * FF), 2 * FF)],
                                     start=True, stop=True).then_inc(S["e_lifted"], 1)
                if f:
                    pe.wait_ge(S["e_turned_kept"], f.freed())
                    pe.wait_ge(xs_in[f.slot], 16 * (f.quad + 1))
                    nc.tensor.transpose(PS[:, f.par, 0:P], xs[:, f.slot, :], identf).then_inc(S["e_turned"], 1)
                if b:
                    e_down = pe.snap(expert_of[b.slot], min_val=0, max_val=E - 1)
                    pe.wait_ge(S["e_kept"], b.freed())
                    pe.wait_ge(S["e_act_kept"], b.done())
                    for i in range(2):
                        last = nc.tensor.matmul(PS[:, 6 + b.par, 0:D], act2T[:, b.par, i * P:i * P + P],
                                                rdn[:, ds(e_down * FF + i * D, D)], start=(i == 0), stop=(i == 1))
                    last.then_inc(S["e_down"], 1)
                if f:
                    if f.slot == 0:
                        pe.reg_mov(four_experts, pe.value_load(texp[0:1, ds(f.quad, 1)],
                                                               min_val=0, max_val=E ** 4 - 1))
                    four = pe.snap(four_experts, min_val=0, max_val=E ** 4 - 1)
                    pe.reg_mov(expert_of[f.slot], four // E ** f.slot % E)
                if a:
                    pe.wait_ge(S["e_act_kept"], a.freed())
                    pe.wait_ge(S["e_acted"], a.done())
                    for i in range(2):
                        last = nc.tensor.transpose(PS[:, 4 + a.par, i * P:i * P + P],
                                                   hact[:, a.par, 0, i * P:i * P + P], identf)
                    last.then_inc(S["e_act_turned"], 1)

            walk(pe, NS, 7, sorted_step)
            pe.wait_ge(S["e_kept"], Tile(NS - 1).done())

            def context_step(stage):
                f, s = stage(1), stage(2)
                if f:
                    pe.wait_ge(S["c_dp_kept"], f.freed())
                    pe.wait_ge(S["c_hp_ready"], f.done())
                    nc.tensor.matmul(PS[:, f.par, 0:D], decay, hp[:, f.par, :], start=True, stop=True)\
                        .then_inc(S["c_depooled"], 1)
                if s:
                    pe.wait_ge(S["c_put"], s.freed())
                    pe.wait_ge(S["c_dp_kept"], s.done())
                    pe.wait_ge(S["c_picked"], s.done())
                    nc.tensor.matmul(PS[:, 2 + s.par, 0:D], pick[:, s.par, :], dp[:, s.par, :], start=True, stop=True)\
                        .then_inc(S["c_placed"], 1)

            walk(pe, NT, 3, context_step)
            pe.wait_ge(S["c_put"], Tile(NT - 1).done())
            pe.wait_ge(bias_ready, 1)

            def last_step(stage):
                f, s, b, r, m, y = (stage(i) for i in (1, 2, 5, 6, 7, 8))
                if r:
                    pe.wait_ge(S["l_lg"], r.freed(back=1))
                    pe.wait_ge(S["l_xnT_kept"], r.done())
                    nc.tensor.matmul(PS[:, 3, 0:64], xnT4[:, r.slot, :], rw1[:], start=True, stop=True)\
                        .then_inc(S["l_routed"], 1)
                if m:
                    pe.wait_ge(S["l_masked"], m.freed(back=1))
                    pe.wait_ge(S["l_mask_ready"], m.done())
                    for e in range(E):
                        last = nc.tensor.matmul(PS[:, 4 + e // 4, e % 4 * P:e % 4 * P + P],
                                                mask1[:, m.par, 1, e:e + 1].to_broadcast([P, P]), ident16[:],
                                                start=True, stop=True)
                    last.then_inc(S["l_spread"], 1)
                if f:
                    pe.wait_ge(S["l_hnT_kept"], f.freed(back=1))
                    if m:
                        pe.wait_ge(S["l_mask_kept"], m.freed(back=1))
                    pe.wait_ge(S["l_hn_ready"], f.done())
                    nc.tensor.transpose(PS[:, 0, 0:P], hn[:, f.par, :], identf).then_inc(S["l_hnT_done"], 1)
                if s:
                    pe.wait_ge(S["l_x3"], s.freed(back=1))
                    pe.wait_ge(S["l_hnT_kept"], s.done())
                    nc.tensor.matmul(PS[:, 1, 0:D], hnT[:, s.par, :], winT[:], start=True, stop=True)\
                        .then_inc(S["l_mixed"], 1)
                if b:
                    pe.wait_ge(S["l_xnT_kept"], b.freed(back=1))
                    pe.wait_ge(S["l_normed"], b.done())
                    nc.tensor.transpose(PS[:, 2, 0:P], xn[:, b.par, :], identf).then_inc(S["l_xnT_done"], 1)
                if y:
                    pe.wait_ge(S["l_out_ready"], y.freed())
                    pe.wait_ge(S["l_masked"], y.done())
                    for e in range(E):
                        nc.tensor.matmul(PS[:, 6 + y.par, 0:D], z[:, y.par, e, :], w1[:, e * D:e * D + D],
                                         start=(e == 0), stop=False)
                if m:
                    pe.wait_ge(*((S["l_hnT_kept"], f.done()) if f else (S["l_mask_kept"], m.freed(back=1))))
                    nc.tensor.transpose(bank16(0)[0:E, 512:512 + P], mask1[:, m.par, 1, :], ident16[:])\
                        .then_inc(S["l_mask_turned"], 1)
                if y:
                    pe.wait_ge(S["l_mask_kept"], y.done())
                    nc.tensor.matmul(PS[:, 6 + y.par, 0:D], mask1T[:, y.par, :], b1[:], start=False, stop=True)\
                        .then_inc(S["l_summed"], 1)

            walk(pe, NT, 9, last_step)


def constants(ns):
    p = np.arange(P)
    same = p[:, None] // 64 == p[None, :] // 64
    ago = p[None, :] - p[:, None]
    keep = np.exp(np.float64(-1e-3))
    fade = -np.expm1(np.float64(-1e-3))
    decay = np.where(same & (ago >= 0), keep * fade ** np.maximum(ago, 0), 0.0)
    rows = (np.arange(8), np.arange(8) - 8, np.arange(ns) * P)
    return np.concatenate([np.eye(P), p[:, None] < p[None, :], np.ones((P, P)), decay]
                          + [np.broadcast_to(r, (P, r.size)) for r in rows]
                          + [p[:, None] % 64, np.broadcast_to(np.arange(64), (P, 64))], 1).astype(np.float32)


def kernel(**inputs):
    import numpy as _np
    import concourse.bacc as _bacc
    from concourse import mybir as _mybir
    from concourse.bass_utils import run_bass_kernel_spmd as _run

    i = {k: _np.asarray(v) for k, v in inputs.items()}
    nt, ns = 32, 40

    def pad64(a):
        return _np.pad(a, ((0, 0), (0, 64 - a.shape[1])))

    def by_tile(a):
        return a.reshape(nt, 128, -1).transpose(1, 0, 2).reshape(128, -1)

    ctx = i["ctx_2048"].reshape(nt, 2, 64, 256)
    arrays = {
        "x": by_tile(i["x"]),
        "ctx_k": by_tile(ctx[..., :128]),
        "ctx_v_swapped": by_tile(ctx[:, ::-1, :, 128:]),
        "consts": constants(ns),
        "gates": _np.broadcast_to(_np.concatenate([i["g_xattn"], i["g_ffn"]]), (128, 4)),
        "w_qkv": i["L0_xattn_w_qkv"].T,
        "w_proj": i["L0_xattn_w_proj"].T,
        "b_proj": _np.broadcast_to(i["L0_xattn_b_proj"], (128, 128)),
        "gate_w": pad64(i["L0_ffn_gate_w"]),
        "sh_gate_up": _np.concatenate([i["L0_ffn_sh_gate"], i["L0_ffn_sh_up"]], 1),
        "sh_down": i["L0_ffn_sh_down"].reshape(2, 128, 128).transpose(1, 0, 2).reshape(128, 256),
        "rt_gate_up": _np.concatenate([i["L0_ffn_rt_gate"], i["L0_ffn_rt_up"]], 2).transpose(1, 0, 2).reshape(128, -1),
        "rt_down": i["L0_ffn_rt_down"].reshape(8, 2, 128, 128).transpose(2, 0, 1, 3).reshape(128, -1),
        "patch_mask": i["mask_BxS2_if0"],
        "w_in": i["L1_xattn_W_in"].T,
        "b_in": _np.broadcast_to(i["L1_xattn_b_in"], (128, 128)),
        "g_res": i["L1_xattn_g_res"].reshape(128, 1),
        "g_init": _np.broadcast_to(i["L1_xattn_g_init"][:128], (128, 128)),
        "router_w": pad64(i["L1_ffn_router_w"].T),
        "router_b": _np.broadcast_to(i["L1_ffn_router_b"], (128, 8)),
        "expert_w": i["L1_ffn_expert_w"].transpose(2, 0, 1).reshape(128, -1),
        "expert_b": i["L1_ffn_expert_b"],
    }
    arrays = {f"in_{k}_dram": _np.ascontiguousarray(v) for k, v in arrays.items()}
    nc = _bacc.Bacc("TRN2", target_bir_lowering=False, num_devices=1)
    args = [nc.dram_tensor(k, v.shape, _mybir.dt.from_np(v.dtype), kind="ExternalInput").ap() for k, v in arrays.items()]
    args.append(nc.dram_tensor("out_dram", (128, nt * 128), _mybir.dt.float32, kind="ExternalOutput").ap())
    flamingo_gated_two_layers(nc, *args)
    r = _run(nc, [arrays], core_ids=[0])
    return r.results[0]["out_dram"].reshape(128, nt, 128).transpose(1, 0, 2).reshape(64, 64, 128)
```
